# Optimizing a Trainium2 kernel written in Bass

```python
import numpy as np
import jax
import jax.numpy as jnp

def _softmax(x, axis=-1):
    return jax.nn.softmax(x, axis=axis)

def _gelu(x):
    return jax.nn.gelu(x, approximate=True)

def _silu(x):
    return jax.nn.silu(x)

def _sigmoid(x):
    return jax.nn.sigmoid(x)

def _layernorm(x, axis=-1, eps=1e-05):
    m = jnp.mean(x, axis=axis, keepdims=True)
    v = jnp.var(x, axis=axis, keepdims=True)
    return (x - m) / jnp.sqrt(v + eps)

def _scatter_add(tgt, idx, src, axis=0):
    return tgt.at[idx].add(src)

def _segment_sum(src, seg, n):
    return jax.ops.segment_sum(src, seg, n)
kernel_name = 'mk_seq_preln_d1_jaxref_r4_410301'

def setup_inputs(seed: int=0):
    np.random.seed(seed)
    _w = jnp.asarray

    def _L0_attn_setup():
        import jax, jax.numpy as jnp
        import numpy as np
        import math
        B, L, D, H = (32, 128, 1024, 32)
        HD = D // H
        key = jax.random.key(seed)
        ks = jax.random.split(key, 9)
        s = 1.0 / math.sqrt(D)
        return {'x': jax.random.normal(ks[0], (B, L, D), jnp.float32), 'Wq': jax.random.normal(ks[1], (D, D), jnp.float32) * s, 'bq': jax.random.normal(ks[2], (D,), jnp.float32) * s, 'Wk': jax.random.normal(ks[3], (D, D), jnp.float32) * s, 'bk': jax.random.normal(ks[4], (D,), jnp.float32) * s, 'Wv': jax.random.normal(ks[5], (D, D), jnp.float32) * s, 'bv': jax.random.normal(ks[6], (D,), jnp.float32) * s, 'Wo': jax.random.normal(ks[7], (D, D), jnp.float32) * s, 'bo': jax.random.normal(ks[8], (D,), jnp.float32) * s}
    _L0_attn_in = _L0_attn_setup()

    def _L0_ffn_setup():
        import jax, jax.numpy as jnp
        import numpy as np
        B_L, B_H = (4, 8)
        LIN_SLOPE, LIN_INTER, EST_T = (1.0, 0.0, 64.0)
        BATCH, SEQ, IN_F, OUT_F = (4, 512, 1024, 1024)
        MAX_BITS = 8

        def dequant_kbit(qweight, lut, bit):
            O, I32 = (qweight.shape[1], qweight.shape[2])
            shifts = jnp.arange(32, dtype=jnp.int32)
            idx = jnp.zeros((O, I32 * 32), dtype=jnp.int32)
            for p in range(bit):
                bits = (qweight[p][:, :, None] >> shifts & 1).reshape(O, I32 * 32)
                idx = idx | bits << p
            return jnp.take_along_axis(lut, idx, axis=1)
        key = jax.random.key(seed)
        k = jax.random.split(key, 5)
        x = jax.random.normal(k[0], (BATCH, SEQ, IN_F), dtype=jnp.float32)
        qweight = jax.random.randint(k[1], (MAX_BITS, OUT_F, IN_F // 32), 0, 2147483647, dtype=jnp.int32)
        lut4 = jax.random.normal(k[2], (OUT_F, 2 ** B_L), dtype=jnp.float32) * 0.02
        lut8 = jax.random.normal(k[3], (OUT_F, 2 ** B_H), dtype=jnp.float32) * 0.02
        bias = jax.random.normal(k[4], (OUT_F,), dtype=jnp.float32) * 0.01
        return {'x': x, 'qweight': qweight, 'lut4': lut4, 'lut8': lut8, 'bias': bias}
    _L0_ffn_in = _L0_ffn_setup()
    _d = {'L0_attn_x': _L0_attn_in['x'], 'L0_attn_Wq': _L0_attn_in['Wq'], 'L0_attn_bq': _L0_attn_in['bq'], 'L0_attn_Wk': _L0_attn_in['Wk'], 'L0_attn_bk': _L0_attn_in['bk'], 'L0_attn_Wv': _L0_attn_in['Wv'], 'L0_attn_bv': _L0_attn_in['bv'], 'L0_attn_Wo': _L0_attn_in['Wo'], 'L0_attn_bo': _L0_attn_in['bo'], 'L0_ffn_qweight': _L0_ffn_in['qweight'], 'L0_ffn_lut4': _L0_ffn_in['lut4'], 'L0_ffn_lut8': _L0_ffn_in['lut8'], 'L0_ffn_bias': _L0_ffn_in['bias']}
    _x0 = _d['L0_attn_x']
    _d['L0_attn_x'] = jax.random.normal(jax.random.fold_in(jax.random.key(seed), 1), (4, 512, 1024), dtype=_x0.dtype)
    del _x0
    return _d

def reference(L0_attn_x, L0_attn_Wq, L0_attn_bq, L0_attn_Wk, L0_attn_bk, L0_attn_Wv, L0_attn_bv, L0_attn_Wo, L0_attn_bo, L0_ffn_qweight, L0_ffn_lut4, L0_ffn_lut8, L0_ffn_bias):

    def _L0_attn_ref(x, Wq, bq, Wk, bk, Wv, bv, Wo, bo):
        import jax, jax.numpy as jnp
        import numpy as np
        import math
        B, L, D, H = (32, 128, 1024, 32)
        HD = D // H
        b, l, d = x.shape
        h, hd = (H, HD)
        q = (x @ Wq.T + bq).reshape(b, l, h, hd).transpose(0, 2, 1, 3)
        k = (x @ Wk.T + bk).reshape(b, l, h, hd).transpose(0, 2, 1, 3)
        v = (x @ Wv.T + bv).reshape(b, l, h, hd).transpose(0, 2, 1, 3)
        scores = jnp.einsum('bhqd,bhkd->bhqk', q, k) / math.sqrt(hd)
        causal = jnp.tril(jnp.ones((l, l), bool))
        scores = jnp.where(causal, scores, -jnp.inf)
        att = jax.nn.softmax(scores, axis=-1)
        out = jnp.einsum('bhqk,bhkd->bhqd', att, v)
        out = out.transpose(0, 2, 1, 3).reshape(b, l, d)
        return out @ Wo.T + bo

    def _L0_ffn_ref(x, qweight, lut4, lut8, bias):
        import jax, jax.numpy as jnp
        import numpy as np
        B_L, B_H = (4, 8)
        LIN_SLOPE, LIN_INTER, EST_T = (1.0, 0.0, 64.0)
        BATCH, SEQ, IN_F, OUT_F = (4, 512, 1024, 1024)
        MAX_BITS = 8

        def dequant_kbit(qweight, lut, bit):
            O, I32 = (qweight.shape[1], qweight.shape[2])
            shifts = jnp.arange(32, dtype=jnp.int32)
            idx = jnp.zeros((O, I32 * 32), dtype=jnp.int32)
            for p in range(bit):
                bits = (qweight[p][:, :, None] >> shifts & 1).reshape(O, I32 * 32)
                idx = idx | bits << p
            return jnp.take_along_axis(lut, idx, axis=1)
        e = jnp.linalg.norm(x, axis=-1) * LIN_SLOPE + LIN_INTER
        mask = e > EST_T
        w_l = dequant_kbit(qweight, lut4, B_L)
        w_h = dequant_kbit(qweight, lut8, B_H)
        y_l = jnp.einsum('bsi,oi->bso', x, w_l)
        y_h = jnp.einsum('bsi,oi->bso', x, w_h)
        y = jnp.where(mask[..., None], y_h, y_l) + bias
        return y
    x = L0_attn_x
    x = x + _L0_attn_ref(_layernorm(x, axis=-1), L0_attn_Wq, L0_attn_bq, L0_attn_Wk, L0_attn_bk, L0_attn_Wv, L0_attn_bv, L0_attn_Wo, L0_attn_bo)
    x = x + _L0_ffn_ref(_layernorm(x, axis=-1), L0_ffn_qweight, L0_ffn_lut4, L0_ffn_lut8, L0_ffn_bias)
    return x

_drawn_inputs = setup_inputs


def setup_inputs(seed=0):
    import zlib

    import numpy as np

    out = dict(_drawn_inputs(seed))
    spreads = {}
    factors = {'L0_attn_bq': 8.0, 'L0_attn_bk': 8.0, 'L0_ffn_bias': 6.862}
    for name, (base, spread) in spreads.items():
        noise = np.random.default_rng([zlib.crc32(name.encode()), seed]).standard_normal(out[name].shape)
        drawn = base * np.exp(spread * noise) if base else spread * noise
        out[name] = jnp.asarray(drawn.astype(out[name].dtype))
    for name, factor in factors.items():
        out[name] = (out[name] * factor).astype(out[name].dtype)
    return out
```

```python
import concourse.bass as bass
from concourse import mybir
from concourse.alu_op_type import AluOpType as ALU
from contextlib import ExitStack

F32 = mybir.dt.float32
F32R = mybir.dt.float32r
BF16 = mybir.dt.bfloat16
I32 = mybir.dt.int32
ACT = mybir.ActivationFunctionType
AXIS = mybir.AxisListType

P = 128
D = 1024
BATCH, SEQ = 4, 512
TOKENS = BATCH * SEQ
HEADS, HD = 32, 32
KT = D // P
GH = P // HD
GROUPS = HEADS // GH
QT = SEQ // P
STEPS = BATCH * GROUPS
SCALE = 1.0 / float(HD) ** 0.5
EPS = 1e-5
MASKED = -3.0e38
THRESHOLD_SQ = 64.0 ** 2
Q, K, V = range(3)

CH = 64
CHUNKS = TOKENS // CH
CHUNKS_AHEAD = SEQ // CH + 1

P_OFF = [0, 128, 384, 768]
P_COLS = 1280
T_FILLS = [[(0, 0), (0, 1), (0, 2), (0, 3)], [(3, 3), (1, 1), (1, 2), (1, 3)], [(2, 2), (2, 3)]]
T_DEST = [640, 128, 1152]
PT_COLS = 1408
PT_KT = [640, 256, 1152, 0]
PT_QT = [0, 1, 2, 2]
S_COL = [0, 256, 512, 1024]
S_KEYS = [256, 256, 384, 512]


class Phase:

    def __init__(self, nc, buffers, outer):
        self.nc, self.buffers, self.outer = nc, buffers, outer

    def sb(self, name, shape, dt=F32):
        return self.buffers.enter_context(self.nc.sbuf_tensor(name, shape, dt))

    def pb(self, name, shape, dt=F32):
        return self.buffers.enter_context(self.nc.psum_tensor(name, shape, dt))

    def sem(self, name):
        return self.outer.enter_context(self.nc.semaphore(name))


def attention_phase(nc, outer, x, w_qkv, b_qkv, att):
    with ExitStack() as buffers:
        ph = Phase(nc, buffers, outer)
        sb, pb, sem = ph.sb, ph.pb, ph.sem
        ident = sb("ident", [P, P])
        identb = sb("identb", [P, P], BF16)
        maskb = sb("maskb", [P, P], BF16)
        bias = sb("bias", [P, 3, GROUPS])
        xT_hi = [sb(f"xT_hi{i}", [P, KT, SEQ], F32R) for i in range(2)]
        xT_lo = [sb(f"xT_lo{i}", [P, KT, SEQ], F32R) for i in range(2)]
        w_raw = sb("w_raw", [P, 3, KT * P])
        w_hi = sb("w_hi", [P, 3, KT * P], F32R)
        w_lo = sb("w_lo", [P, 3, KT * P], F32R)
        qk_hi = sb("qk_hi", [P, 2, SEQ], F32R)
        qk_lo = sb("qk_lo", [P, 2, SEQ], F32R)
        q_stack = sb("q_stack", [3 * HD, GH, SEQ], F32R)
        k_stack = sb("k_stack", [3 * HD, GH, SEQ], F32R)
        vT = sb("vT", [P, SEQ])
        v_parts = sb("v_parts", [P, QT, GH, 2 * HD], F32R)
        probs = [sb(f"probs{i}", [P, P_COLS]) for i in range(2)]
        pT_hi = [sb(f"pT_hi{i}", [P, PT_COLS], F32R) for i in range(2)]
        pT_lo = [sb(f"pT_lo{i}", [P, PT_COLS], F32R) for i in range(2)]
        row_max = [sb(f"row_max{i}", [P, QT]) for i in range(2)]
        neg_max = [sb(f"neg_max{i}", [P, QT]) for i in range(2)]
        row_sum = [sb(f"row_sum{i}", [P, QT]) for i in range(2)]
        inv_sum = [sb(f"inv_sum{i}", [P, QT]) for i in range(2)]
        o_low = sb("o_low", [HD, SEQ])
        o_out = sb("o_out", [P, SEQ])
        x_in = sb("x_in", [CH, D])
        xn = sb("xn", [CH, D])
        bn = sb("bn", [CH, 2, 6])
        mv = sb("mv", [CH, 2])
        rs = sb("rs", [CH, 4])
        neg_half = sb("neg_half", [CH, 1])

        proj_ps = [pb(f"proj_ps{i}", [P, SEQ]) for i in range(2)]
        score_ps = pb("score_ps", [P, 3 * SEQ])
        t_ps = [pb(f"t_ps{i}", [P, SEQ]) for i in range(2)]
        o_ps = pb("o_ps", [2 * HD, SEQ])

        bias_in = sem("bias_in")
        consts = sem("consts")
        zeros_done = sem("zeros_done")
        x_loaded = sem("x_loaded")
        w_loaded = [sem(f"w_loaded{m}") for m in range(3)]
        w_hi_done = sem("w_hi_done")
        w_lo_done = sem("w_lo_done")
        bn_done = sem("bn_done")
        stats_done = sem("stats_done")
        rstd_chain = sem("rstd_chain")
        xn_done = sem("xn_done")
        proj_done = sem("proj_done")
        qk_hi_done = sem("qk_hi_done")
        qk_lo_done = sem("qk_lo_done")
        v_done = sem("v_done")
        stacked = [sem(f"stacked{i}") for i in range(2)]
        scores_done = sem("scores_done")
        max_done = sem("max_done")
        negmax_done = sem("negmax_done")
        exp_done = sem("exp_done")
        inv_done = sem("inv_done")
        norm_done = sem("norm_done")
        fill_done = sem("fill_done")
        hi_done = sem("hi_done")
        lo_done = sem("lo_done")
        pv_done = sem("pv_done")
        low_copied = sem("low_copied")
        head_done = sem("head_done")
        stored = [sem(f"stored{i}") for i in range(GH)]

        def has_chunk(b, g):
            return 8 * b + (g if isinstance(g, int) else 0) + CHUNKS_AHEAD < CHUNKS

        def step_of(b, g):
            return g + GROUPS * b

        def fill(b, g, i):
            with_chunk = CHUNKS - CHUNKS_AHEAD
            base = CHUNKS_AHEAD - 3 + i
            if GROUPS * b >= with_chunk:
                return g * 13 + (14 * with_chunk + 13 * (GROUPS * b - with_chunk) + base)
            return g * 14 + (14 * GROUPS * b + base)

        def slot_fill(h, f):
            return 3 * h + f + (1 if h >= 2 else 0)

        def next_pos(b, g):
            if isinstance(g, int) and g == GROUPS - 1:
                return b + 1, 0
            return b, g + 1

        def emit(eng, prologue, step, tail):
            prologue()
            step(0, 0)
            for b in range(BATCH):
                with eng.Fori(1 if b == 0 else 0, GROUPS - 1) as g:
                    step(b, g)
                step(b, GROUPS - 1)
            tail()

        def slot_before(b, g, h, k):
            return step_of(b, g) * GH + (h - k)

        def first(b, g, h, k):
            return isinstance(g, int) and step_of(b, g) == 0 and h < k

        def last(b, g):
            return isinstance(g, int) and step_of(b, g) == STEPS - 1

        waited = sem("waited")

        def hold(eng):
            eng.sem_inc(waited, 1)

        block = buffers.enter_context(nc.Block())

        @block.sync
        def _(sp):
            def load_w(m, n, wrapped):
                if not (isinstance(n, int) and n == 0):
                    sp.wait_ge(w_lo_done, (n - 1) * 3 + m + 1)
                    hold(sp)
                sp.dma_start(w_raw[:, m, :], w_qkv[wrapped, :, m, :]).then_inc(w_loaded[m], 16)

            def load_x(c):
                if not (isinstance(c, int) and c == 0):
                    sp.wait_ge(xn_done, c)
                    hold(sp)
                sp.dma_start(x_in[:, :], x[bass.ds((c % CHUNKS) * CH, CH), :]).then_inc(x_loaded, 16)

            def stack(n, pair):
                for h in (2 * pair, 2 * pair + 1):
                    rows = slice(h * HD, (h + 1) * HD)
                    for part, src in enumerate((qk_hi, qk_lo, qk_hi)):
                        sp.dma_start(q_stack[part * HD:(part + 1) * HD, h, :].bitcast(F32),
                                     src[rows, Q, :].bitcast(F32))\
                            .then_inc(stacked[pair], 16)
                    for part, src in enumerate((qk_hi, qk_hi, qk_lo)):
                        sp.dma_start(k_stack[part * HD:(part + 1) * HD, h, :].bitcast(F32),
                                     src[rows, K, :].bitcast(F32))\
                            .then_inc(stacked[pair], 16)

            def store(b, g, h):
                if first(b, g, h, 3):
                    return
                head = (h + 1) % GH
                n = step_of(b, g) - (1 if h < 3 else 0)
                sp.wait_ge(head_done, slot_before(b, g, h, 3) + 1)
                hold(sp)
                sp.dma_start(att[n, head * HD:(head + 1) * HD, :],
                             o_out[head * HD:(head + 1) * HD, :]).then_inc(stored[head], 16)

            def prologue():
                for head in range(GH):
                    sp.sem_inc(stored[head], 16)
                sp.dma_start(bias[:, :, :], b_qkv).then_inc(bias_in, 16)
                load_x(0)
                for m in (Q, K, V):
                    load_w(m, 0, 0)
                for c in range(1, CHUNKS_AHEAD + 1):
                    load_x(c)
                for m in (Q, K, V):
                    load_w(m, 1, 1)
                load_w(Q, 2, 2)
                sp.wait_ge(qk_lo_done, 2)
                stack(0, 0)
                stack(0, 1)

            def step(b, g):
                n = step_of(b, g)
                if not last(b, g):
                    load_w(K, n + 2, (g + 2) % GROUPS)
                store(b, g, 0)
                if not last(b, g):
                    load_w(V, n + 2, (g + 2) % GROUPS)
                store(b, g, 1)
                if has_chunk(b, g):
                    load_x(n + CHUNKS_AHEAD + 1)
                store(b, g, 2)
                if not last(b, g):
                    sp.wait_ge(qk_lo_done, (n + 1) * 2 + 2)
                    hold(sp)
                    sp.wait_ge(scores_done, n * GH + 2)
                    hold(sp)
                    stack(n + 1, 0)
                    load_w(Q, n + 3, (g + 3) % GROUPS)
                store(b, g, 3)
                if not last(b, g):
                    sp.wait_ge(scores_done, n * GH + 4)
                    hold(sp)
                    stack(n + 1, 1)

            def tail():
                for h in range(3):
                    sp.wait_ge(head_done, STEPS * GH - 2 + h)
                    head = h + 1
                    sp.dma_start(att[STEPS - 1, head * HD:(head + 1) * HD, :],
                                 o_out[head * HD:(head + 1) * HD, :]).then_inc(stored[head], 16)
                for head in range(GH):
                    sp.wait_ge(stored[head], STEPS * 16 + 16)
                sp.wait_ge(w_loaded[Q], (STEPS + 2) * 16)
                sp.wait_ge(w_loaded[K], (STEPS + 1) * 16)
                sp.wait_ge(w_loaded[V], (STEPS + 1) * 16)
                sp.wait_ge(x_loaded, (CHUNKS + 1) * 16)

            emit(sp, prologue, step, tail)

        @block.gpsimd
        def _(pool):
            def split_w_lo(m, n):
                pool.wait_ge(w_hi_done, n * 3 + m + 1)
                pool.tensor_tensor(w_lo[:, m, :], w_raw[:, m, :], w_hi[:, m, :].bitcast(F32),
                                   ALU.subtract).then_inc(w_lo_done, 1)

            def normalize(c):
                base = c * 6
                pool.wait_ge(stats_done, c + 1)
                hold(pool)
                pool.tensor_scalar(rs[:, 0:1], mv[:, 1:2], EPS, None, ALU.add).then_inc(rstd_chain, 1)
                pool.wait_ge(rstd_chain, base + 1)
                pool.tensor_tensor(rs[:, 1:2], rs[:, 0:1], neg_half[:, :], ALU.pow).then_inc(rstd_chain, 1)
                pool.wait_ge(rstd_chain, base + 2)
                pool.tensor_tensor(rs[:, 2:3], rs[:, 1:2], rs[:, 1:2], ALU.mult).then_inc(rstd_chain, 1)
                pool.wait_ge(rstd_chain, base + 3)
                pool.tensor_tensor(rs[:, 2:3], rs[:, 2:3], rs[:, 0:1], ALU.mult).then_inc(rstd_chain, 1)
                pool.wait_ge(rstd_chain, base + 4)
                hold(pool)
                pool.tensor_scalar(rs[:, 2:3], rs[:, 2:3], -0.5, 1.5, ALU.mult, ALU.add).then_inc(rstd_chain, 1)
                pool.wait_ge(rstd_chain, base + 5)
                pool.tensor_tensor(rs[:, 3:4], rs[:, 1:2], rs[:, 2:3], ALU.mult).then_inc(rstd_chain, 1)
                pool.wait_ge(rstd_chain, base + 6)
                if not (isinstance(c, int) and c == 0):
                    pool.wait_ge(fill_done, chunk_fill(c - 1) + 1)
                hold(pool)
                pool.tensor_scalar(xn[:, :], x_in[:, :], mv[:, 0:1], rs[:, 3:4],
                                   ALU.subtract, ALU.mult).then_inc(xn_done, 1)

            def chunk_fill(c):
                if isinstance(c, int) and c < CHUNKS_AHEAD:
                    return c
                return (c - CHUNKS_AHEAD) * 14 + (CHUNKS_AHEAD - 3 + 13)

            def prologue():
                pool.memset(neg_half[:, :], -0.5)
                pool.memset(ident[:, :], 0.0).then_inc(consts, 1)
                pool.memset(maskb[:, :], 0.0).then_inc(consts, 1)
                pool.wait_ge(consts, 2)
                pool.affine_select(out=ident[:, :], in_=ident[:, :], compare_op=ALU.not_equal, fill=1.0,
                                   base=0, pattern=[[-1, P]], channel_multiplier=1).then_inc(consts, 1)
                pool.affine_select(out=maskb[:, :], in_=maskb[:, :], compare_op=ALU.is_ge, fill=MASKED,
                                   base=0, pattern=[[-1, P]], channel_multiplier=1).then_inc(consts, 1)
                pool.wait_ge(consts, 4)
                pool.tensor_copy(identb[:, :], ident[:, :]).then_inc(consts, 1)
                normalize(0)
                normalize(1)
                for m in (Q, K, V):
                    split_w_lo(m, 0)
                for c in range(2, CHUNKS_AHEAD):
                    normalize(c)
                for m in (Q, K):
                    split_w_lo(m, 1)

            def step(b, g):
                n = step_of(b, g)
                if last(b, g):
                    return
                split_w_lo(V, n + 1)
                if has_chunk(b, g):
                    normalize(n + CHUNKS_AHEAD)
                split_w_lo(Q, n + 2)
                split_w_lo(K, n + 2)

            emit(pool, prologue, step, lambda: None)

        @block.scalar
        def _(act):
            def split_w_hi(m, n):
                act.wait_ge(w_loaded[m], n * 16 + 16)
                if not (isinstance(n, int) and n == 0):
                    act.wait_ge(proj_done, (n - 1) * 3 + m + 1)
                act.activation(w_hi[:, m, :], w_raw[:, m, :], ACT.Copy).then_inc(w_hi_done, 1)

            def chunk_hi(c_col, half, number, bank):
                act.wait_ge(fill_done, number + 1)
                act.activation(xT_hi[half][:, :, bass.ds(c_col, CH)],
                               t_ps[bank][:, :].rearrange("p (k t) -> p k t", k=KT), ACT.Copy)\
                    .then_inc(hi_done, 1)

            def qk_hi_part(m, n, g):
                act.wait_ge(proj_done, n * 3 + m + 1)
                if not (isinstance(n, int) and n == 0) and m == Q:
                    for pair in range(2):
                        act.wait_ge(stacked[pair], n * 12 * 16)
                act.activation(qk_hi[:, m, :], proj_ps[m][:, :], ACT.Identity, bias=bias[:, m, bass.ds(g, 1)])\
                    .then_inc(qk_hi_done, 1)

            def prologue():
                act.wait_ge(bias_in, 16)
                for m in (Q, K, V):
                    split_w_hi(m, 0)
                for c in range(CHUNKS_AHEAD):
                    chunk_hi((c % 8) * CH, c // 8, c, c % 2)
                qk_hi_part(Q, 0, 0)
                split_w_hi(Q, 1)
                qk_hi_part(K, 0, 0)
                split_w_hi(K, 1)

            def step(b, g):
                n = step_of(b, g)
                nb, ng = next_pos(b, g)
                for h in range(GH):
                    s = n * GH + h
                    if not first(b, g, h, 3):
                        act.wait_ge(pv_done, s - 2)
                        act.activation(o_low[:, :], o_ps[HD:2 * HD, :], ACT.Copy).then_inc(low_copied, 1)
                    if h == 0:
                        act.wait_ge(proj_done, n * 3 + V + 1)
                        act.activation(vT[:, :], proj_ps[0][:, :], ACT.Identity, bias=bias[:, V, bass.ds(g, 1)])\
                            .then_inc(v_done, 1)
                    if h == 2:
                        act.wait_ge(fill_done, fill(b, g, 6) + 1)
                        act.activation(v_parts[:, :, :, 0:HD],
                                       t_ps[0][:, :].rearrange("p (k h d) -> p k h d", k=QT, h=GH),
                                       ACT.Copy).then_inc(hi_done, 1)
                    prev = (h + 1) % 2

                    def prob_hi(f):
                        i = slot_fill(h, f)
                        act.wait_ge(fill_done, fill(b, g, i) + 1)
                        w = P * len(T_FILLS[f])
                        act.activation(pT_hi[prev][:, T_DEST[f]:T_DEST[f] + w], t_ps[i % 2][:, 0:w],
                                       ACT.Copy).then_inc(hi_done, 1)

                    if not first(b, g, h, 1):
                        prob_hi(0)
                        prob_hi(1)
                    act.wait_ge(negmax_done, s + 1)
                    for qt in range(QT):
                        w = P * (qt + 1)
                        last_exp = act.activation(
                            probs[h % 2][:, P_OFF[qt]:P_OFF[qt] + w], score_ps[:, S_COL[qt]:S_COL[qt] + w],
                            ACT.Exp, bias=neg_max[h % 2][:, qt:qt + 1], scale=SCALE,
                            accum_out=row_sum[h % 2][:, qt:qt + 1])
                    last_exp.then_inc(exp_done, 1)
                    if not first(b, g, h, 1):
                        prob_hi(2)
                    if last(b, g):
                        continue
                    if h == 0:
                        split_w_hi(V, n + 1)
                    if h == 1:
                        qk_hi_part(Q, n + 1, ng)
                    if h == 2:
                        qk_hi_part(K, n + 1, ng)
                        split_w_hi(Q, n + 2)
                    if h == 3:
                        if has_chunk(b, g):
                            half = (b + 1 + (1 if isinstance(g, int) and g == GROUPS - 1 else 0)) % 2
                            col = 0 if isinstance(g, int) and g == GROUPS - 1 else (g + 1) * CH
                            chunk_hi(col, half, fill(b, g, 13), 1)
                        split_w_hi(K, n + 2)

            def tail():
                s = STEPS * GH
                act.wait_ge(pv_done, s - 2)
                act.activation(o_low[:, :], o_ps[HD:2 * HD, :], ACT.Copy).then_inc(low_copied, 1)
                for f in range(3):
                    act.wait_ge(fill_done, fill(BATCH - 1, GROUPS, f) + 1)
                    w = P * len(T_FILLS[f])
                    act.activation(pT_hi[1][:, T_DEST[f]:T_DEST[f] + w], t_ps[f % 2][:, 0:w],
                                   ACT.Copy).then_inc(hi_done, 1)
                for k in (1, 0):
                    act.wait_ge(pv_done, s - k)
                    act.activation(o_low[:, :], o_ps[HD:2 * HD, :], ACT.Copy).then_inc(low_copied, 1)

            emit(act, prologue, step, tail)

        @block.vector
        def _(dve):
            def stats(c):
                dve.wait_ge(x_loaded, c * 16 + 16)
                for half in range(2):
                    last_bn = dve.bn_stats(bn[:, half, :], x_in[:, half * 512:(half + 1) * 512])
                last_bn.then_inc(bn_done, 1)
                dve.wait_ge(bn_done, c + 1)
                if not (isinstance(c, int) and c == 0):
                    dve.wait_ge(xn_done, c)
                hold(dve)
                dve.bn_aggr(mv[:, :], bn[:, :, :].rearrange("p a b -> p (a b)")).then_inc(stats_done, 1)

            def lo_part(dst, src, hi, number):
                dve.wait_ge(hi_done, number + 1)
                dve.tensor_tensor(dst, src, hi, ALU.subtract).then_inc(lo_done, 1)

            def chunk_lo(c_col, half, number, bank):
                cols = bass.ds(c_col, CH)
                lo_part(xT_lo[half][:, :, cols], t_ps[bank][:, :].rearrange("p (k t) -> p k t", k=KT),
                        xT_hi[half][:, :, cols].bitcast(F32), number)

            def qk_lo_part(m, n, g):
                dve.wait_ge(qk_hi_done, n * 2 + m + 1)
                dve.scalar_tensor_tensor(qk_lo[:, m, :], proj_ps[m][:, :], bias[:, m, bass.ds(g, 1)],
                                         qk_hi[:, m, :].bitcast(F32), ALU.add, ALU.subtract)\
                    .then_inc(qk_lo_done, 1)

            def combine(h, s, quadrant_use):
                head = (h + 1) % GH
                dve.wait_ge(low_copied, s - 2)
                if quadrant_use is not None:
                    dve.wait_ge(stored[head], quadrant_use * 16 + 16)
                dve.tensor_tensor(o_out[head * HD:(head + 1) * HD, :], o_ps[0:HD, :], o_low[:, :],
                                  ALU.add).then_inc(head_done, 1)

            def prologue():
                for i in range(2):
                    dve.memset(pT_hi[i][:, 0:P].bitcast(F32), 0.0)
                    dve.memset(pT_lo[i][:, 0:P].bitcast(F32), 0.0).then_inc(zeros_done, 1)
                dve.wait_ge(bias_in, 16)
                stats(0)
                for c in range(CHUNKS_AHEAD):
                    if c + 1 < CHUNKS_AHEAD:
                        stats(c + 1)
                    chunk_lo((c % 8) * CH, c // 8, c, c % 2)
                qk_lo_part(Q, 0, 0)
                qk_lo_part(K, 0, 0)

            def step(b, g):
                n = step_of(b, g)
                nb, ng = next_pos(b, g)
                for h in range(GH):
                    s = n * GH + h
                    par, prev = h % 2, (h + 1) % 2
                    if not first(b, g, h, 3):
                        uses = (n - 1) if h < 3 else n
                        combine(h, s, uses)
                    if h == 2:
                        lo_part(v_parts[:, :, :, HD:2 * HD],
                                t_ps[0][:, :].rearrange("p (k h d) -> p k h d", k=QT, h=GH),
                                v_parts[:, :, :, 0:HD].bitcast(F32), fill(b, g, 6))
                    dve.wait_ge(scores_done, s + 1)
                    for qt in range(QT):
                        last_max = dve.tensor_reduce(row_max[par][:, qt:qt + 1],
                                                     score_ps[:, S_COL[qt]:S_COL[qt] + P * (qt + 1)],
                                                     AXIS.X, ALU.max)
                    last_max.then_inc(max_done, 1)
                    dve.wait_ge(max_done, s + 1)
                    dve.tensor_scalar(neg_max[par][:, :], row_max[par][:, :], -SCALE, None, ALU.mult)\
                        .then_inc(negmax_done, 1)

                    def prob_lo(f):
                        i = slot_fill(h, f)
                        w = P * len(T_FILLS[f])
                        cols = slice(T_DEST[f], T_DEST[f] + w)
                        lo_part(pT_lo[prev][:, cols], t_ps[i % 2][:, 0:w], pT_hi[prev][:, cols].bitcast(F32),
                                fill(b, g, i))

                    if not first(b, g, h, 1):
                        prob_lo(0)
                        prob_lo(1)
                    dve.wait_ge(exp_done, s + 1)
                    dve.reciprocal(inv_sum[par][:, :], row_sum[par][:, :]).then_inc(inv_done, 1)
                    dve.wait_ge(inv_done, s + 1)
                    for qt in range(QT):
                        cols = slice(P_OFF[qt], P_OFF[qt] + P * (qt + 1))
                        last_norm = dve.tensor_scalar(probs[par][:, cols], probs[par][:, cols],
                                                      inv_sum[par][:, qt:qt + 1], None, ALU.mult)
                    last_norm.then_inc(norm_done, 1)
                    if not first(b, g, h, 1):
                        prob_lo(2)
                    if last(b, g):
                        continue
                    if h == 0 and has_chunk(b, g):
                        stats(n + CHUNKS_AHEAD)
                    if h == 1:
                        qk_lo_part(Q, n + 1, ng)
                    if h == 2:
                        qk_lo_part(K, n + 1, ng)
                    if h == 3 and has_chunk(b, g):
                        half = (b + 1 + (1 if isinstance(g, int) and g == GROUPS - 1 else 0)) % 2
                        col = 0 if isinstance(g, int) and g == GROUPS - 1 else (g + 1) * CH
                        chunk_lo(col, half, fill(b, g, 13), 1)

            def tail():
                s = STEPS * GH
                combine(0, s, STEPS - 1)
                for f in range(3):
                    w = P * len(T_FILLS[f])
                    cols = slice(T_DEST[f], T_DEST[f] + w)
                    lo_part(pT_lo[1][:, cols], t_ps[f % 2][:, 0:w], pT_hi[1][:, cols].bitcast(F32),
                            fill(BATCH - 1, GROUPS, f))
                combine(1, s + 1, STEPS - 1)
                combine(2, s + 2, STEPS - 1)

            emit(dve, prologue, step, tail)

        @block.tensor
        def _(pe):
            def chunk_transposes(c, number, bank):
                pe.wait_ge(xn_done, c + 1)
                bank_free(number)
                hold(pe)
                for kt in range(KT):
                    last = pe.transpose(t_ps[bank][:, kt * CH:(kt + 1) * CH],
                                        xn[:, kt * P:(kt + 1) * P], ident[0:CH, 0:CH])
                last.then_inc(fill_done, 1)

            def bank_free(number, whole=False):
                if isinstance(number, int) and number < 2:
                    return
                pe.wait_ge(lo_done, number if whole else number - 1)

            def project(m, n, half, lo, hi):
                bank = proj_ps[m % 2]
                if lo == 0:
                    pe.wait_ge(w_lo_done, n * 3 + m + 1)
                    if not (isinstance(n, int) and n == 0):
                        if m == Q:
                            pe.wait_ge(v_done, n)
                        elif m == K:
                            pe.wait_ge(qk_lo_done, n * 2)
                    if m == V:
                        pe.wait_ge(qk_lo_done, n * 2 + 1)
                for i in range(lo, hi):
                    kt, part = i // 3, i % 3
                    w = (w_hi, w_hi, w_lo)[part]
                    xt = (xT_hi, xT_lo, xT_hi)[part][half]
                    mm = pe.matmul(bank[:, :], w[:, m, kt * P:(kt + 1) * P], xt[:, kt, :],
                                   start=(i == 0), stop=(i == 23))
                if hi == 24:
                    mm.then_inc(proj_done, 1)

            def scores(b, g, h):
                n = step_of(b, g)
                if h % 2 == 0:
                    pe.wait_ge(stacked[h // 2], n * 12 * 16 + 12 * 16)
                if not first(b, g, h, 1):
                    pe.wait_ge(exp_done, n * GH + h)
                for qt in range(QT):
                    pe.matmul(score_ps[:, S_COL[qt]:S_COL[qt] + S_KEYS[qt]],
                              q_stack[:, h, qt * P:(qt + 1) * P], k_stack[:, h, 0:S_KEYS[qt]],
                              start=True, stop=False)
                    diagonal = S_COL[qt] + qt * P
                    mm = pe.matmul(score_ps[:, diagonal:diagonal + P], identb[:, :], maskb[:, :],
                                   start=False, stop=True)
                mm.then_inc(scores_done, 1)

            def prob_transposes(b, g, h, f, parity):
                i = slot_fill(h, f)
                number = fill(b, g, i)
                bank_free(number, whole=(i == 0))
                for col, (kt, qt) in enumerate(T_FILLS[f]):
                    at = P_OFF[qt] + kt * P
                    mm = pe.transpose(t_ps[i % 2][:, col * P:(col + 1) * P],
                                      probs[parity][:, at:at + P], ident[:, :])
                mm.then_inc(fill_done, 1)

            def attend(h, parity, s, lo_needed):
                pe.wait_ge(lo_done, lo_needed)
                pe.wait_ge(head_done, s - 2) if s is not None else None
                first_mm = True
                for pT in (pT_hi[parity], pT_lo[parity]):
                    for kt in range(QT):
                        at = PT_KT[kt]
                        q0 = PT_QT[kt] * P
                        mm = pe.matmul(o_ps[:, q0:SEQ], v_parts[:, kt, h, :], pT[:, at:at + SEQ - q0],
                                       start=first_mm, stop=(pT is pT_lo[parity] and kt == QT - 1))
                        first_mm = False
                mm.then_inc(pv_done, 1)

            def prologue():
                pe.wait_ge(consts, 5)
                for c in range(CHUNKS_AHEAD):
                    chunk_transposes(c, c, c % 2)
                pe.wait_ge(lo_done, SEQ // CH)
                for m in (Q, K, V):
                    project(m, 0, 0, 0, 24)
                pe.wait_ge(zeros_done, 2)

            def step(b, g):
                n = step_of(b, g)
                nb, ng = next_pos(b, g)
                todo = [] if last(b, g) else [(m, i) for m in (Q, K, V) for i in range(24)]

                def projections(count):
                    while count and todo:
                        m, lo = todo[0]
                        run = min(count, 24 - lo)
                        project(m, n + 1, nb % 2, lo, lo + run)
                        del todo[:run]
                        count -= run

                for h in range(GH):
                    prev = (h + 1) % 2
                    scores(b, g, h)
                    if not first(b, g, h, 1):
                        pe.wait_ge(norm_done, n * GH + h)
                        prob_transposes(b, g, h, 0, prev)
                        prob_transposes(b, g, h, 1, prev)
                    if isinstance(g, int) and g == GROUPS - 1 and h == 0 and b + 1 < BATCH:
                        pe.wait_ge(lo_done, fill(b, g, 0))
                    projections(8)
                    if not first(b, g, h, 1):
                        prob_transposes(b, g, h, 2, prev)
                    projections(10)
                    if not first(b, g, h, 2):
                        needed = fill(b, g, 0) if h == 0 else fill(b, g, slot_fill(h - 1, 2)) + 1
                        attend((h + 2) % GH, h % 2, n * GH + h, needed)
                    if h == 1:
                        pe.wait_ge(v_done, n + 1)
                        bank_free(fill(b, g, 6))
                        for kt in range(QT):
                            mm = pe.transpose(t_ps[0][:, kt * P:(kt + 1) * P], vT[:, kt * P:(kt + 1) * P],
                                              ident[:, :])
                        mm.then_inc(fill_done, 1)
                    if h == 3 and has_chunk(b, g):
                        chunk_transposes(n + CHUNKS_AHEAD, fill(b, g, 13), 1)

            def tail():
                n = STEPS
                pe.wait_ge(norm_done, n * GH)
                for f in range(3):
                    number = fill(BATCH - 1, GROUPS, f)
                    bank_free(number, whole=(f == 0))
                    for col, (kt, qt) in enumerate(T_FILLS[f]):
                        at = P_OFF[qt] + kt * P
                        mm = pe.transpose(t_ps[f % 2][:, col * P:(col + 1) * P],
                                          probs[1][:, at:at + P], ident[:, :])
                    mm.then_inc(fill_done, 1)
                attend(2, 0, n * GH, fill(BATCH - 1, GROUPS, 0))
                attend(3, 1, n * GH + 1, fill(BATCH - 1, GROUPS, 2) + 1)

            emit(pe, prologue, step, tail)


TILES = TOKENS // P
HALVES = D // SEQ
OTILES = D // P
DQ_OPS = 22


def output_phase(nc, outer, x, wo, bo, att, qweight, lut4, x1, wl_hi, wl_lo, shifts):
    with ExitStack() as buffers:
        ph = Phase(nc, buffers, outer)
        sb, pb, sem = ph.sb, ph.pb, ph.sem
        ident = sb("ident2", [P, P])
        wo_hi = sb("wo_hi", [P, KT, D], F32R)
        wo_lo = sb("wo_lo", [P, KT, D], F32R)
        bo_all = sb("bo_all", [P, D])
        att_raw = [sb(f"att_raw{i}", [P, KT, P]) for i in range(2)]
        att_hi = [sb(f"att_hi{i}", [P, KT, P], F32R) for i in range(2)]
        att_lo = [sb(f"att_lo{i}", [P, KT, P], F32R) for i in range(2)]
        x_t = [sb(f"x_t{i}", [P, D]) for i in range(2)]
        words = sb("words", [P, 4, 32], I32)
        lut_in = sb("lut_in", [P, 16])
        lut = sb("lut", [P, 16])
        lut_xor = sb("lut_xor", [P, 8], I32)
        bits = [sb(f"bits{i}", [P, D], I32) for i in range(4)]
        r = [sb(f"r{i}", [P, D], I32) for i in range(4)]
        out_ps = [pb(f"out_ps{i}", [P, SEQ]) for i in range(4)]
        wt_ps = [pb(f"wt_ps{i}", [P, SEQ]) for i in range(2)]

        ident_done = sem("ident2_done")
        bo_loaded = sem("bo_loaded")
        wo_loaded = [sem(f"wo_loaded{i}") for i in range(2)]
        wo_hi_done = sem("wo_hi_done")
        wo_lo_done = sem("wo_lo_done")
        att_loaded = [sem(f"att_loaded{i}") for i in range(2)]
        att_hi_done = sem("att_hi_done")
        att_lo_done = sem("att_lo_done")
        xt_loaded = [sem(f"xt_loaded{i}") for i in range(2)]
        xb_done = sem("xb_done")
        mm_done = sem("mm_done")
        x1_done = sem("x1_done")
        x1_stored = [sem(f"x1_stored{i}") for i in range(2)]
        words_loaded = sem("words_loaded")
        dq_done = sem("dq_done")
        wt_done = sem("wt_done")
        wt_hi_done = sem("wt_hi_done")
        wt_lo_done = sem("wt_lo_done")
        waited = sem("waited2")

        def emit(body, tail):
            return body, tail

        block = buffers.enter_context(nc.Block())

        @block.sync
        def _(sp):
            def load_words(p):
                if not (isinstance(p, int) and p == 0):
                    sp.wait_ge(dq_done, (p - 1) * DQ_OPS + 7)
                    sp.sem_inc(waited, 1)
                sp.dma_start(words[:, :, :], qweight[0:4, bass.ds(p * P, P), :].rearrange("b o w -> o b w"))\
                    .then_inc(words_loaded, 16)
                sp.dma_start(lut_in[:, :], lut4[bass.ds(p * P, P), :]).then_inc(words_loaded, 16)

            def load_att(p, par):
                if not (isinstance(p, int) and p == 0):
                    sp.wait_ge(att_lo_done, p * 2 + (par - 1))
                    sp.sem_inc(waited, 1)
                first_row = (p // 2) * GROUPS
                col = (p % 2) * (2 * P) + par * P
                sp.dma_start(att_raw[par][:, :, :],
                             att[bass.ds(first_row, GROUPS), :, bass.ds(col, P)].rearrange("g p t -> p g t"))\
                    .then_inc(att_loaded[par], 16)

            def store_x1(p, par):
                sp.wait_ge(x1_done, p * 2 + (par + 1))
                sp.sem_inc(waited, 1)
                sp.dma_start(x1[bass.ds(p * (2 * P) + par * P, P), :], x_t[par][:, :]).then_inc(x1_stored[par], 16)

            def load_x(p, par):
                if not (isinstance(p, int) and p == 0):
                    sp.wait_ge(x1_stored[par], p * 16)
                    sp.sem_inc(waited, 1)
                sp.dma_start(x_t[par][:, :], x[bass.ds(p * (2 * P) + par * P, P), :]).then_inc(xt_loaded[par], 16)

            load_words(0)
            for kt in range(KT):
                if kt >= 2:
                    sp.wait_ge(wo_lo_done, kt - 1)
                sp.dma_start(r[kt % 2][:, :].bitcast(F32), wo[:, kt, :]).then_inc(wo_loaded[kt % 2], 16)
                if kt == 1:
                    sp.dma_start(bo_all[:, :], bo.partition_broadcast(P)).then_inc(bo_loaded, 16)
                    for par in range(2):
                        load_att(0, par)
                        load_x(0, par)
            with sp.Fori(1, OTILES) as p:
                load_att(p, 0)
                store_x1(p - 1, 0)
                load_x(p, 0)
                load_words(p)
                load_att(p, 1)
                store_x1(p - 1, 1)
                load_x(p, 1)
            for par in range(2):
                store_x1(OTILES - 1, par)
            for par in range(2):
                sp.wait_ge(x1_stored[par], TILES // 2 * 16)

        @block.gpsimd
        def _(pool):
            def add_bias(p, par):
                pool.wait_ge(xt_loaded[par], p * 16 + 16)
                pool.tensor_tensor(x_t[par][:, :], x_t[par][:, :], bo_all[:, :], ALU.add).then_inc(xb_done, 1)

            def split_lo(t, p, par):
                pool.wait_ge(att_hi_done, t + 1)
                pool.tensor_tensor(att_lo[par][:, :, :], att_raw[par][:, :, :],
                                   att_hi[par][:, :, :].bitcast(F32), ALU.subtract).then_inc(att_lo_done, 1)

            pool.memset(ident[:, :], 0.0).then_inc(ident_done, 1)
            pool.wait_ge(ident_done, 1)
            pool.affine_select(out=ident[:, :], in_=ident[:, :], compare_op=ALU.not_equal, fill=1.0,
                               base=0, pattern=[[-1, P]], channel_multiplier=1).then_inc(ident_done, 1)
            pool.wait_ge(bo_loaded, 16)

            def body(p):
                for par in range(2):
                    split_lo(p * 2 + par, p, par)
                    add_bias(p, par)

            with pool.Fori(0, OTILES) as p:
                body(p)

        @block.scalar
        def _(act):
            def split_hi(p, par):
                act.wait_ge(att_loaded[par], p * 16 + 16)
                if not (isinstance(p, int) and p == 0):
                    act.wait_ge(mm_done, p * 4 + (2 * par - 2))
                act.activation(att_hi[par][:, :, :], att_raw[par][:, :, :], ACT.Copy).then_inc(att_hi_done, 1)

            def weights_hi(p):
                for half in range(2):
                    act.wait_ge(wt_done, p * 2 + half + 1)
                    act.activation(wl_hi[:, 4 * half:4 * half + 4, bass.ds(p * P, P)],
                                   wt_ps[half][:, :].rearrange("p (k o) -> p k o", k=4), ACT.Copy)\
                        .then_inc(wt_hi_done, 1)

            for kt in range(KT):
                act.wait_ge(wo_loaded[kt % 2], 16 * (kt // 2 + 1))
                act.activation(wo_hi[:, kt, :], r[kt % 2][:, :].bitcast(F32), ACT.Copy).then_inc(wo_hi_done, 1)
                if kt == 1:
                    split_hi(0, 0)
                    split_hi(0, 1)
            with act.Fori(1, OTILES) as p:
                split_hi(p, 0)
                split_hi(p, 1)
                weights_hi(p - 1)
            weights_hi(OTILES - 1)

        @block.vector
        def _(dve):
            def dequantize(p):
                count = [0]

                def chained(instruction):
                    count[0] += 1
                    instruction.then_inc(dq_done, 1)
                    dve.wait_ge(dq_done, p * DQ_OPS + count[0])

                def by_bit(n):
                    return r[n][:, :]

                def leaf(n, j):
                    chained(dve.tensor_scalar(r[n][:, :], bits[0][:, :], lut_xor[:, j:j + 1],
                                              lut[:, 2 * j:2 * j + 1].bitcast(I32),
                                              ALU.bitwise_and, ALU.bitwise_xor))

                def select(n, plane, m):
                    dve.sem_inc(waited, 1)
                    chained(dve.copy_predicated(by_bit(n), bits[plane][:, :], by_bit(m)))

                def word(plane):
                    return words[:, plane, :].unsqueeze(2).to_broadcast([P, 32, 32])

                def pattern(row):
                    return shifts[:, row, :].unsqueeze(1).to_broadcast([P, 32, 32])

                def spread(plane):
                    return bits[plane][:, :].rearrange("p (w s) -> p w s", s=32)

                dve.wait_ge(words_loaded, p * 32 + 32)
                chained(dve.tensor_copy(lut[:, :], lut_in[:, :]))
                yield
                pairs = lut[:, :].bitcast(I32).rearrange("p (j b) -> p j b", b=2)
                chained(dve.tensor_tensor(lut_xor[:, :], pairs[:, :, 0], pairs[:, :, 1], ALU.bitwise_xor))
                yield
                chained(dve.tensor_tensor(spread(0), word(0), pattern(0), ALU.logical_shift_left))
                yield
                for plane in (1, 2, 3):
                    chained(dve.tensor_tensor(spread(plane), word(plane), pattern(1), ALU.bitwise_and))
                    yield
                chained(dve.tensor_scalar(bits[0][:, :], bits[0][:, :], 31, None, ALU.arith_shift_right))
                yield
                if not (isinstance(p, int) and p == 0):
                    dve.wait_ge(wt_done, p * 2)
                leaf(0, 0)
                yield
                leaf(1, 1)
                yield
                select(0, 1, 1)
                yield
                leaf(1, 2)
                yield
                leaf(2, 3)
                yield
                select(1, 1, 2)
                yield
                select(0, 2, 1)
                yield
                leaf(1, 4)
                yield
                leaf(2, 5)
                yield
                select(1, 1, 2)
                yield
                leaf(2, 6)
                yield
                leaf(3, 7)
                yield
                select(2, 1, 3)
                yield
                select(1, 2, 2)
                yield
                select(0, 3, 1)
                assert count[0] == DQ_OPS
                yield

            def finish_x1(p, par):
                dve.wait_ge(xb_done, p * 2 + (par + 1))
                for half in range(HALVES):
                    cols = slice(half * SEQ, (half + 1) * SEQ)
                    dve.wait_ge(mm_done, p * 4 + (2 * par + half + 1))
                    add = dve.tensor_tensor(x_t[par][:, cols], out_ps[2 * par + half][:, :], x_t[par][:, cols],
                                            ALU.add)
                add.then_inc(x1_done, 1)

            def weights_lo(p):
                for half in range(2):
                    at = wl_hi[:, 4 * half:4 * half + 4, bass.ds(p * P, P)]
                    dve.wait_ge(wt_hi_done, p * 2 + half + 1)
                    dve.tensor_tensor(wl_lo[:, 4 * half:4 * half + 4, bass.ds(p * P, P)],
                                      wt_ps[half][:, :].rearrange("p (k o) -> p k o", k=4), at.bitcast(F32),
                                      ALU.subtract).then_inc(wt_lo_done, 1)

            for kt in range(KT):
                dve.wait_ge(wo_hi_done, kt + 1)
                dve.tensor_tensor(wo_lo[:, kt, :], r[kt % 2][:, :].bitcast(F32), wo_hi[:, kt, :].bitcast(F32),
                                  ALU.subtract).then_inc(wo_lo_done, 1)

            def body(p):
                ops = dequantize(p)
                for _ in range(7):
                    next(ops)
                if not (isinstance(p, int) and p == 0):
                    weights_lo(p - 1)
                for _ in range(5):
                    next(ops)
                finish_x1(p, 0)
                for _ in ops:
                    pass
                finish_x1(p, 1)

            dve.wait_ge(wo_lo_done, KT)
            dve.sem_inc(wt_lo_done, 2)
            body(0)
            with dve.Fori(1, OTILES) as p:
                body(p)
            weights_lo(OTILES - 1)

        @block.tensor
        def _(pe):
            def multiply(p, par, half):
                if half == 0:
                    pe.wait_ge(att_lo_done, p * 2 + (par + 1))
                if not (isinstance(p, int) and p == 0):
                    pe.wait_ge(x1_done, p * 2 + (par - 1))
                cols = slice(half * SEQ, (half + 1) * SEQ)
                for kt in range(KT):
                    for part in range(3):
                        if isinstance(p, int) and p == 0 and par == 0 and half == 0 and part == 0:
                            pe.wait_ge(wo_lo_done, kt + 1)
                        a = (att_hi, att_lo, att_hi)[part][par]
                        w = (wo_hi, wo_hi, wo_lo)[part]
                        mm = pe.matmul(out_ps[2 * par + half][:, :], a[:, kt, :], w[:, kt, cols],
                                       start=(kt == 0 and part == 0), stop=(kt == KT - 1 and part == 2))
                mm.then_inc(mm_done, 1)

            def transpose_weights(p):
                pe.wait_ge(dq_done, (p + 1) * DQ_OPS)
                pe.wait_ge(wt_lo_done, p * 2 + 2)
                for half in range(2):
                    for i in range(4):
                        at = (4 * half + i) * P
                        mm = pe.transpose(wt_ps[half][:, i * P:(i + 1) * P], r[0][:, at:at + P].bitcast(F32),
                                          ident[:, :])
                    mm.then_inc(wt_done, 1)

            pe.wait_ge(ident_done, 2)

            def body(p):
                multiply(p, 0, 0)
                if not (isinstance(p, int) and p == 0):
                    transpose_weights(p - 1)
                multiply(p, 0, 1)
                multiply(p, 1, 0)
                multiply(p, 1, 1)

            body(0)
            with pe.Fori(1, OTILES) as p:
                body(p)
            transpose_weights(OTILES - 1)


def feed_forward_phase(nc, outer, x1, fbias, out, wl_hi, wl_lo, flag, tag, high, run_if=None):
    with ExitStack() as buffers:
        ph = Phase(nc, buffers, outer)

        def sb(name, shape, dt=F32):
            return ph.sb(name + tag, shape, dt)

        def pb(name, shape, dt=F32):
            return ph.pb(name + tag, shape, dt)

        def sem(name):
            return ph.sem(name + tag)

        ident = sb("f_ident", [P, P])
        neg_half = sb("f_neg_half", [P, 1])
        bias_all = sb("f_bias_all", [P, D])
        x_t = [sb(f"f_x{i}", [P, D]) for i in range(2)]
        xb = [sb(f"f_xb{i}", [P, D]) for i in range(2)]
        xn = [sb(f"f_xn{i}", [P, D]) for i in range(2)]
        squares = sb("f_squares", [P, D])
        bn = sb("f_bn", [P, 2, 6])
        mv = sb("f_mv", [P, 2])
        rs = sb("f_rs", [P, 4])
        xT_hi = [sb(f"f_xT_hi{i}", [P, KT, P], F32R) for i in range(2)]
        xT_lo = [sb(f"f_xT_lo{i}", [P, KT, P], F32R) for i in range(2)]
        norm_sq = [sb(f"f_norm_sq{i}", [P, 1]) for i in range(2)]
        worst = sb("f_worst", [P, 1])
        worst_all = sb("f_worst_all", [P, 1])
        chosen = [sb(f"f_chosen{i}", [P, 1], I32) for i in range(2)]
        old = [sb(f"f_old{i}", [P, D]) for i in range(2)] if high else None
        t_ps = [pb(f"f_t{i}", [P, SEQ]) for i in range(2)]
        y_ps = [pb(f"f_y{i}", [P, SEQ]) for i in range(4)]

        consts = sem("f_consts")
        bias_loaded = sem("f_bias_loaded")
        x_loaded = [sem(f"f_x_loaded{i}") for i in range(2)]
        old_loaded = [sem(f"f_old_loaded{i}") for i in range(2)]
        bn_done = sem("f_bn_done")
        stats_done = sem("f_stats_done")
        rstd_chain = sem("f_rstd_chain")
        rstd_done = sem("f_rstd_done")
        xn_done = sem("f_xn_done")
        norm_done = sem("f_norm_done")
        worst_done = sem("f_worst_done")
        xb_done = sem("f_xb_done")
        fill_done = sem("f_fill_done")
        hi_done = sem("f_hi_done")
        lo_done = sem("f_lo_done")
        mm_done = sem("f_mm_done")
        y_done = sem("f_y_done")
        out_done = sem("f_out_done")
        stored = [sem(f"f_stored{i}") for i in range(2)]
        worst_all_done = sem("f_worst_all_done")
        waited = sem("f_waited")

        block = buffers.enter_context(nc.Block())

        def guarded(eng, program):
            if run_if is None:
                program()
                return
            value = eng.value_load(run_if[0:1, 0:1], min_val=0, max_val=1)
            with eng.If(value > 0):
                program()
            with eng.Else():
                eng.nop()

        @block.sync
        def _(sp):
            def load(p, par):
                rows = bass.ds(p * (2 * P) + par * P, P)
                if not (isinstance(p, int) and p == 0):
                    sp.wait_ge(xn_done, p * 2 + (par - 1))
                    sp.sem_inc(waited, 1)
                    sp.wait_ge(xb_done, p * 2 + (par - 1))
                    sp.sem_inc(waited, 1)
                sp.dma_start(x_t[par][:, :], x1[rows, :]).then_inc(x_loaded[par], 16)
                if high:
                    if not (isinstance(p, int) and p == 0):
                        sp.wait_ge(stored[par], p * 16)
                        sp.sem_inc(waited, 1)
                    sp.dma_start(old[par][:, :], out[rows, :]).then_inc(old_loaded[par], 16)

            def store(p, par):
                sp.wait_ge(out_done, p * 2 + (par + 1))
                sp.sem_inc(waited, 1)
                src = old[par] if high else xb[par]
                sp.dma_start(out[bass.ds(p * (2 * P) + par * P, P), :], src[:, :]).then_inc(stored[par], 16)

            def program():
                load(0, 0)
                sp.dma_start(bias_all[:, :], fbias.partition_broadcast(P)).then_inc(bias_loaded, 16)
                load(0, 1)
                with sp.Fori(1, TILES // 2) as p:
                    if high:
                        store(p - 1, 0)
                        load(p, 0)
                        store(p - 1, 1)
                        load(p, 1)
                    else:
                        load(p, 0)
                        store(p - 1, 0)
                        load(p, 1)
                        store(p - 1, 1)
                for par in range(2):
                    store(TILES // 2 - 1, par)
                for par in range(2):
                    sp.wait_ge(stored[par], TILES // 2 * 16)

            guarded(sp, program)

        @block.gpsimd
        def _(pool):
            def rstd(p, par):
                t = p * 2 + par
                base = p * 10 + par * 5
                pool.wait_ge(stats_done, t + 1)
                pool.sem_inc(waited, 1)
                pool.tensor_scalar(rs[:, 0:1], mv[:, 1:2], EPS, None, ALU.add).then_inc(rstd_chain, 1)
                pool.wait_ge(rstd_chain, base + 1)
                pool.tensor_tensor(rs[:, 1:2], rs[:, 0:1], neg_half[:, :], ALU.pow).then_inc(rstd_chain, 1)
                pool.wait_ge(rstd_chain, base + 2)
                pool.tensor_tensor(rs[:, 2:3], rs[:, 1:2], rs[:, 1:2], ALU.mult).then_inc(rstd_chain, 1)
                pool.wait_ge(rstd_chain, base + 3)
                pool.tensor_tensor(rs[:, 2:3], rs[:, 2:3], rs[:, 0:1], ALU.mult).then_inc(rstd_chain, 1)
                pool.wait_ge(rstd_chain, base + 4)
                pool.sem_inc(waited, 1)
                pool.tensor_scalar(rs[:, 2:3], rs[:, 2:3], -0.5, 1.5, ALU.mult, ALU.add).then_inc(rstd_chain, 1)
                pool.wait_ge(rstd_chain, base + 5)
                pool.tensor_tensor(rs[:, 3:4], rs[:, 1:2], rs[:, 2:3], ALU.mult).then_inc(rstd_done, 1)

            def add_bias(p, par):
                if not (isinstance(p, int) and p == 0):
                    if high:
                        pool.wait_ge(out_done, p * 2 + (par - 1))
                    else:
                        pool.wait_ge(stored[par], p * 16)
                pool.wait_ge(x_loaded[par], p * 16 + 16)
                pool.tensor_tensor(xb[par][:, :], x_t[par][:, :], bias_all[:, :], ALU.add).then_inc(xb_done, 1)

            def program():
                pool.memset(neg_half[:, :], -0.5)
                pool.memset(ident[:, :], 0.0).then_inc(consts, 1)
                pool.wait_ge(consts, 1)
                pool.affine_select(out=ident[:, :], in_=ident[:, :], compare_op=ALU.not_equal, fill=1.0,
                                   base=0, pattern=[[-1, P]], channel_multiplier=1).then_inc(consts, 1)
                pool.wait_ge(bias_loaded, 16)

                def body(p):
                    for par in range(2):
                        rstd(p, par)
                        add_bias(p, par)

                body(0)
                with pool.Fori(1, TILES // 2) as p:
                    body(p)
                if not high:
                    pool.wait_ge(worst_done, TILES + 1)
                    pool.partition_all_reduce(worst_all[:, :], worst[:, :], P, bass.bass_isa.ReduceOp.max)\
                        .then_inc(worst_all_done, 1)

            guarded(pool, program)

        @block.scalar
        def _(act):
            def norms(p, par):
                t = p * 2 + par
                act.wait_ge(xn_done, t + 1)
                if not (isinstance(p, int) and p == 0):
                    act.wait_ge(worst_done, t)
                act.activation(squares[:, :], xn[par][:, :], ACT.Square, accum_out=norm_sq[par][:, :])\
                    .then_inc(norm_done, 1)

            def split_hi(p, par):
                for half in range(2):
                    act.wait_ge(fill_done, p * 4 + (2 * par + half + 1))
                    act.activation(xT_hi[par][:, 4 * half:4 * half + 4, :],
                                   t_ps[half][:, :].rearrange("p (k t) -> p k t", k=4), ACT.Copy)\
                        .then_inc(hi_done, 1)

            def program():
                def body(p):
                    for par in range(2):
                        split_hi(p, par)
                        if not (isinstance(p, int) and p == 0 and par == 0):
                            act.wait_ge(norm_done, p * 2 + par)
                        norms(p, par)

                body(0)
                with act.Fori(1, TILES // 2) as p:
                    body(p)

            guarded(act, program)

        @block.vector
        def _(dve):
            def normalize(p, par):
                t = p * 2 + par
                dve.wait_ge(x_loaded[par], p * 16 + 16)
                for half in range(2):
                    last = dve.bn_stats(bn[:, half, :], x_t[par][:, half * SEQ:(half + 1) * SEQ])
                last.then_inc(bn_done, 1)
                dve.wait_ge(bn_done, t + 1)
                dve.sem_inc(waited, 1)
                dve.bn_aggr(mv[:, :], bn[:, :, :].rearrange("p a b -> p (a b)")).then_inc(stats_done, 1)
                dve.wait_ge(rstd_done, t + 1)
                if not (isinstance(p, int) and p == 0):
                    dve.wait_ge(fill_done, p * 4 + (2 * par - 2))
                    dve.wait_ge(norm_done, p * 2 + (par - 1))
                dve.tensor_scalar(xn[par][:, :], x_t[par][:, :], mv[:, 0:1], rs[:, 3:4],
                                  ALU.subtract, ALU.mult).then_inc(xn_done, 1)

            def split_lo(p, par):
                for half in range(2):
                    dve.wait_ge(hi_done, p * 4 + (2 * par + half + 1))
                    dve.tensor_tensor(xT_lo[par][:, 4 * half:4 * half + 4, :],
                                      t_ps[half][:, :].rearrange("p (k t) -> p k t", k=4),
                                      xT_hi[par][:, 4 * half:4 * half + 4, :].bitcast(F32),
                                      ALU.subtract).then_inc(lo_done, 1)

            def judge(p, par):
                t = p * 2 + par
                dve.wait_ge(norm_done, t + 1)
                dve.wait_ge(worst_done, t + 1)
                if high:
                    dve.sem_inc(waited, 1)
                    dve.tensor_scalar(chosen[par][:, :], norm_sq[par][:, :], THRESHOLD_SQ, None, ALU.is_gt)\
                        .then_inc(worst_done, 1)
                else:
                    dve.tensor_tensor(worst[:, :], worst[:, :], norm_sq[par][:, :], ALU.max)\
                        .then_inc(worst_done, 1)

            def finish(p, par):
                t = p * 2 + par
                dve.wait_ge(xb_done, t + 1)
                for half in range(HALVES):
                    cols = slice(half * SEQ, (half + 1) * SEQ)
                    dve.wait_ge(mm_done, p * 4 + (2 * par + half + 1))
                    add = dve.tensor_tensor(xb[par][:, cols], y_ps[2 * par + half][:, :], xb[par][:, cols],
                                            ALU.add)
                add.then_inc(y_done if high else out_done, 1)
                if high:
                    dve.wait_ge(y_done, t + 1)
                    dve.wait_ge(old_loaded[par], p * 16 + 16)
                    dve.sem_inc(waited, 1)
                    dve.copy_predicated(old[par][:, :], chosen[par][:, 0:1].to_broadcast([P, D]), xb[par][:, :])\
                        .then_inc(out_done, 1)

            def program():
                dve.memset(worst[:, :], 0.0).then_inc(worst_done, 1)
                normalize(0, 0)
                split_lo(0, 0)
                judge(0, 0)

                def body(p):
                    normalize(p, 1)
                    split_lo(p, 1)
                    judge(p, 1)
                    finish(p, 0)
                    normalize(p + 1, 0)
                    split_lo(p + 1, 0)
                    judge(p + 1, 0)
                    finish(p, 1)

                body(0)
                with dve.Fori(1, TILES // 2 - 1) as p:
                    body(p)
                p = TILES // 2 - 1
                normalize(p, 1)
                split_lo(p, 1)
                judge(p, 1)
                finish(p, 0)
                finish(p, 1)
                if not high:
                    dve.wait_ge(worst_all_done, 1)
                    dve.tensor_scalar(flag[:, :], worst_all[0:1, :], THRESHOLD_SQ, None, ALU.is_gt)\
                        .then_inc(y_done, 1)
                    dve.wait_ge(y_done, 1)

            guarded(dve, program)

        @block.tensor
        def _(pe):
            def transposes(p, par):
                t = p * 2 + par
                pe.wait_ge(xn_done, t + 1)
                for half in range(2):
                    if not (isinstance(p, int) and p == 0 and par == 0):
                        pe.wait_ge(lo_done, p * 4 + (2 * par + half - 1))
                    for i in range(4):
                        at = (4 * half + i) * P
                        mm = pe.transpose(t_ps[half][:, i * P:(i + 1) * P], xn[par][:, at:at + P], ident[:, :])
                    mm.then_inc(fill_done, 1)

            def multiply(p, par):
                pe.wait_ge(lo_done, p * 4 + (2 * par + 2))
                if not (isinstance(p, int) and p == 0):
                    pe.wait_ge(y_done if high else out_done, p * 2 + (par - 1))
                for half in range(HALVES):
                    cols = slice(half * SEQ, (half + 1) * SEQ)
                    for kt in range(KT):
                        for part in range(3):
                            a = (xT_hi, xT_lo, xT_hi)[part][par]
                            w = (wl_hi, wl_hi, wl_lo)[part]
                            mm = pe.matmul(y_ps[2 * par + half][:, :], a[:, kt, :], w[:, kt, cols],
                                           start=(kt == 0 and part == 0), stop=(kt == KT - 1 and part == 2))
                    mm.then_inc(mm_done, 1)

            def program():
                pe.wait_ge(consts, 2)
                transposes(0, 0)
                transposes(0, 1)
                multiply(0, 0)
                transposes(1, 0)
                multiply(0, 1)
                with pe.Fori(1, TILES // 2 - 1) as p:
                    transposes(p, 1)
                    multiply(p, 0)
                    transposes(p + 1, 0)
                    multiply(p, 1)
                p = TILES // 2 - 1
                transposes(p, 1)
                multiply(p, 0)
                multiply(p, 1)

            guarded(pe, program)


def wide_weights_phase(nc, outer, qweight, lut8, wl_hi, wl_lo, shifts, flag):
    with ExitStack() as buffers:
        ph = Phase(nc, buffers, outer)
        sb, pb, sem = ph.sb, ph.pb, ph.sem
        ident = sb("w_ident", [P, P])
        words = sb("w_words", [P, 8, 32], I32)
        table = sb("w_table", [P, 256])
        code = sb("w_code", [P, D], I32)
        bit = sb("w_bit", [P, D], I32)
        codef = sb("w_codef", [P, D])
        entry = sb("w_entry", [P, D])
        weights = sb("w_weights", [P, D])
        index = sb("w_index", [P, 1])
        wt_ps = [pb(f"w_t{i}", [P, SEQ]) for i in range(2)]
        ident_done = sem("w_ident_done")
        loaded = sem("w_loaded")
        chain = sem("w_chain")
        entries = sem("w_entries")
        built = sem("w_built")
        fill_done = sem("w_fill_done")
        hi_done = sem("w_hi8_done")
        lo_done = sem("w_lo8_done")
        waited = sem("w_waited")
        CODES = 256
        BITS = 8
        CHAIN = 3 * BITS + 2

        block = buffers.enter_context(nc.Block())

        def guarded(eng, program):
            value = eng.value_load(flag[0:1, 0:1], min_val=0, max_val=1)
            with eng.If(value > 0):
                program()
            with eng.Else():
                eng.nop()

        @block.sync
        def _(sp):
            def program():
                with sp.Fori(0, OTILES) as o:
                    sp.wait_ge(built, o + 1)
                    sp.sem_inc(waited, 1)
                    sp.dma_start(words[:, :, :], qweight[:, bass.ds(o * P, P), :].rearrange("b o w -> o b w"))\
                        .then_inc(loaded, 16)
                    sp.dma_start(table[:, :], lut8[bass.ds(o * P, P), :]).then_inc(loaded, 16)

            guarded(sp, program)

        @block.gpsimd
        def _(pool):
            def program():
                pool.memset(ident[:, :], 0.0).then_inc(ident_done, 1)
                pool.wait_ge(ident_done, 1)
                pool.affine_select(out=ident[:, :], in_=ident[:, :], compare_op=ALU.not_equal, fill=1.0,
                                   base=0, pattern=[[-1, P]], channel_multiplier=1).then_inc(ident_done, 1)

            guarded(pool, program)

        @block.vector
        def _(dve):
            def program():
                dve.sem_inc(built, 1)
                dve.sem_inc(lo_done, 2)
                with dve.Fori(0, OTILES) as o:
                    count = [0]

                    def chained(instruction):
                        count[0] += 1
                        instruction.then_inc(chain, 1)
                        dve.wait_ge(chain, o * CHAIN + count[0])

                    dve.wait_ge(loaded, o * 32 + 32)
                    for b in range(BITS):
                        target = code if b == 0 else bit
                        spread = target[:, :].rearrange("p (w s) -> p w s", s=32)
                        chained(dve.tensor_tensor(spread, words[:, b, :].unsqueeze(2).to_broadcast([P, 32, 32]),
                                                  shifts[:, 2, :].unsqueeze(1).to_broadcast([P, 32, 32]),
                                                  ALU.logical_shift_right))
                        dve.sem_inc(waited, 1)
                        chained(dve.tensor_scalar(target[:, :], target[:, :], 1, b,
                                                  ALU.bitwise_and, ALU.logical_shift_left))
                        if b:
                            chained(dve.tensor_tensor(code[:, :], code[:, :], bit[:, :], ALU.bitwise_or))
                    chained(dve.tensor_copy(codef[:, :], code[:, :]))
                    dve.wait_ge(fill_done, o * 2 + 2)
                    dve.sem_inc(waited, 1)
                    chained(dve.memset(weights[:, :], 0.0))
                    chained(dve.memset(index[:, :], 0.0))
                    dve.sem_inc(waited, 1)
                    assert count[0] == CHAIN
                    with dve.Fori(0, CODES) as j:
                        at = o * (3 * CODES) + j * 3
                        dve.tensor_scalar(entry[:, :], codef[:, :], index[:, 0:1], table[:, bass.ds(j, 1)],
                                          ALU.is_equal, ALU.mult).then_inc(entries, 1)
                        dve.wait_ge(entries, at + 1)
                        dve.tensor_tensor(weights[:, :], weights[:, :], entry[:, :], ALU.add).then_inc(entries, 1)
                        dve.wait_ge(entries, at + 2)
                        dve.sem_inc(waited, 1)
                        dve.tensor_scalar(index[:, :], index[:, :], 1.0, None, ALU.add).then_inc(entries, 1)
                        dve.wait_ge(entries, at + 3)
                        dve.sem_inc(waited, 1)
                    dve.sem_inc(built, 1)
                    for half in range(2):
                        at = wl_hi[:, 4 * half:4 * half + 4, bass.ds(o * P, P)]
                        dve.wait_ge(hi_done, o * 2 + half + 1)
                        dve.tensor_tensor(wl_lo[:, 4 * half:4 * half + 4, bass.ds(o * P, P)],
                                          wt_ps[half][:, :].rearrange("p (k o) -> p k o", k=4),
                                          at.bitcast(F32), ALU.subtract).then_inc(lo_done, 1)

            guarded(dve, program)

        @block.tensor
        def _(pe):
            def program():
                pe.wait_ge(ident_done, 2)
                pe.sem_inc(fill_done, 2)
                with pe.Fori(0, OTILES) as o:
                    pe.wait_ge(built, o + 2)
                    pe.wait_ge(lo_done, o * 2 + 2)
                    for half in range(2):
                        for i in range(4):
                            at = (4 * half + i) * P
                            mm = pe.transpose(wt_ps[half][:, i * P:(i + 1) * P], weights[:, at:at + P],
                                              ident[:, :])
                        mm.then_inc(fill_done, 1)

            guarded(pe, program)

        @block.scalar
        def _(act):
            def program():
                with act.Fori(0, OTILES) as o:
                    for half in range(2):
                        act.wait_ge(fill_done, o * 2 + half + 3)
                        act.activation(wl_hi[:, 4 * half:4 * half + 4, bass.ds(o * P, P)],
                                       wt_ps[half][:, :].rearrange("p (k o) -> p k o", k=4), ACT.Copy)\
                            .then_inc(hi_done, 1)

            guarded(act, program)


def build(nc, x, w_qkv, b_qkv, wo, bo, qweight, lut4, lut8, fbias, out):
    att = nc.dram_tensor("att_scratch", (STEPS, P, SEQ), F32, kind="Internal").ap()
    x1 = nc.dram_tensor("x1_scratch", (TOKENS, D), F32, kind="Internal").ap()
    with ExitStack() as outer:
        attention_phase(nc, outer, x, w_qkv, b_qkv, att)
        keep = Phase(nc, outer, outer)
        wl_hi = keep.sb("wl_hi", [P, KT, D], F32R)
        wl_lo = keep.sb("wl_lo", [P, KT, D], F32R)
        flag = keep.sb("flag", [1, 1], I32)
        shifts = keep.sb("shifts", [P, 3, 32], I32)
        ones = keep.sb("ones", [P, 32], I32)
        tables_done = keep.sem("tables_done")
        with nc.Block() as block:
            @block.gpsimd
            def _(pool):
                pool.iota(shifts[:, 0, :], pattern=[[-1, 32]], base=31, channel_multiplier=0).then_inc(tables_done, 1)
                pool.iota(shifts[:, 2, :], pattern=[[1, 32]], base=0, channel_multiplier=0).then_inc(tables_done, 1)
                pool.iota(ones[:, :], pattern=[[0, 32]], base=1, channel_multiplier=0).then_inc(tables_done, 1)

            @block.vector
            def _(dve):
                dve.wait_ge(tables_done, 3)
                dve.tensor_tensor(shifts[:, 1, :], ones[:, :], shifts[:, 2, :], ALU.logical_shift_left)\
                    .then_inc(tables_done, 1)
                dve.wait_ge(tables_done, 4)
        output_phase(nc, outer, x, wo, bo, att, qweight, lut4, x1, wl_hi, wl_lo, shifts)
        feed_forward_phase(nc, outer, x1, fbias, out, wl_hi, wl_lo, flag, "", high=False)
        wide_weights_phase(nc, outer, qweight, lut8, wl_hi, wl_lo, shifts, flag)
        feed_forward_phase(nc, outer, x1, fbias, out, wl_hi, wl_lo, flag, "_8", high=True, run_if=flag)


def kernel(**inputs):
    import numpy as np
    import concourse.bacc as bacc
    from concourse.bass_utils import run_bass_kernel_spmd

    a = {name.split("_", 1)[1]: np.asarray(value) for name, value in inputs.items()}
    w = np.stack([a["attn_Wq"], a["attn_Wk"], a["attn_Wv"]]).reshape(3, GROUPS, P, KT, P)
    b = np.stack([a["attn_bq"], a["attn_bk"], a["attn_bv"]]).reshape(3, GROUPS, P)
    arrays = {
        "x": a["attn_x"].reshape(TOKENS, D),
        "w_qkv": np.ascontiguousarray(w.transpose(1, 4, 0, 3, 2)).reshape(GROUPS, P, 3, KT * P),
        "b_qkv": np.ascontiguousarray(b.transpose(2, 0, 1)),
        "wo": np.ascontiguousarray(a["attn_Wo"].reshape(D, KT, P).transpose(2, 1, 0)),
        "bo": a["attn_bo"],
        "qweight": a["ffn_qweight"],
        "lut4": a["ffn_lut4"],
        "lut8": a["ffn_lut8"],
        "fbias": a["ffn_bias"],
    }
    nc = bacc.Bacc("TRN2", target_bir_lowering=False, num_devices=1)
    args = {}
    for name, value in arrays.items():
        args[name] = nc.dram_tensor(name, value.shape, mybir.dt.from_np(value.dtype), kind="ExternalInput").ap()
    args["out"] = nc.dram_tensor("out", (TOKENS, D), F32, kind="ExternalOutput").ap()
    build(nc, **args)
    result = run_bass_kernel_spmd(nc, [arrays], core_ids=[0])
    return result.results[0]["out"].reshape(BATCH, SEQ, D)
```

```python
import concourse.bass as bass
from concourse import mybir
from concourse.alu_op_type import AluOpType as ALU
from contextlib import ExitStack

F32 = mybir.dt.float32
F32R = mybir.dt.float32r
BF16 = mybir.dt.bfloat16
I32 = mybir.dt.int32
ACT = mybir.ActivationFunctionType
AXIS = mybir.AxisListType

P = 128
D = 1024
BATCH, SEQ = 4, 512
TOKENS = BATCH * SEQ
HEADS, HD = 32, 32
KT = D // P
GH = P // HD
GROUPS = HEADS // GH
QT = SEQ // P
STEPS = BATCH * GROUPS
SCALE = 1.0 / float(HD) ** 0.5
EPS = 1e-5
MASKED = -3.0e38
THRESHOLD_SQ = 64.0 ** 2
Q, K, V = range(3)

CH = 64
CHUNKS = TOKENS // CH
CHUNKS_AHEAD = SEQ // CH + 1
AHEAD = SEQ // P + 1
FILLS_AHEAD = 2 * (SEQ // P) + 1

P_OFF = [0, 128, 384, 768]
P_COLS = 1280
T_FILLS = [[(0, 0), (0, 1), (0, 2), (0, 3)], [(3, 3), (1, 1), (1, 2), (1, 3)], [(2, 2), (2, 3)]]
T_DEST = [640, 128, 1152]
PT_COLS = 1408
PT_KT = [640, 256, 1152, 0]
PT_QT = [0, 1, 2, 2]
S_COL = [0, 256, 512, 1024]
S_KEYS = [256, 256, 384, 512]


class Phase:

    def __init__(self, nc, buffers, outer):
        self.nc, self.buffers, self.outer = nc, buffers, outer

    def sb(self, name, shape, dt=F32):
        return self.buffers.enter_context(self.nc.sbuf_tensor(name, shape, dt))

    def pb(self, name, shape, dt=F32):
        return self.buffers.enter_context(self.nc.psum_tensor(name, shape, dt))

    def sem(self, name):
        return self.outer.enter_context(self.nc.semaphore(name))


def attention_phase(nc, outer, x, w_qkv, b_qkv, att):
    with ExitStack() as buffers:
        ph = Phase(nc, buffers, outer)
        sb, pb, sem = ph.sb, ph.pb, ph.sem
        ident = sb("ident", [P, P])
        identb = sb("identb", [P, P], BF16)
        maskb = sb("maskb", [P, P], BF16)
        bias = sb("bias", [P, 3, GROUPS])
        xT_hi = [sb(f"xT_hi{i}", [P, KT, SEQ], F32R) for i in range(2)]
        xT_lo = [sb(f"xT_lo{i}", [P, KT, SEQ], F32R) for i in range(2)]
        w_raw = sb("w_raw", [P, 3, KT * P])
        w_hi = sb("w_hi", [P, 3, KT * P], F32R)
        w_lo = sb("w_lo", [P, 3, KT * P], F32R)
        qk_hi = sb("qk_hi", [P, 2, SEQ], F32R)
        qk_lo = sb("qk_lo", [P, 2, SEQ], F32R)
        q_stack = sb("q_stack", [3 * HD, GH, SEQ], F32R)
        k_stack = sb("k_stack", [3 * HD, GH, SEQ], F32R)
        vT = sb("vT", [P, SEQ])
        v_parts = sb("v_parts", [P, QT, GH, 2 * HD], F32R)
        probs = [sb(f"probs{i}", [P, P_COLS]) for i in range(2)]
        pT_hi = [sb(f"pT_hi{i}", [P, PT_COLS], F32R) for i in range(2)]
        pT_lo = [sb(f"pT_lo{i}", [P, PT_COLS], F32R) for i in range(2)]
        row_max = [sb(f"row_max{i}", [P, QT]) for i in range(2)]
        neg_max = [sb(f"neg_max{i}", [P, QT]) for i in range(2)]
        row_sum = [sb(f"row_sum{i}", [P, QT]) for i in range(2)]
        inv_sum = [sb(f"inv_sum{i}", [P, QT]) for i in range(2)]
        o_low = sb("o_low", [HD, SEQ])
        o_out = sb("o_out", [P, SEQ])
        x_in = sb("x_in", [CH, D])
        xn = sb("xn", [CH, D])
        x_first = [sb(f"x_first{i}", [P, D]) for i in range(2)]
        bn = sb("bn", [P, 2, 6])
        mv = sb("mv", [P, 2])
        rs = sb("rs", [P, 4])
        neg_half = sb("neg_half", [P, 1])

        proj_ps = [pb(f"proj_ps{i}", [P, SEQ]) for i in range(2)]
        score_ps = pb("score_ps", [P, 3 * SEQ])
        t_ps = [pb(f"t_ps{i}", [P, SEQ]) for i in range(2)]
        o_ps = pb("o_ps", [2 * HD, SEQ])

        bias_in = sem("bias_in")
        consts = sem("consts")
        zeros_done = sem("zeros_done")
        x_loaded = sem("x_loaded")
        first_loaded = [sem(f"first_loaded{i}") for i in range(2)]
        w_loaded = [sem(f"w_loaded{m}") for m in range(3)]
        w_hi_done = sem("w_hi_done")
        w_lo_done = sem("w_lo_done")
        bn_done = sem("bn_done")
        rstd_done = sem("rstd_done")
        stats_done = sem("stats_done")
        rstd_chain = sem("rstd_chain")
        xn_done = sem("xn_done")
        proj_done = sem("proj_done")
        qk_hi_done = sem("qk_hi_done")
        qk_lo_done = sem("qk_lo_done")
        v_done = sem("v_done")
        stacked = [sem(f"stacked{i}") for i in range(2)]
        scores_done = sem("scores_done")
        max_done = sem("max_done")
        negmax_done = sem("negmax_done")
        exp_done = sem("exp_done")
        inv_done = sem("inv_done")
        norm_done = sem("norm_done")
        fill_done = sem("fill_done")
        hi_done = sem("hi_done")
        lo_done = sem("lo_done")
        pv_done = sem("pv_done")
        low_copied = sem("low_copied")
        head_done = sem("head_done")
        stored = [sem(f"stored{i}") for i in range(GH)]

        def has_chunk(b, g):
            return 8 * b + (g if isinstance(g, int) else 0) + CHUNKS_AHEAD < CHUNKS

        def step_of(b, g):
            return g + GROUPS * b

        def fill(b, g, i):
            with_chunk = CHUNKS - CHUNKS_AHEAD
            base = FILLS_AHEAD - 3 + i
            if GROUPS * b >= with_chunk:
                return g * 13 + (14 * with_chunk + 13 * (GROUPS * b - with_chunk) + base)
            return g * 14 + (14 * GROUPS * b + base)

        def slot_fill(h, f):
            return 3 * h + f + (1 if h >= 2 else 0)

        def next_pos(b, g):
            if isinstance(g, int) and g == GROUPS - 1:
                return b + 1, 0
            return b, g + 1

        def emit(eng, prologue, step, tail):
            prologue()
            step(0, 0)
            for b in range(BATCH):
                with eng.Fori(1 if b == 0 else 0, GROUPS - 1) as g:
                    step(b, g)
                step(b, GROUPS - 1)
            tail()

        def slot_before(b, g, h, k):
            return step_of(b, g) * GH + (h - k)

        def first(b, g, h, k):
            return isinstance(g, int) and step_of(b, g) == 0 and h < k

        def last(b, g):
            return isinstance(g, int) and step_of(b, g) == STEPS - 1

        waited = sem("waited")

        def hold(eng):
            eng.sem_inc(waited, 1)

        block = buffers.enter_context(nc.Block())

        @block.sync
        def _(sp):
            def load_w(m, n, wrapped):
                if not (isinstance(n, int) and n == 0):
                    sp.wait_ge(w_lo_done, (n - 1) * 3 + m + 1)
                    hold(sp)
                sp.dma_start(w_raw[:, m, :], w_qkv[wrapped, :, m, :]).then_inc(w_loaded[m], 16)

            def load_first(t):
                if t >= 2:
                    sp.wait_ge(fill_done, 2 * (t - 1))
                sp.dma_start(x_first[t % 2][:, :], x[t * P:(t + 1) * P, :]).then_inc(first_loaded[t % 2], 16)

            def load_x(k):
                if not (isinstance(k, int) and k == AHEAD - 1):
                    sp.wait_ge(xn_done, k)
                    hold(sp)
                c = (k + (CHUNKS_AHEAD - AHEAD)) % CHUNKS
                sp.dma_start(x_in[:, :], x[bass.ds(c * CH, CH), :]).then_inc(x_loaded, 16)

            def stack(pair, m):
                stack_of, parts = ((q_stack, (qk_hi, qk_lo, qk_hi)), (k_stack, (qk_hi, qk_hi, qk_lo)))[m]
                for h in (2 * pair, 2 * pair + 1):
                    for part, src in enumerate(parts):
                        sp.dma_start(stack_of[part * HD:(part + 1) * HD, h, :].bitcast(F32),
                                     src[h * HD:(h + 1) * HD, m, :].bitcast(F32))\
                            .then_inc(stacked[pair], 16)

            def store(b, g, h):
                if first(b, g, h, 3):
                    return
                head = (h + 1) % GH
                n = step_of(b, g) - (1 if h < 3 else 0)
                sp.wait_ge(head_done, slot_before(b, g, h, 3) + 1)
                hold(sp)
                sp.dma_start(att[n, head * HD:(head + 1) * HD, :],
                             o_out[head * HD:(head + 1) * HD, :]).then_inc(stored[head], 16)

            def prologue():
                for head in range(GH):
                    sp.sem_inc(stored[head], 16)
                sp.dma_start(bias[:, :, :], b_qkv).then_inc(bias_in, 16)
                load_first(0)
                load_first(1)
                load_w(Q, 0, 0)
                load_first(2)
                load_w(K, 0, 0)
                load_first(3)
                load_w(V, 0, 0)
                load_x(AHEAD - 1)
                for m in (Q, K, V):
                    load_w(m, 1, 1)
                load_x(AHEAD)
                load_w(Q, 2, 2)
                sp.wait_ge(qk_lo_done, 2)
                for pair in range(2):
                    for m in (Q, K):
                        stack(pair, m)

            def step(b, g):
                n = step_of(b, g)
                if not last(b, g):
                    load_w(K, n + 2, (g + 2) % GROUPS)
                store(b, g, 0)
                if not last(b, g):
                    load_w(V, n + 2, (g + 2) % GROUPS)
                store(b, g, 1)
                if has_chunk(b, g):
                    load_x(n + AHEAD + 1)
                store(b, g, 2)
                if not last(b, g):
                    sp.wait_ge(qk_lo_done, (n + 1) * 2 + 1)
                    hold(sp)
                    sp.wait_ge(scores_done, n * GH + 2)
                    hold(sp)
                    stack(0, Q)
                    sp.wait_ge(qk_lo_done, (n + 1) * 2 + 2)
                    hold(sp)
                    stack(0, K)
                    load_w(Q, n + 3, (g + 3) % GROUPS)
                store(b, g, 3)
                if not last(b, g):
                    sp.wait_ge(scores_done, n * GH + 4)
                    hold(sp)
                    stack(1, Q)
                    stack(1, K)

            def tail():
                for h in range(3):
                    sp.wait_ge(head_done, STEPS * GH - 2 + h)
                    head = h + 1
                    sp.dma_start(att[STEPS - 1, head * HD:(head + 1) * HD, :],
                                 o_out[head * HD:(head + 1) * HD, :]).then_inc(stored[head], 16)
                for head in range(GH):
                    sp.wait_ge(stored[head], STEPS * 16 + 16)
                sp.wait_ge(w_loaded[Q], (STEPS + 2) * 16)
                sp.wait_ge(w_loaded[K], (STEPS + 1) * 16)
                sp.wait_ge(w_loaded[V], (STEPS + 1) * 16)
                sp.wait_ge(x_loaded, (CHUNKS - CHUNKS_AHEAD + 2) * 16)

            emit(sp, prologue, step, tail)

        @block.gpsimd
        def _(pool):
            def split_w_lo(m, n):
                pool.wait_ge(w_hi_done, n * 3 + m + 1)
                pool.tensor_tensor(w_lo[:, m, :], w_raw[:, m, :], w_hi[:, m, :].bitcast(F32),
                                   ALU.subtract).then_inc(w_lo_done, 1)

            def rstd(c):
                base = c * 5
                pool.wait_ge(stats_done, c + 1)
                hold(pool)
                pool.tensor_scalar(rs[:, 0:1], mv[:, 1:2], EPS, None, ALU.add).then_inc(rstd_chain, 1)
                pool.wait_ge(rstd_chain, base + 1)
                pool.tensor_tensor(rs[:, 1:2], rs[:, 0:1], neg_half[:, :], ALU.pow).then_inc(rstd_chain, 1)
                pool.wait_ge(rstd_chain, base + 2)
                pool.tensor_tensor(rs[:, 2:3], rs[:, 1:2], rs[:, 1:2], ALU.mult).then_inc(rstd_chain, 1)
                pool.wait_ge(rstd_chain, base + 3)
                pool.tensor_tensor(rs[:, 2:3], rs[:, 2:3], rs[:, 0:1], ALU.mult).then_inc(rstd_chain, 1)
                pool.wait_ge(rstd_chain, base + 4)
                hold(pool)
                pool.tensor_scalar(rs[:, 2:3], rs[:, 2:3], -0.5, 1.5, ALU.mult, ALU.add).then_inc(rstd_chain, 1)
                pool.wait_ge(rstd_chain, base + 5)
                pool.tensor_tensor(rs[:, 3:4], rs[:, 1:2], rs[:, 2:3], ALU.mult).then_inc(rstd_done, 1)

            def prologue():
                pool.memset(neg_half[:, :], -0.5)
                pool.memset(ident[:, :], 0.0).then_inc(consts, 1)
                pool.memset(maskb[:, :], 0.0).then_inc(consts, 1)
                pool.wait_ge(consts, 2)
                pool.affine_select(out=ident[:, :], in_=ident[:, :], compare_op=ALU.not_equal, fill=1.0,
                                   base=0, pattern=[[-1, P]], channel_multiplier=1).then_inc(consts, 1)
                pool.affine_select(out=maskb[:, :], in_=maskb[:, :], compare_op=ALU.is_ge, fill=MASKED,
                                   base=0, pattern=[[-1, P]], channel_multiplier=1).then_inc(consts, 1)
                pool.wait_ge(consts, 4)
                pool.tensor_copy(identb[:, :], ident[:, :]).then_inc(consts, 1)
                for c in range(AHEAD):
                    rstd(c)
                for m in (Q, K, V):
                    split_w_lo(m, 0)
                for m in (Q, K):
                    split_w_lo(m, 1)

            def step(b, g):
                n = step_of(b, g)
                if last(b, g):
                    return
                if has_chunk(b, g):
                    rstd(n + AHEAD)
                split_w_lo(V, n + 1)
                split_w_lo(Q, n + 2)
                split_w_lo(K, n + 2)

            emit(pool, prologue, step, lambda: None)

        @block.scalar
        def _(act):
            def split_w_hi(m, n):
                act.wait_ge(w_loaded[m], n * 16 + 16)
                if not (isinstance(n, int) and n == 0):
                    act.wait_ge(proj_done, (n - 1) * 3 + m + 1)
                act.activation(w_hi[:, m, :], w_raw[:, m, :], ACT.Copy).then_inc(w_hi_done, 1)

            def chunk_hi(c_col, half, number, bank):
                act.wait_ge(fill_done, number + 1)
                act.activation(xT_hi[half][:, :, bass.ds(c_col, CH)],
                               t_ps[bank][:, :].rearrange("p (k t) -> p k t", k=KT), ACT.Copy)\
                    .then_inc(hi_done, 1)

            def qk_hi_part(m, n, g):
                act.wait_ge(proj_done, n * 3 + m + 1)
                if not (isinstance(n, int) and n == 0) and m == Q:
                    for pair in range(2):
                        act.wait_ge(stacked[pair], n * 12 * 16)
                act.activation(qk_hi[:, m, :], proj_ps[m][:, :], ACT.Identity, bias=bias[:, m, bass.ds(g, 1)])\
                    .then_inc(qk_hi_done, 1)

            def prologue():
                act.wait_ge(bias_in, 16)
                for t in range(SEQ // P):
                    for half in range(2):
                        act.wait_ge(fill_done, 2 * t + half + 1)
                        act.activation(xT_hi[0][:, 4 * half:4 * half + 4, t * P:(t + 1) * P],
                                       t_ps[half][:, :].rearrange("p (k t) -> p k t", k=4), ACT.Copy)\
                            .then_inc(hi_done, 1)
                    if t >= 1:
                        split_w_hi(t - 1, 0)
                chunk_hi(0, 1, FILLS_AHEAD - 1, 0)
                qk_hi_part(Q, 0, 0)
                split_w_hi(Q, 1)
                qk_hi_part(K, 0, 0)
                split_w_hi(K, 1)

            def step(b, g):
                n = step_of(b, g)
                nb, ng = next_pos(b, g)
                for h in range(GH):
                    s = n * GH + h
                    if not first(b, g, h, 3):
                        act.wait_ge(pv_done, s - 2)
                        act.activation(o_low[:, :], o_ps[HD:2 * HD, :], ACT.Copy).then_inc(low_copied, 1)
                    if h == 0:
                        act.wait_ge(proj_done, n * 3 + V + 1)
                        act.activation(vT[:, :], proj_ps[0][:, :], ACT.Identity, bias=bias[:, V, bass.ds(g, 1)])\
                            .then_inc(v_done, 1)
                    if h == 2:
                        act.wait_ge(fill_done, fill(b, g, 6) + 1)
                        act.activation(v_parts[:, :, :, 0:HD],
                                       t_ps[0][:, :].rearrange("p (k h d) -> p k h d", k=QT, h=GH),
                                       ACT.Copy).then_inc(hi_done, 1)
                    prev = (h + 1) % 2

                    def prob_hi(f):
                        i = slot_fill(h, f)
                        act.wait_ge(fill_done, fill(b, g, i) + 1)
                        w = P * len(T_FILLS[f])
                        act.activation(pT_hi[prev][:, T_DEST[f]:T_DEST[f] + w], t_ps[i % 2][:, 0:w],
                                       ACT.Copy).then_inc(hi_done, 1)

                    if not first(b, g, h, 1):
                        prob_hi(0)
                        prob_hi(1)
                    act.wait_ge(negmax_done, s + 1)
                    for qt in range(QT):
                        w = P * (qt + 1)
                        last_exp = act.activation(
                            probs[h % 2][:, P_OFF[qt]:P_OFF[qt] + w], score_ps[:, S_COL[qt]:S_COL[qt] + w],
                            ACT.Exp, bias=neg_max[h % 2][:, qt:qt + 1], scale=SCALE,
                            accum_out=row_sum[h % 2][:, qt:qt + 1])
                    last_exp.then_inc(exp_done, 1)
                    if not first(b, g, h, 1):
                        prob_hi(2)
                    if last(b, g):
                        continue
                    if h == 0:
                        split_w_hi(V, n + 1)
                    if h == 1:
                        qk_hi_part(Q, n + 1, ng)
                    if h == 2:
                        qk_hi_part(K, n + 1, ng)
                        split_w_hi(Q, n + 2)
                    if h == 3:
                        if has_chunk(b, g):
                            half = (b + 1 + (1 if isinstance(g, int) and g == GROUPS - 1 else 0)) % 2
                            col = 0 if isinstance(g, int) and g == GROUPS - 1 else (g + 1) * CH
                            chunk_hi(col, half, fill(b, g, 13), 1)
                        split_w_hi(K, n + 2)

            def tail():
                s = STEPS * GH
                act.wait_ge(pv_done, s - 2)
                act.activation(o_low[:, :], o_ps[HD:2 * HD, :], ACT.Copy).then_inc(low_copied, 1)
                for f in range(3):
                    act.wait_ge(fill_done, fill(BATCH - 1, GROUPS, f) + 1)
                    w = P * len(T_FILLS[f])
                    act.activation(pT_hi[1][:, T_DEST[f]:T_DEST[f] + w], t_ps[f % 2][:, 0:w],
                                   ACT.Copy).then_inc(hi_done, 1)
                for k in (1, 0):
                    act.wait_ge(pv_done, s - k)
                    act.activation(o_low[:, :], o_ps[HD:2 * HD, :], ACT.Copy).then_inc(low_copied, 1)

            emit(act, prologue, step, tail)

        @block.vector
        def _(dve):
            def stats(k, src, rows):
                for half in range(2):
                    last_bn = dve.bn_stats(bn[0:rows, half, :], src[:, half * 512:(half + 1) * 512])
                last_bn.then_inc(bn_done, 1)
                dve.wait_ge(bn_done, k + 1)
                hold(dve)
                dve.bn_aggr(mv[0:rows, :], bn[0:rows, :, :].rearrange("p a b -> p (a b)")).then_inc(stats_done, 1)

            def normalize(k, dst, src, rows):
                dve.wait_ge(rstd_done, k + 1)
                dve.tensor_scalar(dst, src, mv[0:rows, 0:1], rs[0:rows, 3:4], ALU.subtract, ALU.mult)\
                    .then_inc(xn_done, 1)

            def chunk_stats(k):
                dve.wait_ge(x_loaded, k * 16 + (16 - 16 * (AHEAD - 1)))
                stats(k, x_in[:, :], CH)

            def chunk_normalize(k, number):
                if number is not None:
                    dve.wait_ge(fill_done, number)
                normalize(k, xn[:, :], x_in[:, :], CH)

            def lo_part(dst, src, hi, number):
                dve.wait_ge(hi_done, number + 1)
                dve.tensor_tensor(dst, src, hi, ALU.subtract).then_inc(lo_done, 1)

            def chunk_lo(c_col, half, number, bank):
                cols = bass.ds(c_col, CH)
                lo_part(xT_lo[half][:, :, cols], t_ps[bank][:, :].rearrange("p (k t) -> p k t", k=KT),
                        xT_hi[half][:, :, cols].bitcast(F32), number)

            def qk_lo_part(m, n, g):
                dve.wait_ge(qk_hi_done, n * 2 + m + 1)
                dve.scalar_tensor_tensor(qk_lo[:, m, :], proj_ps[m][:, :], bias[:, m, bass.ds(g, 1)],
                                         qk_hi[:, m, :].bitcast(F32), ALU.add, ALU.subtract)\
                    .then_inc(qk_lo_done, 1)

            def combine(h, s, quadrant_use):
                head = (h + 1) % GH
                dve.wait_ge(low_copied, s - 2)
                if quadrant_use is not None:
                    dve.wait_ge(stored[head], quadrant_use * 16 + 16)
                dve.tensor_tensor(o_out[head * HD:(head + 1) * HD, :], o_ps[0:HD, :], o_low[:, :],
                                  ALU.add).then_inc(head_done, 1)

            def prologue():
                for i in range(2):
                    dve.memset(pT_hi[i][:, 0:P].bitcast(F32), 0.0)
                    dve.memset(pT_lo[i][:, 0:P].bitcast(F32), 0.0).then_inc(zeros_done, 1)
                dve.wait_ge(bias_in, 16)

                def first_lo(t):
                    for half in range(2):
                        cols = (slice(None), slice(4 * half, 4 * half + 4), slice(t * P, (t + 1) * P))
                        lo_part(xT_lo[0][cols], t_ps[half][:, :].rearrange("p (k t) -> p k t", k=4),
                                xT_hi[0][cols].bitcast(F32), 2 * t + half)

                for t in range(SEQ // P):
                    tile = x_first[t % 2][:, :]
                    dve.wait_ge(first_loaded[t % 2], 16 * (t // 2 + 1))
                    stats(t, tile, P)
                    if t:
                        first_lo(t - 1)
                    normalize(t, tile, tile, P)
                chunk_stats(AHEAD - 1)
                first_lo(SEQ // P - 1)
                chunk_normalize(AHEAD - 1, None)
                chunk_lo(0, 1, FILLS_AHEAD - 1, 0)
                qk_lo_part(Q, 0, 0)
                qk_lo_part(K, 0, 0)

            def step(b, g):
                n = step_of(b, g)
                nb, ng = next_pos(b, g)
                for h in range(GH):
                    s = n * GH + h
                    par, prev = h % 2, (h + 1) % 2
                    if not first(b, g, h, 3):
                        uses = (n - 1) if h < 3 else n
                        combine(h, s, uses)
                    if h == 2:
                        lo_part(v_parts[:, :, :, HD:2 * HD],
                                t_ps[0][:, :].rearrange("p (k h d) -> p k h d", k=QT, h=GH),
                                v_parts[:, :, :, 0:HD].bitcast(F32), fill(b, g, 6))
                    dve.wait_ge(scores_done, s + 1)
                    for qt in range(QT):
                        last_max = dve.tensor_reduce(row_max[par][:, qt:qt + 1],
                                                     score_ps[:, S_COL[qt]:S_COL[qt] + P * (qt + 1)],
                                                     AXIS.X, ALU.max)
                    last_max.then_inc(max_done, 1)
                    dve.wait_ge(max_done, s + 1)
                    dve.tensor_scalar(neg_max[par][:, :], row_max[par][:, :], -SCALE, None, ALU.mult)\
                        .then_inc(negmax_done, 1)

                    def prob_lo(f):
                        i = slot_fill(h, f)
                        w = P * len(T_FILLS[f])
                        cols = slice(T_DEST[f], T_DEST[f] + w)
                        lo_part(pT_lo[prev][:, cols], t_ps[i % 2][:, 0:w], pT_hi[prev][:, cols].bitcast(F32),
                                fill(b, g, i))

                    if not first(b, g, h, 1):
                        prob_lo(0)
                        prob_lo(1)
                    dve.wait_ge(exp_done, s + 1)
                    dve.reciprocal(inv_sum[par][:, :], row_sum[par][:, :]).then_inc(inv_done, 1)
                    dve.wait_ge(inv_done, s + 1)
                    for qt in range(QT):
                        cols = slice(P_OFF[qt], P_OFF[qt] + P * (qt + 1))
                        last_norm = dve.tensor_scalar(probs[par][:, cols], probs[par][:, cols],
                                                      inv_sum[par][:, qt:qt + 1], None, ALU.mult)
                    last_norm.then_inc(norm_done, 1)
                    if not first(b, g, h, 1):
                        prob_lo(2)
                    if last(b, g):
                        continue
                    if h == 0 and has_chunk(b, g):
                        chunk_stats(n + AHEAD)
                    if h == 1:
                        qk_lo_part(Q, n + 1, ng)
                        if has_chunk(b, g):
                            chunk_normalize(n + AHEAD, fill(b, g, 0))
                    if h == 2:
                        qk_lo_part(K, n + 1, ng)
                    if h == 3 and has_chunk(b, g):
                        half = (b + 1 + (1 if isinstance(g, int) and g == GROUPS - 1 else 0)) % 2
                        col = 0 if isinstance(g, int) and g == GROUPS - 1 else (g + 1) * CH
                        chunk_lo(col, half, fill(b, g, 13), 1)

            def tail():
                s = STEPS * GH
                combine(0, s, STEPS - 1)
                for f in range(3):
                    w = P * len(T_FILLS[f])
                    cols = slice(T_DEST[f], T_DEST[f] + w)
                    lo_part(pT_lo[1][:, cols], t_ps[f % 2][:, 0:w], pT_hi[1][:, cols].bitcast(F32),
                            fill(BATCH - 1, GROUPS, f))
                combine(1, s + 1, STEPS - 1)
                combine(2, s + 2, STEPS - 1)

            emit(dve, prologue, step, tail)

        @block.tensor
        def _(pe):
            def chunk_transposes(k, number, bank):
                pe.wait_ge(xn_done, k + 1)
                bank_free(number)
                hold(pe)
                for kt in range(KT):
                    last = pe.transpose(t_ps[bank][:, kt * CH:(kt + 1) * CH],
                                        xn[:, kt * P:(kt + 1) * P], ident[0:CH, 0:CH])
                last.then_inc(fill_done, 1)

            def bank_free(number, whole=False):
                if isinstance(number, int) and number < 2:
                    return
                pe.wait_ge(lo_done, number if whole else number - 1)

            def project(m, n, half, lo, hi):
                bank = proj_ps[m % 2]
                if lo == 0:
                    pe.wait_ge(w_lo_done, n * 3 + m + 1)
                    if not (isinstance(n, int) and n == 0):
                        if m == Q:
                            pe.wait_ge(v_done, n)
                        elif m == K:
                            pe.wait_ge(qk_lo_done, n * 2)
                    if m == V:
                        pe.wait_ge(qk_lo_done, n * 2 + 1)
                for i in range(lo, hi):
                    kt, part = i // 3, i % 3
                    w = (w_hi, w_hi, w_lo)[part]
                    xt = (xT_hi, xT_lo, xT_hi)[part][half]
                    mm = pe.matmul(bank[:, :], w[:, m, kt * P:(kt + 1) * P], xt[:, kt, :],
                                   start=(i == 0), stop=(i == 23))
                if hi == 24:
                    mm.then_inc(proj_done, 1)

            def scores(b, g, h):
                n = step_of(b, g)
                if h % 2 == 0:
                    pe.wait_ge(stacked[h // 2], n * 12 * 16 + 12 * 16)
                if not first(b, g, h, 1):
                    pe.wait_ge(exp_done, n * GH + h)
                for qt in range(QT):
                    pe.matmul(score_ps[:, S_COL[qt]:S_COL[qt] + S_KEYS[qt]],
                              q_stack[:, h, qt * P:(qt + 1) * P], k_stack[:, h, 0:S_KEYS[qt]],
                              start=True, stop=False)
                    diagonal = S_COL[qt] + qt * P
                    mm = pe.matmul(score_ps[:, diagonal:diagonal + P], identb[:, :], maskb[:, :],
                                   start=False, stop=True)
                mm.then_inc(scores_done, 1)

            def prob_transposes(b, g, h, f, parity):
                i = slot_fill(h, f)
                number = fill(b, g, i)
                bank_free(number, whole=(i == 0))
                for col, (kt, qt) in enumerate(T_FILLS[f]):
                    at = P_OFF[qt] + kt * P
                    mm = pe.transpose(t_ps[i % 2][:, col * P:(col + 1) * P],
                                      probs[parity][:, at:at + P], ident[:, :])
                mm.then_inc(fill_done, 1)

            def attend(h, parity, s, lo_needed):
                pe.wait_ge(lo_done, lo_needed)
                pe.wait_ge(head_done, s - 2) if s is not None else None
                first_mm = True
                for pT in (pT_hi[parity], pT_lo[parity]):
                    for kt in range(QT):
                        at = PT_KT[kt]
                        q0 = PT_QT[kt] * P
                        mm = pe.matmul(o_ps[:, q0:SEQ], v_parts[:, kt, h, :], pT[:, at:at + SEQ - q0],
                                       start=first_mm, stop=(pT is pT_lo[parity] and kt == QT - 1))
                        first_mm = False
                mm.then_inc(pv_done, 1)

            def prologue():
                pe.wait_ge(consts, 5)
                for t in range(SEQ // P):
                    pe.wait_ge(xn_done, t + 1)
                    for half in range(2):
                        bank_free(2 * t + half)
                        for i in range(4):
                            at = (4 * half + i) * P
                            mm = pe.transpose(t_ps[half][:, i * P:(i + 1) * P], x_first[t % 2][:, at:at + P],
                                              ident[:, :])
                        mm.then_inc(fill_done, 1)
                chunk_transposes(AHEAD - 1, FILLS_AHEAD - 1, 0)
                pe.wait_ge(lo_done, FILLS_AHEAD - 1)
                for m in (Q, K, V):
                    project(m, 0, 0, 0, 24)
                pe.wait_ge(zeros_done, 2)

            def step(b, g):
                n = step_of(b, g)
                nb, ng = next_pos(b, g)
                todo = [] if last(b, g) else [(m, i) for m in (Q, K, V) for i in range(24)]

                def projections(count):
                    while count and todo:
                        m, lo = todo[0]
                        run = min(count, 24 - lo)
                        project(m, n + 1, nb % 2, lo, lo + run)
                        del todo[:run]
                        count -= run

                for h in range(GH):
                    prev = (h + 1) % 2
                    scores(b, g, h)
                    if not first(b, g, h, 1):
                        pe.wait_ge(norm_done, n * GH + h)
                        prob_transposes(b, g, h, 0, prev)
                        prob_transposes(b, g, h, 1, prev)
                    if isinstance(g, int) and g == GROUPS - 1 and h == 0 and b + 1 < BATCH:
                        pe.wait_ge(lo_done, fill(b, g, 0))
                    projections(12)
                    if not first(b, g, h, 1):
                        prob_transposes(b, g, h, 2, prev)
                    projections(6)
                    if not first(b, g, h, 2):
                        needed = fill(b, g, 0) if h == 0 else fill(b, g, slot_fill(h - 1, 2)) + 1
                        attend((h + 2) % GH, h % 2, n * GH + h, needed)
                    if h == 1:
                        pe.wait_ge(v_done, n + 1)
                        bank_free(fill(b, g, 6))
                        for kt in range(QT):
                            mm = pe.transpose(t_ps[0][:, kt * P:(kt + 1) * P], vT[:, kt * P:(kt + 1) * P],
                                              ident[:, :])
                        mm.then_inc(fill_done, 1)
                    if h == 3 and has_chunk(b, g):
                        chunk_transposes(n + AHEAD, fill(b, g, 13), 1)

            def tail():
                n = STEPS
                pe.wait_ge(norm_done, n * GH)
                for f in range(3):
                    number = fill(BATCH - 1, GROUPS, f)
                    bank_free(number, whole=(f == 0))
                    for col, (kt, qt) in enumerate(T_FILLS[f]):
                        at = P_OFF[qt] + kt * P
                        mm = pe.transpose(t_ps[f % 2][:, col * P:(col + 1) * P],
                                          probs[1][:, at:at + P], ident[:, :])
                    mm.then_inc(fill_done, 1)
                attend(2, 0, n * GH, fill(BATCH - 1, GROUPS, 0))
                attend(3, 1, n * GH + 1, fill(BATCH - 1, GROUPS, 2) + 1)

            emit(pe, prologue, step, tail)


TILES = TOKENS // P
HALVES = D // SEQ
OTILES = D // P
DQ_OPS = 22


def output_phase(nc, outer, x, wo, bo, att, qweight, lut4, x1, wl_hi, wl_lo, shifts):
    with ExitStack() as buffers:
        ph = Phase(nc, buffers, outer)
        sb, pb, sem = ph.sb, ph.pb, ph.sem
        ident = sb("ident2", [P, P])
        wo_hi = sb("wo_hi", [P, KT, D], F32R)
        wo_lo = sb("wo_lo", [P, KT, D], F32R)
        bo_all = sb("bo_all", [P, D])
        att_raw = [sb(f"att_raw{i}", [P, KT, P]) for i in range(2)]
        att_hi = [sb(f"att_hi{i}", [P, KT, P], F32R) for i in range(2)]
        att_lo = [sb(f"att_lo{i}", [P, KT, P], F32R) for i in range(2)]
        x_t = [sb(f"x_t{i}", [P, D]) for i in range(2)]
        words = sb("words", [P, 4, 32], I32)
        lut_in = sb("lut_in", [P, 16])
        lut = sb("lut", [P, 16])
        lut_xor = sb("lut_xor", [P, 8], I32)
        bits = [sb(f"bits{i}", [P, D], I32) for i in range(4)]
        r = [sb(f"r{i}", [P, D], I32) for i in range(4)]
        out_ps = [pb(f"out_ps{i}", [P, SEQ]) for i in range(4)]
        wt_ps = [pb(f"wt_ps{i}", [P, SEQ]) for i in range(2)]

        ident_done = sem("ident2_done")
        bo_loaded = sem("bo_loaded")
        wo_loaded = [sem(f"wo_loaded{i}") for i in range(2)]
        wo_hi_done = sem("wo_hi_done")
        wo_lo_done = sem("wo_lo_done")
        att_loaded = [sem(f"att_loaded{i}") for i in range(2)]
        att_hi_done = sem("att_hi_done")
        att_lo_done = sem("att_lo_done")
        xt_loaded = [sem(f"xt_loaded{i}") for i in range(2)]
        xb_done = sem("xb_done")
        mm_done = sem("mm_done")
        x1_done = sem("x1_done")
        x1_stored = [sem(f"x1_stored{i}") for i in range(2)]
        words_loaded = sem("words_loaded")
        dq_done = sem("dq_done")
        wt_done = sem("wt_done")
        wt_hi_done = sem("wt_hi_done")
        wt_lo_done = sem("wt_lo_done")
        waited = sem("waited2")

        def emit(body, tail):
            return body, tail

        block = buffers.enter_context(nc.Block())

        @block.sync
        def _(sp):
            def load_words(p):
                if not (isinstance(p, int) and p == 0):
                    sp.wait_ge(dq_done, (p - 1) * DQ_OPS + 7)
                    sp.sem_inc(waited, 1)
                sp.dma_start(words[:, :, :], qweight[0:4, bass.ds(p * P, P), :].rearrange("b o w -> o b w"))\
                    .then_inc(words_loaded, 16)
                sp.dma_start(lut_in[:, :], lut4[bass.ds(p * P, P), :]).then_inc(words_loaded, 16)

            def load_att(p, par):
                if not (isinstance(p, int) and p == 0):
                    sp.wait_ge(att_lo_done, p * 2 + (par - 1))
                    sp.sem_inc(waited, 1)
                first_row = (p // 2) * GROUPS
                col = (p % 2) * (2 * P) + par * P
                sp.dma_start(att_raw[par][:, :, :],
                             att[bass.ds(first_row, GROUPS), :, bass.ds(col, P)].rearrange("g p t -> p g t"))\
                    .then_inc(att_loaded[par], 16)

            def store_x1(p, par):
                sp.wait_ge(x1_done, p * 2 + (par + 1))
                sp.sem_inc(waited, 1)
                sp.dma_start(x1[bass.ds(p * (2 * P) + par * P, P), :], x_t[par][:, :]).then_inc(x1_stored[par], 16)

            def load_x(p, par):
                if not (isinstance(p, int) and p == 0):
                    sp.wait_ge(x1_stored[par], p * 16)
                    sp.sem_inc(waited, 1)
                sp.dma_start(x_t[par][:, :], x[bass.ds(p * (2 * P) + par * P, P), :]).then_inc(xt_loaded[par], 16)

            load_words(0)
            for kt in range(KT):
                if kt >= 2:
                    sp.wait_ge(wo_lo_done, kt - 1)
                sp.dma_start(r[kt % 2][:, :].bitcast(F32), wo[:, kt, :]).then_inc(wo_loaded[kt % 2], 16)
                if kt == 1:
                    sp.dma_start(bo_all[:, :], bo.partition_broadcast(P)).then_inc(bo_loaded, 16)
                    for par in range(2):
                        load_att(0, par)
                        load_x(0, par)
            with sp.Fori(1, OTILES) as p:
                load_att(p, 0)
                store_x1(p - 1, 0)
                load_x(p, 0)
                load_words(p)
                load_att(p, 1)
                store_x1(p - 1, 1)
                load_x(p, 1)
            for par in range(2):
                store_x1(OTILES - 1, par)
            for par in range(2):
                sp.wait_ge(x1_stored[par], TILES // 2 * 16)

        @block.gpsimd
        def _(pool):
            def add_bias(p, par):
                pool.wait_ge(xt_loaded[par], p * 16 + 16)
                pool.tensor_tensor(x_t[par][:, :], x_t[par][:, :], bo_all[:, :], ALU.add).then_inc(xb_done, 1)

            def split_lo(t, p, par):
                pool.wait_ge(att_hi_done, t + 1)
                pool.tensor_tensor(att_lo[par][:, :, :], att_raw[par][:, :, :],
                                   att_hi[par][:, :, :].bitcast(F32), ALU.subtract).then_inc(att_lo_done, 1)

            pool.memset(ident[:, :], 0.0).then_inc(ident_done, 1)
            pool.wait_ge(ident_done, 1)
            pool.affine_select(out=ident[:, :], in_=ident[:, :], compare_op=ALU.not_equal, fill=1.0,
                               base=0, pattern=[[-1, P]], channel_multiplier=1).then_inc(ident_done, 1)
            pool.wait_ge(bo_loaded, 16)

            def body(p):
                for par in range(2):
                    split_lo(p * 2 + par, p, par)
                    add_bias(p, par)

            with pool.Fori(0, OTILES) as p:
                body(p)

        @block.scalar
        def _(act):
            def split_hi(p, par):
                act.wait_ge(att_loaded[par], p * 16 + 16)
                if not (isinstance(p, int) and p == 0):
                    act.wait_ge(mm_done, p * 4 + (2 * par - 2))
                act.activation(att_hi[par][:, :, :], att_raw[par][:, :, :], ACT.Copy).then_inc(att_hi_done, 1)

            def weights_hi(p):
                for half in range(2):
                    act.wait_ge(wt_done, p * 2 + half + 1)
                    act.activation(wl_hi[:, 4 * half:4 * half + 4, bass.ds(p * P, P)],
                                   wt_ps[half][:, :].rearrange("p (k o) -> p k o", k=4), ACT.Copy)\
                        .then_inc(wt_hi_done, 1)

            for kt in range(KT):
                act.wait_ge(wo_loaded[kt % 2], 16 * (kt // 2 + 1))
                act.activation(wo_hi[:, kt, :], r[kt % 2][:, :].bitcast(F32), ACT.Copy).then_inc(wo_hi_done, 1)
                if kt == 1:
                    split_hi(0, 0)
                    split_hi(0, 1)
            with act.Fori(1, OTILES) as p:
                split_hi(p, 0)
                split_hi(p, 1)
                weights_hi(p - 1)
            weights_hi(OTILES - 1)

        @block.vector
        def _(dve):
            def dequantize(p):
                count = [0]

                def chained(instruction):
                    count[0] += 1
                    instruction.then_inc(dq_done, 1)
                    dve.wait_ge(dq_done, p * DQ_OPS + count[0])

                def by_bit(n):
                    return r[n][:, :]

                def leaf(n, j):
                    chained(dve.tensor_scalar(r[n][:, :], bits[0][:, :], lut_xor[:, j:j + 1],
                                              lut[:, 2 * j:2 * j + 1].bitcast(I32),
                                              ALU.bitwise_and, ALU.bitwise_xor))

                def select(n, plane, m):
                    dve.sem_inc(waited, 1)
                    chained(dve.copy_predicated(by_bit(n), bits[plane][:, :], by_bit(m)))

                def word(plane):
                    return words[:, plane, :].unsqueeze(2).to_broadcast([P, 32, 32])

                def pattern(row):
                    return shifts[:, row, :].unsqueeze(1).to_broadcast([P, 32, 32])

                def spread(plane):
                    return bits[plane][:, :].rearrange("p (w s) -> p w s", s=32)

                dve.wait_ge(words_loaded, p * 32 + 32)
                chained(dve.tensor_copy(lut[:, :], lut_in[:, :]))
                yield
                pairs = lut[:, :].bitcast(I32).rearrange("p (j b) -> p j b", b=2)
                chained(dve.tensor_tensor(lut_xor[:, :], pairs[:, :, 0], pairs[:, :, 1], ALU.bitwise_xor))
                yield
                chained(dve.tensor_tensor(spread(0), word(0), pattern(0), ALU.logical_shift_left))
                yield
                for plane in (1, 2, 3):
                    chained(dve.tensor_tensor(spread(plane), word(plane), pattern(1), ALU.bitwise_and))
                    yield
                chained(dve.tensor_scalar(bits[0][:, :], bits[0][:, :], 31, None, ALU.arith_shift_right))
                yield
                if not (isinstance(p, int) and p == 0):
                    dve.wait_ge(wt_done, p * 2)
                leaf(0, 0)
                yield
                leaf(1, 1)
                yield
                select(0, 1, 1)
                yield
                leaf(1, 2)
                yield
                leaf(2, 3)
                yield
                select(1, 1, 2)
                yield
                select(0, 2, 1)
                yield
                leaf(1, 4)
                yield
                leaf(2, 5)
                yield
                select(1, 1, 2)
                yield
                leaf(2, 6)
                yield
                leaf(3, 7)
                yield
                select(2, 1, 3)
                yield
                select(1, 2, 2)
                yield
                select(0, 3, 1)
                assert count[0] == DQ_OPS
                yield

            def finish_x1(p, par):
                dve.wait_ge(xb_done, p * 2 + (par + 1))
                for half in range(HALVES):
                    cols = slice(half * SEQ, (half + 1) * SEQ)
                    dve.wait_ge(mm_done, p * 4 + (2 * par + half + 1))
                    add = dve.tensor_tensor(x_t[par][:, cols], out_ps[2 * par + half][:, :], x_t[par][:, cols],
                                            ALU.add)
                add.then_inc(x1_done, 1)

            def weights_lo(p):
                for half in range(2):
                    at = wl_hi[:, 4 * half:4 * half + 4, bass.ds(p * P, P)]
                    dve.wait_ge(wt_hi_done, p * 2 + half + 1)
                    dve.tensor_tensor(wl_lo[:, 4 * half:4 * half + 4, bass.ds(p * P, P)],
                                      wt_ps[half][:, :].rearrange("p (k o) -> p k o", k=4), at.bitcast(F32),
                                      ALU.subtract).then_inc(wt_lo_done, 1)

            for kt in range(KT):
                dve.wait_ge(wo_hi_done, kt + 1)
                dve.tensor_tensor(wo_lo[:, kt, :], r[kt % 2][:, :].bitcast(F32), wo_hi[:, kt, :].bitcast(F32),
                                  ALU.subtract).then_inc(wo_lo_done, 1)

            def body(p):
                ops = dequantize(p)
                for _ in range(7):
                    next(ops)
                if not (isinstance(p, int) and p == 0):
                    weights_lo(p - 1)
                for _ in range(5):
                    next(ops)
                finish_x1(p, 0)
                for _ in ops:
                    pass
                finish_x1(p, 1)

            dve.wait_ge(wo_lo_done, KT)
            dve.sem_inc(wt_lo_done, 2)
            body(0)
            with dve.Fori(1, OTILES) as p:
                body(p)
            weights_lo(OTILES - 1)

        @block.tensor
        def _(pe):
            def multiply(p, par, half):
                if half == 0:
                    pe.wait_ge(att_lo_done, p * 2 + (par + 1))
                if not (isinstance(p, int) and p == 0):
                    pe.wait_ge(x1_done, p * 2 + (par - 1))
                cols = slice(half * SEQ, (half + 1) * SEQ)
                for kt in range(KT):
                    for part in range(3):
                        if isinstance(p, int) and p == 0 and par == 0 and half == 0 and part == 0:
                            pe.wait_ge(wo_lo_done, kt + 1)
                        a = (att_hi, att_lo, att_hi)[part][par]
                        w = (wo_hi, wo_hi, wo_lo)[part]
                        mm = pe.matmul(out_ps[2 * par + half][:, :], a[:, kt, :], w[:, kt, cols],
                                       start=(kt == 0 and part == 0), stop=(kt == KT - 1 and part == 2))
                mm.then_inc(mm_done, 1)

            def transpose_weights(p):
                pe.wait_ge(dq_done, (p + 1) * DQ_OPS)
                pe.wait_ge(wt_lo_done, p * 2 + 2)
                for half in range(2):
                    for i in range(4):
                        at = (4 * half + i) * P
                        mm = pe.transpose(wt_ps[half][:, i * P:(i + 1) * P], r[0][:, at:at + P].bitcast(F32),
                                          ident[:, :])
                    mm.then_inc(wt_done, 1)

            pe.wait_ge(ident_done, 2)

            def body(p):
                multiply(p, 0, 0)
                if not (isinstance(p, int) and p == 0):
                    transpose_weights(p - 1)
                multiply(p, 0, 1)
                multiply(p, 1, 0)
                multiply(p, 1, 1)

            body(0)
            with pe.Fori(1, OTILES) as p:
                body(p)
            transpose_weights(OTILES - 1)


def feed_forward_phase(nc, outer, x1, fbias, out, wl_hi, wl_lo, flag, tag, high, run_if=None):
    with ExitStack() as buffers:
        ph = Phase(nc, buffers, outer)

        def sb(name, shape, dt=F32):
            return ph.sb(name + tag, shape, dt)

        def pb(name, shape, dt=F32):
            return ph.pb(name + tag, shape, dt)

        def sem(name):
            return ph.sem(name + tag)

        ident = sb("f_ident", [P, P])
        neg_half = sb("f_neg_half", [P, 1])
        bias_all = sb("f_bias_all", [P, D])
        x_t = [sb(f"f_x{i}", [P, D]) for i in range(2)]
        xb = [sb(f"f_xb{i}", [P, D]) for i in range(2)]
        xn = [sb(f"f_xn{i}", [P, D]) for i in range(2)]
        squares = sb("f_squares", [P, D])
        bn = sb("f_bn", [P, 2, 6])
        mv = sb("f_mv", [P, 2])
        rs = sb("f_rs", [P, 4])
        xT_hi = [sb(f"f_xT_hi{i}", [P, KT, P], F32R) for i in range(2)]
        xT_lo = [sb(f"f_xT_lo{i}", [P, KT, P], F32R) for i in range(2)]
        norm_sq = [sb(f"f_norm_sq{i}", [P, 1]) for i in range(2)]
        worst = sb("f_worst", [P, 1])
        worst_all = sb("f_worst_all", [P, 1])
        chosen = [sb(f"f_chosen{i}", [P, 1], I32) for i in range(2)]
        old = [sb(f"f_old{i}", [P, D]) for i in range(2)] if high else None
        t_ps = [pb(f"f_t{i}", [P, SEQ]) for i in range(2)]
        y_ps = [pb(f"f_y{i}", [P, SEQ]) for i in range(4)]

        consts = sem("f_consts")
        bias_loaded = sem("f_bias_loaded")
        x_loaded = [sem(f"f_x_loaded{i}") for i in range(2)]
        old_loaded = [sem(f"f_old_loaded{i}") for i in range(2)]
        bn_done = sem("f_bn_done")
        stats_done = sem("f_stats_done")
        rstd_chain = sem("f_rstd_chain")
        rstd_done = sem("f_rstd_done")
        xn_done = sem("f_xn_done")
        norm_done = sem("f_norm_done")
        worst_done = sem("f_worst_done")
        xb_done = sem("f_xb_done")
        fill_done = sem("f_fill_done")
        hi_done = sem("f_hi_done")
        lo_done = sem("f_lo_done")
        mm_done = sem("f_mm_done")
        y_done = sem("f_y_done")
        out_done = sem("f_out_done")
        stored = [sem(f"f_stored{i}") for i in range(2)]
        worst_all_done = sem("f_worst_all_done")
        waited = sem("f_waited")

        block = buffers.enter_context(nc.Block())

        def guarded(eng, program):
            if run_if is None:
                program()
                return
            value = eng.value_load(run_if[0:1, 0:1], min_val=0, max_val=1)
            with eng.If(value > 0):
                program()
            with eng.Else():
                eng.nop()

        def tile(p, c):
            return p * 2 + c, c % 2, p + c // 2

        def early(t):
            return isinstance(t, int) and t < 2

        def hold(eng):
            eng.sem_inc(waited, 1)

        @block.sync
        def _(sp):
            def load(p, c):
                t, par, uses = tile(p, c)
                if not early(t):
                    sp.wait_ge(xn_done, t - 1)
                    hold(sp)
                    sp.wait_ge(xb_done, t - 1)
                    hold(sp)
                sp.dma_start(x_t[par][:, :], x1[bass.ds(t * P, P), :]).then_inc(x_loaded[par], 16)
                if high:
                    if not early(t):
                        sp.wait_ge(stored[par], uses * 16)
                        hold(sp)
                    sp.dma_start(old[par][:, :], out[bass.ds(t * P, P), :]).then_inc(old_loaded[par], 16)

            def store(p, c):
                t, par, _ = tile(p, c)
                sp.wait_ge(out_done, t + 1)
                hold(sp)
                src = old[par] if high else xb[par]
                sp.dma_start(out[bass.ds(t * P, P), :], src[:, :]).then_inc(stored[par], 16)

            def program():
                load(0, 0)
                sp.dma_start(bias_all[:, :], fbias.partition_broadcast(P)).then_inc(bias_loaded, 16)
                load(0, 1)
                with sp.Fori(1, TILES // 2) as p:
                    for c in range(2):
                        if high:
                            store(p, c - 2)
                            load(p, c)
                        else:
                            load(p, c)
                            store(p, c - 2)
                for c in range(2):
                    store(TILES // 2 - 1, c)
                for par in range(2):
                    sp.wait_ge(stored[par], TILES // 2 * 16)

            guarded(sp, program)

        @block.gpsimd
        def _(pool):
            def rstd(p, c):
                t, _, _ = tile(p, c)
                base = t * 5
                pool.wait_ge(stats_done, t + 1)
                hold(pool)
                pool.tensor_scalar(rs[:, 0:1], mv[:, 1:2], EPS, None, ALU.add).then_inc(rstd_chain, 1)
                pool.wait_ge(rstd_chain, base + 1)
                pool.tensor_tensor(rs[:, 1:2], rs[:, 0:1], neg_half[:, :], ALU.pow).then_inc(rstd_chain, 1)
                pool.wait_ge(rstd_chain, base + 2)
                pool.tensor_tensor(rs[:, 2:3], rs[:, 1:2], rs[:, 1:2], ALU.mult).then_inc(rstd_chain, 1)
                pool.wait_ge(rstd_chain, base + 3)
                pool.tensor_tensor(rs[:, 2:3], rs[:, 2:3], rs[:, 0:1], ALU.mult).then_inc(rstd_chain, 1)
                pool.wait_ge(rstd_chain, base + 4)
                hold(pool)
                pool.tensor_scalar(rs[:, 2:3], rs[:, 2:3], -0.5, 1.5, ALU.mult, ALU.add).then_inc(rstd_chain, 1)
                pool.wait_ge(rstd_chain, base + 5)
                pool.tensor_tensor(rs[:, 3:4], rs[:, 1:2], rs[:, 2:3], ALU.mult).then_inc(rstd_done, 1)

            def add_bias(p, c):
                t, par, uses = tile(p, c)
                if not early(t):
                    if high:
                        pool.wait_ge(out_done, t - 1)
                    else:
                        pool.wait_ge(stored[par], uses * 16)
                pool.wait_ge(x_loaded[par], uses * 16 + 16)
                pool.tensor_tensor(xb[par][:, :], x_t[par][:, :], bias_all[:, :], ALU.add).then_inc(xb_done, 1)

            def program():
                pool.memset(neg_half[:, :], -0.5)
                pool.memset(ident[:, :], 0.0).then_inc(consts, 1)
                pool.wait_ge(consts, 1)
                pool.affine_select(out=ident[:, :], in_=ident[:, :], compare_op=ALU.not_equal, fill=1.0,
                                   base=0, pattern=[[-1, P]], channel_multiplier=1).then_inc(consts, 1)
                rstd(0, 0)
                pool.wait_ge(bias_loaded, 16)
                for t in range(3):
                    rstd(0, t + 1)
                    add_bias(0, t)
                with pool.Fori(2, TILES // 2) as p:
                    rstd(p, 0)
                    add_bias(p, -1)
                    rstd(p, 1)
                    add_bias(p, 0)
                add_bias(TILES // 2 - 1, 1)
                if not high:
                    pool.wait_ge(worst_done, TILES + 1)
                    pool.partition_all_reduce(worst_all[:, :], worst[:, :], P, bass.bass_isa.ReduceOp.max)\
                        .then_inc(worst_all_done, 1)

            guarded(pool, program)

        @block.scalar
        def _(act):
            def norms(p, c):
                t, par, _ = tile(p, c)
                act.wait_ge(xn_done, t + 1)
                if not early(t):
                    act.wait_ge(worst_done, t)
                if not (isinstance(t, int) and t == 0):
                    act.wait_ge(norm_done, t)
                act.activation(squares[:, :], xn[par][:, :], ACT.Square, accum_out=norm_sq[par][:, :])\
                    .then_inc(norm_done, 1)

            def split_hi(p, c):
                t, par, _ = tile(p, c)
                for half in range(2):
                    act.wait_ge(fill_done, t * 2 + (half + 1))
                    act.activation(xT_hi[par][:, 4 * half:4 * half + 4, :],
                                   t_ps[half][:, :].rearrange("p (k t) -> p k t", k=4), ACT.Copy)\
                        .then_inc(hi_done, 1)

            def program():
                def pair(p):
                    for c in range(2):
                        split_hi(p, c)
                        norms(p, c)

                pair(0)
                with act.Fori(1, TILES // 2) as p:
                    pair(p)

            guarded(act, program)

        @block.vector
        def _(dve):
            def normalize(p, c):
                t, par, uses = tile(p, c)
                dve.wait_ge(x_loaded[par], uses * 16 + 16)
                for half in range(2):
                    last = dve.bn_stats(bn[:, half, :], x_t[par][:, half * SEQ:(half + 1) * SEQ])
                last.then_inc(bn_done, 1)
                dve.wait_ge(bn_done, t + 1)
                hold(dve)
                dve.bn_aggr(mv[:, :], bn[:, :, :].rearrange("p a b -> p (a b)")).then_inc(stats_done, 1)
                dve.wait_ge(rstd_done, t + 1)
                if not early(t):
                    dve.wait_ge(fill_done, t * 2 - 2)
                    dve.wait_ge(norm_done, t - 1)
                dve.tensor_scalar(xn[par][:, :], x_t[par][:, :], mv[:, 0:1], rs[:, 3:4],
                                  ALU.subtract, ALU.mult).then_inc(xn_done, 1)

            def split_lo(p, c):
                t, par, _ = tile(p, c)
                for half in range(2):
                    dve.wait_ge(hi_done, t * 2 + (half + 1))
                    dve.tensor_tensor(xT_lo[par][:, 4 * half:4 * half + 4, :],
                                      t_ps[half][:, :].rearrange("p (k t) -> p k t", k=4),
                                      xT_hi[par][:, 4 * half:4 * half + 4, :].bitcast(F32),
                                      ALU.subtract).then_inc(lo_done, 1)

            def judge(p, c):
                t, par, _ = tile(p, c)
                dve.wait_ge(norm_done, t + 1)
                dve.wait_ge(worst_done, t + 1)
                if high:
                    hold(dve)
                    dve.tensor_scalar(chosen[par][:, :], norm_sq[par][:, :], THRESHOLD_SQ, None, ALU.is_gt)\
                        .then_inc(worst_done, 1)
                else:
                    dve.tensor_tensor(worst[:, :], worst[:, :], norm_sq[par][:, :], ALU.max)\
                        .then_inc(worst_done, 1)

            def finish(p, c, half):
                t, par, uses = tile(p, c)
                if half == 0:
                    dve.wait_ge(xb_done, t + 1)
                cols = slice(half * SEQ, (half + 1) * SEQ)
                dve.wait_ge(mm_done, t * 2 + (half + 1))
                add = dve.tensor_tensor(xb[par][:, cols], y_ps[2 * par + half][:, :], xb[par][:, cols], ALU.add)
                if half == 1:
                    add.then_inc(y_done if high else out_done, 1)
                if half == 1 and high:
                    dve.wait_ge(y_done, t + 1)
                    dve.wait_ge(old_loaded[par], uses * 16 + 16)
                    hold(dve)
                    dve.copy_predicated(old[par][:, :], chosen[par][:, 0:1].to_broadcast([P, D]), xb[par][:, :])\
                        .then_inc(out_done, 1)

            def slot(p, c, before=True, ahead=True, next_tile=True):
                if next_tile:
                    split_lo(p, c + 1)
                    if not high:
                        judge(p, c + 1)
                if before:
                    finish(p, c - 1, 1)
                if next_tile and high:
                    judge(p, c + 1)
                if ahead:
                    normalize(p, c + 2)
                finish(p, c, 0)

            def program():
                dve.memset(worst[:, :], 0.0).then_inc(worst_done, 1)
                normalize(0, 0)
                normalize(0, 1)
                split_lo(0, 0)
                judge(0, 0)
                for t in range(3):
                    slot(0, t, before=t > 0)
                with dve.Fori(1, TILES // 2 - 2) as p:
                    slot(p, 1)
                    slot(p, 2)
                for t in range(TILES - 3, TILES):
                    slot(0, t, ahead=t < TILES - 2, next_tile=t < TILES - 1)
                finish(0, TILES - 1, 1)
                if not high:
                    dve.wait_ge(worst_all_done, 1)
                    dve.tensor_scalar(flag[:, :], worst_all[0:1, :], THRESHOLD_SQ, None, ALU.is_gt)\
                        .then_inc(y_done, 1)
                    dve.wait_ge(y_done, 1)

            guarded(dve, program)

        @block.tensor
        def _(pe):
            def transposes(p, c):
                t, par, _ = tile(p, c)
                pe.wait_ge(xn_done, t + 1)
                for half in range(2):
                    if not (isinstance(t, int) and t == 0):
                        pe.wait_ge(lo_done, t * 2 + (half - 1))
                    for i in range(4):
                        at = (4 * half + i) * P
                        mm = pe.transpose(t_ps[half][:, i * P:(i + 1) * P], xn[par][:, at:at + P], ident[:, :])
                    mm.then_inc(fill_done, 1)

            def multiply(p, c):
                t, par, _ = tile(p, c)
                pe.wait_ge(lo_done, t * 2 + 2)
                if not early(t):
                    pe.wait_ge(y_done if high else out_done, t - 1)
                for half in range(HALVES):
                    cols = slice(half * SEQ, (half + 1) * SEQ)
                    for kt in range(KT):
                        for part in range(3):
                            a = (xT_hi, xT_lo, xT_hi)[part][par]
                            w = (wl_hi, wl_hi, wl_lo)[part]
                            mm = pe.matmul(y_ps[2 * par + half][:, :], a[:, kt, :], w[:, kt, cols],
                                           start=(kt == 0 and part == 0), stop=(kt == KT - 1 and part == 2))
                    mm.then_inc(mm_done, 1)

            def program():
                pe.wait_ge(consts, 2)
                transposes(0, 0)
                for t in range(3):
                    transposes(0, t + 1)
                    multiply(0, t)
                with pe.Fori(1, TILES // 2 - 1) as p:
                    for c in (1, 2):
                        transposes(p, c + 1)
                        multiply(p, c)
                multiply(0, TILES - 1)

            guarded(pe, program)


def wide_weights_phase(nc, outer, qweight, lut8, wl_hi, wl_lo, shifts, flag):
    with ExitStack() as buffers:
        ph = Phase(nc, buffers, outer)
        sb, pb, sem = ph.sb, ph.pb, ph.sem
        ident = sb("w_ident", [P, P])
        words = sb("w_words", [P, 8, 32], I32)
        table = sb("w_table", [P, 256])
        code = sb("w_code", [P, D], I32)
        bit = sb("w_bit", [P, D], I32)
        codef = sb("w_codef", [P, D])
        entry = sb("w_entry", [P, D])
        weights = sb("w_weights", [P, D])
        index = sb("w_index", [P, 1])
        wt_ps = [pb(f"w_t{i}", [P, SEQ]) for i in range(2)]
        ident_done = sem("w_ident_done")
        loaded = sem("w_loaded")
        chain = sem("w_chain")
        entries = sem("w_entries")
        built = sem("w_built")
        fill_done = sem("w_fill_done")
        hi_done = sem("w_hi8_done")
        lo_done = sem("w_lo8_done")
        waited = sem("w_waited")
        CODES = 256
        BITS = 8
        CHAIN = 3 * BITS + 2

        block = buffers.enter_context(nc.Block())

        def guarded(eng, program):
            value = eng.value_load(flag[0:1, 0:1], min_val=0, max_val=1)
            with eng.If(value > 0):
                program()
            with eng.Else():
                eng.nop()

        @block.sync
        def _(sp):
            def program():
                with sp.Fori(0, OTILES) as o:
                    sp.wait_ge(built, o + 1)
                    sp.sem_inc(waited, 1)
                    sp.dma_start(words[:, :, :], qweight[:, bass.ds(o * P, P), :].rearrange("b o w -> o b w"))\
                        .then_inc(loaded, 16)
                    sp.dma_start(table[:, :], lut8[bass.ds(o * P, P), :]).then_inc(loaded, 16)

            guarded(sp, program)

        @block.gpsimd
        def _(pool):
            def program():
                pool.memset(ident[:, :], 0.0).then_inc(ident_done, 1)
                pool.wait_ge(ident_done, 1)
                pool.affine_select(out=ident[:, :], in_=ident[:, :], compare_op=ALU.not_equal, fill=1.0,
                                   base=0, pattern=[[-1, P]], channel_multiplier=1).then_inc(ident_done, 1)

            guarded(pool, program)

        @block.vector
        def _(dve):
            def program():
                dve.sem_inc(built, 1)
                dve.sem_inc(lo_done, 2)
                with dve.Fori(0, OTILES) as o:
                    count = [0]

                    def chained(instruction):
                        count[0] += 1
                        instruction.then_inc(chain, 1)
                        dve.wait_ge(chain, o * CHAIN + count[0])

                    dve.wait_ge(loaded, o * 32 + 32)
                    for b in range(BITS):
                        target = code if b == 0 else bit
                        spread = target[:, :].rearrange("p (w s) -> p w s", s=32)
                        chained(dve.tensor_tensor(spread, words[:, b, :].unsqueeze(2).to_broadcast([P, 32, 32]),
                                                  shifts[:, 2, :].unsqueeze(1).to_broadcast([P, 32, 32]),
                                                  ALU.logical_shift_right))
                        dve.sem_inc(waited, 1)
                        chained(dve.tensor_scalar(target[:, :], target[:, :], 1, b,
                                                  ALU.bitwise_and, ALU.logical_shift_left))
                        if b:
                            chained(dve.tensor_tensor(code[:, :], code[:, :], bit[:, :], ALU.bitwise_or))
                    chained(dve.tensor_copy(codef[:, :], code[:, :]))
                    dve.wait_ge(fill_done, o * 2 + 2)
                    dve.sem_inc(waited, 1)
                    chained(dve.memset(weights[:, :], 0.0))
                    chained(dve.memset(index[:, :], 0.0))
                    dve.sem_inc(waited, 1)
                    assert count[0] == CHAIN
                    with dve.Fori(0, CODES) as j:
                        at = o * (3 * CODES) + j * 3
                        dve.tensor_scalar(entry[:, :], codef[:, :], index[:, 0:1], table[:, bass.ds(j, 1)],
                                          ALU.is_equal, ALU.mult).then_inc(entries, 1)
                        dve.wait_ge(entries, at + 1)
                        dve.tensor_tensor(weights[:, :], weights[:, :], entry[:, :], ALU.add).then_inc(entries, 1)
                        dve.wait_ge(entries, at + 2)
                        dve.sem_inc(waited, 1)
                        dve.tensor_scalar(index[:, :], index[:, :], 1.0, None, ALU.add).then_inc(entries, 1)
                        dve.wait_ge(entries, at + 3)
                        dve.sem_inc(waited, 1)
                    dve.sem_inc(built, 1)
                    for half in range(2):
                        at = wl_hi[:, 4 * half:4 * half + 4, bass.ds(o * P, P)]
                        dve.wait_ge(hi_done, o * 2 + half + 1)
                        dve.tensor_tensor(wl_lo[:, 4 * half:4 * half + 4, bass.ds(o * P, P)],
                                          wt_ps[half][:, :].rearrange("p (k o) -> p k o", k=4),
                                          at.bitcast(F32), ALU.subtract).then_inc(lo_done, 1)

            guarded(dve, program)

        @block.tensor
        def _(pe):
            def program():
                pe.wait_ge(ident_done, 2)
                pe.sem_inc(fill_done, 2)
                with pe.Fori(0, OTILES) as o:
                    pe.wait_ge(built, o + 2)
                    pe.wait_ge(lo_done, o * 2 + 2)
                    for half in range(2):
                        for i in range(4):
                            at = (4 * half + i) * P
                            mm = pe.transpose(wt_ps[half][:, i * P:(i + 1) * P], weights[:, at:at + P],
                                              ident[:, :])
                        mm.then_inc(fill_done, 1)

            guarded(pe, program)

        @block.scalar
        def _(act):
            def program():
                with act.Fori(0, OTILES) as o:
                    for half in range(2):
                        act.wait_ge(fill_done, o * 2 + half + 3)
                        act.activation(wl_hi[:, 4 * half:4 * half + 4, bass.ds(o * P, P)],
                                       wt_ps[half][:, :].rearrange("p (k o) -> p k o", k=4), ACT.Copy)\
                            .then_inc(hi_done, 1)

            guarded(act, program)


def build(nc, x, w_qkv, b_qkv, wo, bo, qweight, lut4, lut8, fbias, out):
    att = nc.dram_tensor("att_scratch", (STEPS, P, SEQ), F32, kind="Internal").ap()
    x1 = nc.dram_tensor("x1_scratch", (TOKENS, D), F32, kind="Internal").ap()
    with ExitStack() as outer:
        attention_phase(nc, outer, x, w_qkv, b_qkv, att)
        keep = Phase(nc, outer, outer)
        wl_hi = keep.sb("wl_hi", [P, KT, D], F32R)
        wl_lo = keep.sb("wl_lo", [P, KT, D], F32R)
        flag = keep.sb("flag", [1, 1], I32)
        shifts = keep.sb("shifts", [P, 3, 32], I32)
        ones = keep.sb("ones", [P, 32], I32)
        tables_done = keep.sem("tables_done")
        with nc.Block() as block:
            @block.gpsimd
            def _(pool):
                pool.iota(shifts[:, 0, :], pattern=[[-1, 32]], base=31, channel_multiplier=0).then_inc(tables_done, 1)
                pool.iota(shifts[:, 2, :], pattern=[[1, 32]], base=0, channel_multiplier=0).then_inc(tables_done, 1)
                pool.iota(ones[:, :], pattern=[[0, 32]], base=1, channel_multiplier=0).then_inc(tables_done, 1)

            @block.vector
            def _(dve):
                dve.wait_ge(tables_done, 3)
                dve.tensor_tensor(shifts[:, 1, :], ones[:, :], shifts[:, 2, :], ALU.logical_shift_left)\
                    .then_inc(tables_done, 1)
                dve.wait_ge(tables_done, 4)
        output_phase(nc, outer, x, wo, bo, att, qweight, lut4, x1, wl_hi, wl_lo, shifts)
        feed_forward_phase(nc, outer, x1, fbias, out, wl_hi, wl_lo, flag, "", high=False)
        wide_weights_phase(nc, outer, qweight, lut8, wl_hi, wl_lo, shifts, flag)
        feed_forward_phase(nc, outer, x1, fbias, out, wl_hi, wl_lo, flag, "_8", high=True, run_if=flag)


def kernel(**inputs):
    import numpy as np
    import concourse.bacc as bacc
    from concourse.bass_utils import run_bass_kernel_spmd

    a = {name.split("_", 1)[1]: np.asarray(value) for name, value in inputs.items()}
    w = np.stack([a["attn_Wq"], a["attn_Wk"], a["attn_Wv"]]).reshape(3, GROUPS, P, KT, P)
    b = np.stack([a["attn_bq"], a["attn_bk"], a["attn_bv"]]).reshape(3, GROUPS, P)
    arrays = {
        "x": a["attn_x"].reshape(TOKENS, D),
        "w_qkv": np.ascontiguousarray(w.transpose(1, 4, 0, 3, 2)).reshape(GROUPS, P, 3, KT * P),
        "b_qkv": np.ascontiguousarray(b.transpose(2, 0, 1)),
        "wo": np.ascontiguousarray(a["attn_Wo"].reshape(D, KT, P).transpose(2, 1, 0)),
        "bo": a["attn_bo"],
        "qweight": a["ffn_qweight"],
        "lut4": a["ffn_lut4"],
        "lut8": a["ffn_lut8"],
        "fbias": a["ffn_bias"],
    }
    nc = bacc.Bacc("TRN2", target_bir_lowering=False, num_devices=1)
    args = {}
    for name, value in arrays.items():
        args[name] = nc.dram_tensor(name, value.shape, mybir.dt.from_np(value.dtype), kind="ExternalInput").ap()
    args["out"] = nc.dram_tensor("out", (TOKENS, D), F32, kind="ExternalOutput").ap()
    build(nc, **args)
    result = run_bass_kernel_spmd(nc, [arrays], core_ids=[0])
    return result.results[0]["out"].reshape(BATCH, SEQ, D)
```

```python
import concourse.bass as bass
from concourse import mybir
from concourse.alu_op_type import AluOpType as ALU
from contextlib import ExitStack

F32 = mybir.dt.float32
F32R = mybir.dt.float32r
BF16 = mybir.dt.bfloat16
I32 = mybir.dt.int32
ACT = mybir.ActivationFunctionType
AXIS = mybir.AxisListType

P = 128
D = 1024
BATCH, SEQ = 4, 512
TOKENS = BATCH * SEQ
HEADS, HD = 32, 32
KT = D // P
GH = P // HD
GROUPS = HEADS // GH
QT = SEQ // P
STEPS = BATCH * GROUPS
SCALE = 1.0 / float(HD) ** 0.5
EPS = 1e-5
MASKED = -3.0e38
THRESHOLD_SQ = 64.0 ** 2
Q, K, V = range(3)

CH = 64
CHUNKS = TOKENS // CH
CHUNKS_AHEAD = SEQ // CH + 1
AHEAD = SEQ // P + 1
FILLS_AHEAD = 2 * (SEQ // P) + 1

P_OFF = [0, 128, 384, 768]
P_COLS = 1280
T_FILLS = [[(0, 0), (0, 1), (0, 2), (0, 3)], [(3, 3), (1, 1), (1, 2), (1, 3)], [(2, 2), (2, 3)]]
T_DEST = [640, 128, 1152]
PT_COLS = 1408
PT_KT = [640, 256, 1152, 0]
PT_QT = [0, 1, 2, 2]
S_COL = [0, 256, 512, 1024]
S_KEYS = [256, 256, 384, 512]


class Phase:

    def __init__(self, nc, buffers, outer):
        self.nc, self.buffers, self.outer = nc, buffers, outer

    def sb(self, name, shape, dt=F32):
        return self.buffers.enter_context(self.nc.sbuf_tensor(name, shape, dt))

    def pb(self, name, shape, dt=F32):
        return self.buffers.enter_context(self.nc.psum_tensor(name, shape, dt))

    def sem(self, name):
        return self.outer.enter_context(self.nc.semaphore(name))


def attention_phase(nc, outer, x, w_qkv, b_qkv, att, wo, stage, wo_raw, att_raw, wo_loaded, att_loaded,
                    att_stored, o_out):
    with ExitStack() as buffers:
        ph = Phase(nc, buffers, outer)
        sb, pb, sem = ph.sb, ph.pb, ph.sem
        ident = sb("ident", [P, P])
        identb = sb("identb", [P, P], BF16)
        maskb = sb("maskb", [P, P], BF16)
        bias = sb("bias", [P, 3, GROUPS])
        staged = stage[:, :, :].rearrange("p (part k) (two t) -> p part (k two) t", part=2, two=2)
        xT_hi = [staged[:, 0], sb("xT_hi1", [P, KT, SEQ], F32R)]
        xT_lo = [staged[:, 1], sb("xT_lo1", [P, KT, SEQ], F32R)]
        w_raw = sb("w_raw", [P, 3, KT * P])
        w_hi = sb("w_hi", [P, 3, KT * P], F32R)
        w_lo = sb("w_lo", [P, 3, KT * P], F32R)
        qk_hi = sb("qk_hi", [P, 2, SEQ], F32R)
        qk_lo = sb("qk_lo", [P, 2, SEQ], F32R)
        q_stack = sb("q_stack", [3 * HD, GH, SEQ], F32R)
        k_stack = sb("k_stack", [3 * HD, GH, SEQ], F32R)
        vT = sb("vT", [P, SEQ])
        v_parts = sb("v_parts", [P, QT, GH, 2 * HD], F32R)
        probs = [sb(f"probs{i}", [P, P_COLS]) for i in range(2)]
        pT_hi = [sb(f"pT_hi{i}", [P, PT_COLS], F32R) for i in range(2)]
        pT_lo = [sb(f"pT_lo{i}", [P, PT_COLS], F32R) for i in range(2)]
        row_max = [sb(f"row_max{i}", [P, QT]) for i in range(2)]
        neg_max = [sb(f"neg_max{i}", [P, QT]) for i in range(2)]
        row_sum = [sb(f"row_sum{i}", [P, QT]) for i in range(2)]
        inv_sum = [sb(f"inv_sum{i}", [P, QT]) for i in range(2)]
        o_low = sb("o_low", [HD, SEQ])
        x_in = sb("x_in", [CH, D])
        xn = sb("xn", [CH, D])
        x_first = [sb(f"x_first{i}", [P, D]) for i in range(2)] + [probs[i][:, 0:D] for i in range(2)]
        first_mv = sb("first_mv", [P, 2, 2, 2])
        first_rs = sb("first_rs", [P, 2, 4, 2])
        bn = sb("bn", [P, 2, 6])
        mv = sb("mv", [P, 2])
        rs = sb("rs", [P, 4])
        neg_half = sb("neg_half", [P, 2])

        proj_ps = [pb(f"proj_ps{i}", [P, SEQ]) for i in range(2)]
        score_ps = pb("score_ps", [P, 3 * SEQ])
        t_ps = [pb(f"t_ps{i}", [P, SEQ]) for i in range(2)]
        o_ps = pb("o_ps", [2 * HD, SEQ])

        bias_in = sem("bias_in")
        consts = sem("consts")
        zeros_done = sem("zeros_done")
        x_loaded = sem("x_loaded")
        first_loaded = [sem(f"first_loaded{i}") for i in range(SEQ // P)]
        first_bn_done = sem("first_bn_done")
        first_stats_done = sem("first_stats_done")
        first_chain = sem("first_chain")
        first_rstd_done = sem("first_rstd_done")
        w_loaded = [sem(f"w_loaded{m}") for m in range(3)]
        w_hi_done = sem("w_hi_done")
        w_lo_done = sem("w_lo_done")
        bn_done = sem("bn_done")
        rstd_done = sem("rstd_done")
        stats_done = sem("stats_done")
        rstd_chain = sem("rstd_chain")
        xn_done = sem("xn_done")
        proj_done = sem("proj_done")
        qk_hi_done = sem("qk_hi_done")
        qk_lo_done = sem("qk_lo_done")
        v_done = sem("v_done")
        stacked = [sem(f"stacked{i}") for i in range(2)]
        scores_done = sem("scores_done")
        max_done = sem("max_done")
        negmax_done = sem("negmax_done")
        exp_done = sem("exp_done")
        inv_done = sem("inv_done")
        norm_done = sem("norm_done")
        fill_done = sem("fill_done")
        hi_done = sem("hi_done")
        lo_done = sem("lo_done")
        pv_done = sem("pv_done")
        low_copied = sem("low_copied")
        head_done = sem("head_done")

        def has_chunk(b, g):
            return 8 * b + (g if isinstance(g, int) else 0) + CHUNKS_AHEAD < CHUNKS

        def after_chunk(b, g):
            return 8 * b + (g if isinstance(g, int) else 0) - 1 + CHUNKS_AHEAD < CHUNKS

        def step_of(b, g):
            return g + GROUPS * b

        def fill(b, g, i):
            with_chunk = CHUNKS - CHUNKS_AHEAD
            base = FILLS_AHEAD - 3 + i
            if GROUPS * b >= with_chunk:
                return g * 13 + (14 * with_chunk + 13 * (GROUPS * b - with_chunk) + base)
            return g * 14 + (14 * GROUPS * b + base)

        def slot_fill(h, f):
            return 3 * h + f + (1 if h >= 2 else 0)

        def next_pos(b, g):
            if isinstance(g, int) and g == GROUPS - 1:
                return b + 1, 0
            return b, g + 1

        def emit(eng, prologue, step, tail):
            prologue()
            step(0, 0)
            for b in range(BATCH):
                with eng.Fori(1 if b == 0 else 0, GROUPS - 1) as g:
                    step(b, g)
                step(b, GROUPS - 1)
            tail()

        def slot_before(b, g, h, k):
            return step_of(b, g) * GH + (h - k)

        def first(b, g, h, k):
            return isinstance(g, int) and step_of(b, g) == 0 and h < k

        def last(b, g):
            return isinstance(g, int) and step_of(b, g) == STEPS - 1

        waited = sem("waited")

        def hold(eng):
            eng.sem_inc(waited, 1)

        block = buffers.enter_context(nc.Block())

        @block.sync
        def _(sp):
            def load_w(m, n, wrapped):
                if not (isinstance(n, int) and n == 0):
                    sp.wait_ge(w_lo_done, (n - 1) * 3 + m + 1)
                    hold(sp)
                sp.dma_start(w_raw[:, m, :], w_qkv[wrapped, :, m, :]).then_inc(w_loaded[m], 16)

            def load_first(t):
                sp.dma_start(x_first[t][:, :], x[t * P:(t + 1) * P, :]).then_inc(first_loaded[t], 16)

            def load_x(k):
                if not (isinstance(k, int) and k == AHEAD - 1):
                    sp.wait_ge(xn_done, k)
                    hold(sp)
                c = (k + (CHUNKS_AHEAD - AHEAD)) % CHUNKS
                sp.dma_start(x_in[:, :], x[bass.ds(c * CH, CH), :]).then_inc(x_loaded, 16)

            def stack(pair, m):
                stack_of, parts = ((q_stack, (qk_hi, qk_lo, qk_hi)), (k_stack, (qk_hi, qk_hi, qk_lo)))[m]
                for h in (2 * pair, 2 * pair + 1):
                    for part, src in enumerate(parts):
                        sp.dma_start(stack_of[part * HD:(part + 1) * HD, h, :].bitcast(F32),
                                     src[h * HD:(h + 1) * HD, m, :].bitcast(F32))\
                            .then_inc(stacked[pair], 16)

            def store(b, g, h):
                if first(b, g, h, 3):
                    return
                head = (h + 1) % GH
                n = step_of(b, g) - (1 if h < 3 else 0)
                sp.wait_ge(head_done, slot_before(b, g, h, 3) + 1)
                hold(sp)
                sp.dma_start(att[n, head * HD:(head + 1) * HD, :],
                             o_out[head * HD:(head + 1) * HD, :]).then_inc(att_stored[head], 16)

            def prologue():
                for head in range(GH):
                    sp.sem_inc(att_stored[head], 16)
                for t in range(SEQ // P):
                    load_first(t)
                sp.dma_start(bias[:, :, :], b_qkv).then_inc(bias_in, 16)
                for m in (Q, K, V):
                    load_w(m, 0, 0)
                load_x(AHEAD - 1)
                for m in (Q, K, V):
                    load_w(m, 1, 1)
                load_x(AHEAD)
                for m in (Q, K):
                    sp.wait_ge(qk_lo_done, m + 1)
                    stack(0, m)
                load_w(Q, 2, 2)
                stack(1, Q)
                stack(1, K)

            def step(b, g):
                n = step_of(b, g)
                if not last(b, g):
                    load_w(K, n + 2, (g + 2) % GROUPS)
                store(b, g, 0)
                if not last(b, g):
                    load_w(V, n + 2, (g + 2) % GROUPS)
                store(b, g, 1)
                if b == BATCH - 1:
                    sp.wait_ge(proj_done, 3 * GROUPS * b)
                    sp.dma_start(wo_raw[:, bass.ds(g, 1), :], wo[:, bass.ds(g, 1), :]).then_inc(wo_loaded, 16)
                if not last(b, g):
                    sp.wait_ge(qk_lo_done, (n + 1) * 2 + 1)
                    hold(sp)
                    sp.wait_ge(scores_done, n * GH + 2)
                    hold(sp)
                    stack(0, Q)
                store(b, g, 2)
                if not last(b, g):
                    sp.wait_ge(qk_lo_done, (n + 1) * 2 + 2)
                    hold(sp)
                    stack(0, K)
                if has_chunk(b, g):
                    load_x(n + AHEAD + 1)
                if not last(b, g):
                    load_w(Q, n + 3, (g + 3) % GROUPS)
                store(b, g, 3)
                if not last(b, g):
                    sp.wait_ge(scores_done, n * GH + 4)
                    hold(sp)
                    stack(1, Q)
                    stack(1, K)

            def tail():
                for head in range(GH):
                    sp.wait_ge(att_stored[head], GROUPS * 16 + 16)
                for par in range(2):
                    sp.dma_start(att_raw[par][:, :, :],
                                 att[0:GROUPS, :, par * P:(par + 1) * P].rearrange("g p t -> p g t"))\
                        .then_inc(att_loaded[par], 16)
                for h in range(3):
                    sp.wait_ge(head_done, STEPS * GH - 2 + h)
                    head = h + 1
                    sp.dma_start(att[STEPS - 1, head * HD:(head + 1) * HD, :],
                                 o_out[head * HD:(head + 1) * HD, :]).then_inc(att_stored[head], 16)
                sp.wait_ge(w_loaded[Q], (STEPS + 2) * 16)
                sp.wait_ge(w_loaded[K], (STEPS + 1) * 16)
                sp.wait_ge(w_loaded[V], (STEPS + 1) * 16)
                sp.wait_ge(x_loaded, (CHUNKS - CHUNKS_AHEAD + 2) * 16)

            emit(sp, prologue, step, tail)

        @block.gpsimd
        def _(pool):
            def split_w_lo(m, n):
                pool.wait_ge(w_hi_done, n * 3 + m + 1)
                pool.tensor_tensor(w_lo[:, m, :], w_raw[:, m, :], w_hi[:, m, :].bitcast(F32),
                                   ALU.subtract).then_inc(w_lo_done, 1)

            def rstd(chain, base, done, var, v):
                pool.tensor_scalar(v[0], var, EPS, None, ALU.add).then_inc(chain, 1)
                pool.wait_ge(chain, base + 1)
                pool.tensor_tensor(v[1], v[0], neg_half[0:var.shape[0], 0:var.shape[1]], ALU.pow).then_inc(chain, 1)
                pool.wait_ge(chain, base + 2)
                pool.tensor_tensor(v[2], v[1], v[1], ALU.mult).then_inc(chain, 1)
                pool.wait_ge(chain, base + 3)
                pool.tensor_tensor(v[2], v[2], v[0], ALU.mult).then_inc(chain, 1)
                pool.wait_ge(chain, base + 4)
                hold(pool)
                pool.tensor_scalar(v[2], v[2], -0.5, 1.5, ALU.mult, ALU.add).then_inc(chain, 1)
                pool.wait_ge(chain, base + 5)
                pool.tensor_tensor(v[3], v[1], v[2], ALU.mult).then_inc(done, 1)

            def chunk_rstd(c):
                pool.wait_ge(stats_done, c + 1)
                hold(pool)
                rstd(rstd_chain, c * 5, rstd_done, mv[0:CH, 1:2],
                     [rs[0:CH, i:i + 1] for i in range(4)])

            def prologue():
                pool.memset(neg_half[:, :], -0.5)
                pool.memset(ident[:, :], 0.0).then_inc(consts, 1)
                pool.memset(maskb[:, :], 0.0).then_inc(consts, 1)
                pool.wait_ge(consts, 2)
                pool.affine_select(out=ident[:, :], in_=ident[:, :], compare_op=ALU.not_equal, fill=1.0,
                                   base=0, pattern=[[-1, P]], channel_multiplier=1).then_inc(consts, 1)
                pool.affine_select(out=maskb[:, :], in_=maskb[:, :], compare_op=ALU.is_ge, fill=MASKED,
                                   base=0, pattern=[[-1, P]], channel_multiplier=1).then_inc(consts, 1)
                pool.wait_ge(consts, 4)
                pool.tensor_copy(identb[:, :], ident[:, :]).then_inc(consts, 1)
                for pair in range(2):
                    pool.wait_ge(first_stats_done, 2 * pair + 2)
                    rstd(first_chain, 5 * pair, first_rstd_done, first_mv[:, pair, :, 1],
                         [first_rs[:, pair, i, :] for i in range(4)])
                split_w_lo(Q, 0)
                chunk_rstd(0)
                split_w_lo(K, 0)
                split_w_lo(V, 0)
                for m in (Q, K):
                    split_w_lo(m, 1)

            def step(b, g):
                n = step_of(b, g)
                if last(b, g):
                    return
                if has_chunk(b, g):
                    chunk_rstd(n + 1)
                split_w_lo(V, n + 1)
                split_w_lo(Q, n + 2)
                split_w_lo(K, n + 2)

            emit(pool, prologue, step, lambda: None)

        @block.scalar
        def _(act):
            def split_w_hi(m, n):
                act.wait_ge(w_loaded[m], n * 16 + 16)
                if not (isinstance(n, int) and n == 0):
                    act.wait_ge(proj_done, (n - 1) * 3 + m + 1)
                act.activation(w_hi[:, m, :], w_raw[:, m, :], ACT.Copy).then_inc(w_hi_done, 1)

            def chunk_hi(c_col, half, number, bank):
                act.wait_ge(fill_done, number + 1)
                act.activation(xT_hi[half][:, :, bass.ds(c_col, CH)],
                               t_ps[bank][:, :].rearrange("p (k t) -> p k t", k=KT), ACT.Copy)\
                    .then_inc(hi_done, 1)

            def qk_hi_part(m, n, g):
                act.wait_ge(proj_done, n * 3 + m + 1)
                if not (isinstance(n, int) and n == 0) and m == Q:
                    for pair in range(2):
                        act.wait_ge(stacked[pair], n * 12 * 16)
                act.activation(qk_hi[:, m, :], proj_ps[m][:, :], ACT.Identity, bias=bias[:, m, bass.ds(g, 1)])\
                    .then_inc(qk_hi_done, 1)

            def biased_v(n, g):
                act.wait_ge(proj_done, n * 3 + V + 1)
                act.activation(vT[:, :], proj_ps[0][:, :], ACT.Identity, bias=bias[:, V, bass.ds(g, 1)])\
                    .then_inc(v_done, 1)

            def prologue():
                split_w_hi(Q, 0)
                for t in range(SEQ // P):
                    for half in range(2):
                        act.wait_ge(fill_done, 2 * t + half + 1)
                        act.activation(xT_hi[0][:, 4 * half:4 * half + 4, t * P:(t + 1) * P],
                                       t_ps[half][:, :].rearrange("p (k t) -> p k t", k=4), ACT.Copy)\
                            .then_inc(hi_done, 1)
                    if t in (1, 2):
                        split_w_hi(t, 0)
                chunk_hi(0, 1, FILLS_AHEAD - 1, 0)
                act.wait_ge(bias_in, 16)
                qk_hi_part(Q, 0, 0)
                split_w_hi(Q, 1)
                qk_hi_part(K, 0, 0)
                split_w_hi(K, 1)
                biased_v(0, 0)

            def step(b, g):
                n = step_of(b, g)
                _, ng = next_pos(b, g)
                for h in range(GH):
                    s = n * GH + h
                    if not first(b, g, h, 3):
                        act.wait_ge(pv_done, s - 2)
                    if h == 2:
                        act.wait_ge(fill_done, fill(b, g, 6) + 1)
                        act.activation(v_parts[:, :, :, 0:HD],
                                       t_ps[0][:, :].rearrange("p (k h d) -> p k h d", k=QT, h=GH),
                                       ACT.Copy).then_inc(hi_done, 1)
                    if not first(b, g, h, 3):
                        act.activation(o_low[:, :], o_ps[HD:2 * HD, :], ACT.Copy).then_inc(low_copied, 1)
                    prev = (h + 1) % 2

                    def prob_hi(f):
                        i = slot_fill(h, f)
                        act.wait_ge(fill_done, fill(b, g, i) + 1)
                        w = P * len(T_FILLS[f])
                        act.activation(pT_hi[prev][:, T_DEST[f]:T_DEST[f] + w], t_ps[i % 2][:, 0:w],
                                       ACT.Copy).then_inc(hi_done, 1)

                    if not first(b, g, h, 1):
                        prob_hi(0)
                        prob_hi(1)
                    act.wait_ge(negmax_done, s + 1)
                    for qt in range(QT):
                        w = P * (qt + 1)
                        last_exp = act.activation(
                            probs[h % 2][:, P_OFF[qt]:P_OFF[qt] + w], score_ps[:, S_COL[qt]:S_COL[qt] + w],
                            ACT.Exp, bias=neg_max[h % 2][:, qt:qt + 1], scale=SCALE,
                            accum_out=row_sum[h % 2][:, qt:qt + 1])
                    last_exp.then_inc(exp_done, 1)
                    if not first(b, g, h, 1):
                        prob_hi(2)
                    if last(b, g):
                        continue
                    if h == 0:
                        split_w_hi(V, n + 1)
                    if h == 1:
                        qk_hi_part(Q, n + 1, ng)
                    if h == 2:
                        qk_hi_part(K, n + 1, ng)
                        split_w_hi(Q, n + 2)
                    if h == 3:
                        biased_v(n + 1, ng)
                        if has_chunk(b, g):
                            half = (b + 1 + (1 if isinstance(g, int) and g == GROUPS - 1 else 0)) % 2
                            col = 0 if isinstance(g, int) and g == GROUPS - 1 else (g + 1) * CH
                            chunk_hi(col, half, fill(b, g, 13), 1)
                        split_w_hi(K, n + 2)

            def tail():
                s = STEPS * GH
                act.wait_ge(pv_done, s - 2)
                act.activation(o_low[:, :], o_ps[HD:2 * HD, :], ACT.Copy).then_inc(low_copied, 1)
                for f in range(3):
                    act.wait_ge(fill_done, fill(BATCH - 1, GROUPS, f) + 1)
                    w = P * len(T_FILLS[f])
                    act.activation(pT_hi[1][:, T_DEST[f]:T_DEST[f] + w], t_ps[f % 2][:, 0:w],
                                   ACT.Copy).then_inc(hi_done, 1)
                for k in (1, 0):
                    act.wait_ge(pv_done, s - k)
                    act.activation(o_low[:, :], o_ps[HD:2 * HD, :], ACT.Copy).then_inc(low_copied, 1)

            emit(act, prologue, step, tail)

        @block.vector
        def _(dve):
            def stats(src, rows, bn_sem, bn_count, dst, done):
                for half in range(2):
                    last_bn = dve.bn_stats(bn[0:rows, half, :], src[:, half * 512:(half + 1) * 512])
                last_bn.then_inc(bn_sem, 1)
                dve.wait_ge(bn_sem, bn_count)
                hold(dve)
                dve.bn_aggr(dst, bn[0:rows, :, :].rearrange("p a b -> p (a b)")).then_inc(done, 1)

            def chunk_stats(c):
                dve.wait_ge(x_loaded, c * 16 + 16)
                stats(x_in[:, :], CH, bn_done, c + 1, mv[0:CH, :], stats_done)

            def chunk_normalize(c, number):
                if number is not None:
                    dve.wait_ge(fill_done, number)
                dve.wait_ge(rstd_done, c + 1)
                dve.tensor_scalar(xn[:, :], x_in[:, :], mv[0:CH, 0:1], rs[0:CH, 3:4], ALU.subtract, ALU.mult)\
                    .then_inc(xn_done, 1)

            def lo_part(dst, src, hi, number):
                dve.wait_ge(hi_done, number + 1)
                dve.tensor_tensor(dst, src, hi, ALU.subtract).then_inc(lo_done, 1)

            def chunk_lo(c_col, half, number, bank):
                cols = bass.ds(c_col, CH)
                lo_part(xT_lo[half][:, :, cols], t_ps[bank][:, :].rearrange("p (k t) -> p k t", k=KT),
                        xT_hi[half][:, :, cols].bitcast(F32), number)

            def qk_lo_part(m, n, g):
                dve.wait_ge(qk_hi_done, n * 2 + m + 1)
                dve.scalar_tensor_tensor(qk_lo[:, m, :], proj_ps[m][:, :], bias[:, m, bass.ds(g, 1)],
                                         qk_hi[:, m, :].bitcast(F32), ALU.add, ALU.subtract)\
                    .then_inc(qk_lo_done, 1)

            def combine(h, s, quadrant_use):
                head = (h + 1) % GH
                dve.wait_ge(low_copied, s - 2)
                if quadrant_use is not None:
                    dve.wait_ge(att_stored[head], quadrant_use * 16 + 16)
                dve.tensor_tensor(o_out[head * HD:(head + 1) * HD, :], o_ps[0:HD, :], o_low[:, :],
                                  ALU.add).then_inc(head_done, 1)

            def prologue():
                for i in range(2):
                    dve.memset(pT_hi[i][:, 0:P].bitcast(F32), 0.0)
                    dve.memset(pT_lo[i][:, 0:P].bitcast(F32), 0.0).then_inc(zeros_done, 1)

                def first_lo(t):
                    for half in range(2):
                        cols = (slice(None), slice(4 * half, 4 * half + 4), slice(t * P, (t + 1) * P))
                        lo_part(xT_lo[0][cols], t_ps[half][:, :].rearrange("p (k t) -> p k t", k=4),
                                xT_hi[0][cols].bitcast(F32), 2 * t + half)

                def first_stats(t):
                    dve.wait_ge(first_loaded[t], 16)
                    if t:
                        dve.wait_ge(first_stats_done, t)
                    stats(x_first[t], P, first_bn_done, t + 1, first_mv[:, t // 2, t % 2, :], first_stats_done)

                def first_normalize(t):
                    if t % 2 == 0:
                        dve.wait_ge(first_rstd_done, t // 2 + 1)
                    dve.tensor_scalar(x_first[t][:, :], x_first[t][:, :], first_mv[:, t // 2, t % 2, 0:1],
                                      first_rs[:, t // 2, 3, t % 2:t % 2 + 1], ALU.subtract, ALU.mult)\
                        .then_inc(xn_done, 1)

                for t in range(3):
                    first_stats(t)
                first_normalize(0)
                first_stats(3)
                for t in range(1, SEQ // P):
                    first_normalize(t)
                    first_lo(t - 1)
                chunk_stats(0)
                first_lo(SEQ // P - 1)
                chunk_normalize(0, None)
                chunk_lo(0, 1, FILLS_AHEAD - 1, 0)
                dve.wait_ge(bias_in, 16)
                qk_lo_part(Q, 0, 0)
                qk_lo_part(K, 0, 0)

            def step(b, g):
                n = step_of(b, g)
                _, ng = next_pos(b, g)
                for h in range(GH):
                    s = n * GH + h
                    par, prev = h % 2, (h + 1) % 2
                    if h == 2:
                        lo_part(v_parts[:, :, :, HD:2 * HD],
                                t_ps[0][:, :].rearrange("p (k h d) -> p k h d", k=QT, h=GH),
                                v_parts[:, :, :, 0:HD].bitcast(F32), fill(b, g, 6))
                    dve.wait_ge(scores_done, s + 1)
                    for qt in range(QT):
                        last_max = dve.tensor_reduce(row_max[par][:, qt:qt + 1],
                                                     score_ps[:, S_COL[qt]:S_COL[qt] + P * (qt + 1)],
                                                     AXIS.X, ALU.max)
                    last_max.then_inc(max_done, 1)
                    dve.wait_ge(max_done, s + 1)
                    dve.tensor_scalar(neg_max[par][:, :], row_max[par][:, :], -SCALE, None, ALU.mult)\
                        .then_inc(negmax_done, 1)

                    def prob_lo(f):
                        i = slot_fill(h, f)
                        w = P * len(T_FILLS[f])
                        cols = slice(T_DEST[f], T_DEST[f] + w)
                        lo_part(pT_lo[prev][:, cols], t_ps[i % 2][:, 0:w], pT_hi[prev][:, cols].bitcast(F32),
                                fill(b, g, i))

                    if not first(b, g, h, 1):
                        prob_lo(0)
                        prob_lo(1)
                    if not first(b, g, h, 3):
                        uses = (n - 1) if h < 3 else n
                        combine(h, s, uses)
                    dve.wait_ge(exp_done, s + 1)
                    dve.reciprocal(inv_sum[par][:, :], row_sum[par][:, :]).then_inc(inv_done, 1)
                    dve.wait_ge(inv_done, s + 1)
                    for qt in range(QT):
                        cols = slice(P_OFF[qt], P_OFF[qt] + P * (qt + 1))
                        last_norm = dve.tensor_scalar(probs[par][:, cols], probs[par][:, cols],
                                                      inv_sum[par][:, qt:qt + 1], None, ALU.mult)
                    last_norm.then_inc(norm_done, 1)
                    if not first(b, g, h, 1):
                        prob_lo(2)
                    if last(b, g):
                        continue
                    if h == 0 and has_chunk(b, g):
                        chunk_stats(n + 1)
                    if h == 1:
                        qk_lo_part(Q, n + 1, ng)
                    if h == 2:
                        qk_lo_part(K, n + 1, ng)
                        if has_chunk(b, g):
                            chunk_normalize(n + 1, fill(b, g, 0))
                    if h == 3 and has_chunk(b, g):
                        half = (b + 1 + (1 if isinstance(g, int) and g == GROUPS - 1 else 0)) % 2
                        col = 0 if isinstance(g, int) and g == GROUPS - 1 else (g + 1) * CH
                        chunk_lo(col, half, fill(b, g, 13), 1)

            def tail():
                s = STEPS * GH
                combine(0, s, STEPS - 1)
                for f in range(3):
                    w = P * len(T_FILLS[f])
                    cols = slice(T_DEST[f], T_DEST[f] + w)
                    lo_part(pT_lo[1][:, cols], t_ps[f % 2][:, 0:w], pT_hi[1][:, cols].bitcast(F32),
                            fill(BATCH - 1, GROUPS, f))
                combine(1, s + 1, STEPS - 1)
                combine(2, s + 2, STEPS - 1)

            emit(dve, prologue, step, tail)

        @block.tensor
        def _(pe):
            def chunk_transposes(k, number, bank):
                pe.wait_ge(xn_done, k + 1)
                bank_free(number)
                hold(pe)
                for kt in range(KT):
                    last = pe.transpose(t_ps[bank][:, kt * CH:(kt + 1) * CH],
                                        xn[:, kt * P:(kt + 1) * P], ident[0:CH, 0:CH])
                last.then_inc(fill_done, 1)

            def bank_free(number, whole=False):
                if isinstance(number, int) and number < 2:
                    return
                pe.wait_ge(lo_done, number if whole else number - 1)

            def project(m, n, half, lo, hi):
                bank = proj_ps[m % 2]
                if lo == 0:
                    pe.wait_ge(w_lo_done, n * 3 + m + 1)
                    if not (isinstance(n, int) and n == 0):
                        if m == Q:
                            pe.wait_ge(v_done, n)
                        elif m == K:
                            pe.wait_ge(qk_lo_done, n * 2)
                    if m == V:
                        pe.wait_ge(qk_lo_done, n * 2 + 1)
                for i in range(lo, hi):
                    kt, part = i // 3, i % 3
                    w = (w_hi, w_hi, w_lo)[part]
                    xt = (xT_hi, xT_lo, xT_hi)[part][half]
                    mm = pe.matmul(bank[:, :], w[:, m, kt * P:(kt + 1) * P], xt[:, kt, :],
                                   start=(i == 0), stop=(i == 23))
                if hi == 24:
                    mm.then_inc(proj_done, 1)

            def scores(b, g, h):
                n = step_of(b, g)
                if h % 2 == 0:
                    pe.wait_ge(stacked[h // 2], n * 12 * 16 + 12 * 16)
                if not first(b, g, h, 1):
                    pe.wait_ge(exp_done, n * GH + h)
                for qt in range(QT):
                    pe.matmul(score_ps[:, S_COL[qt]:S_COL[qt] + S_KEYS[qt]],
                              q_stack[:, h, qt * P:(qt + 1) * P], k_stack[:, h, 0:S_KEYS[qt]],
                              start=(qt != 1), stop=False)
                both = score_ps[:, 0:SEQ].rearrange("p (i c) -> p i c", c=P)[:, 0:QT:QT - 1, :]
                pe.matmul(both, identb[:, :], maskb[:, :].unsqueeze(1).to_broadcast([P, 2, P]),
                          start=False, stop=True)
                for qt in (2, 3):
                    diagonal = S_COL[qt] + qt * P
                    mm = pe.matmul(score_ps[:, diagonal:diagonal + P], identb[:, :], maskb[:, :],
                                   start=False, stop=True)
                mm.then_inc(scores_done, 1)

            def prob_transposes(b, g, h, f, parity):
                i = slot_fill(h, f)
                number = fill(b, g, i)
                bank_free(number, whole=(i == 0 and not after_chunk(b, g)))
                for col, (kt, qt) in enumerate(T_FILLS[f]):
                    at = P_OFF[qt] + kt * P
                    mm = pe.transpose(t_ps[i % 2][:, col * P:(col + 1) * P],
                                      probs[parity][:, at:at + P], ident[:, :])
                mm.then_inc(fill_done, 1)

            def attend(h, parity, s, lo_needed):
                pe.wait_ge(lo_done, lo_needed)
                if not (isinstance(s, int) and s == 2):
                    pe.wait_ge(head_done, s - 2)
                first_mm = True
                for pT in (pT_hi[parity], pT_lo[parity]):
                    for kt in range(QT):
                        at = PT_KT[kt]
                        q0 = PT_QT[kt] * P
                        mm = pe.matmul(o_ps[:, q0:SEQ], v_parts[:, kt, h, :], pT[:, at:at + SEQ - q0],
                                       start=first_mm, stop=(pT is pT_lo[parity] and kt == QT - 1))
                        first_mm = False
                mm.then_inc(pv_done, 1)

            def prologue():
                pe.wait_ge(consts, 5)
                for t in range(SEQ // P):
                    pe.wait_ge(xn_done, t + 1)
                    for half in range(2):
                        bank_free(2 * t + half)
                        for i in range(4):
                            at = (4 * half + i) * P
                            mm = pe.transpose(t_ps[half][:, i * P:(i + 1) * P], x_first[t][:, at:at + P],
                                              ident[:, :])
                        mm.then_inc(fill_done, 1)
                pe.wait_ge(lo_done, FILLS_AHEAD - 1)
                project(Q, 0, 0, 0, 24)
                chunk_transposes(AHEAD - 1, FILLS_AHEAD - 1, 0)
                for m in (K, V):
                    project(m, 0, 0, 0, 24)
                pe.wait_ge(zeros_done, 2)

            def step(b, g):
                n = step_of(b, g)
                nb, _ = next_pos(b, g)
                todo = [] if last(b, g) else [(m, i) for m in (Q, K, V) for i in range(24)]

                def projections(count):
                    while count and todo:
                        m, lo = todo[0]
                        run = min(count, 24 - lo)
                        project(m, n + 1, nb % 2, lo, lo + run)
                        del todo[:run]
                        count -= run

                for h in range(GH):
                    prev = (h + 1) % 2
                    scores(b, g, h)
                    if not first(b, g, h, 1):
                        pe.wait_ge(norm_done, n * GH + h)
                        prob_transposes(b, g, h, 0, prev)
                    if isinstance(g, int) and g == GROUPS - 1 and h == 0 and b + 1 < BATCH:
                        pe.wait_ge(lo_done, fill(b, g, 0))
                    between = 3 if h % 2 == 0 else 0
                    projections(between)
                    if not first(b, g, h, 1):
                        prob_transposes(b, g, h, 1, prev)
                    projections(12 - between)
                    if not first(b, g, h, 1):
                        prob_transposes(b, g, h, 2, prev)
                    projections(6)
                    if h == 1:
                        pe.wait_ge(v_done, n + 1)
                        bank_free(fill(b, g, 6))
                        for kt in range(QT):
                            mm = pe.transpose(t_ps[0][:, kt * P:(kt + 1) * P], vT[:, kt * P:(kt + 1) * P],
                                              ident[:, :])
                        mm.then_inc(fill_done, 1)
                    if not first(b, g, h, 2):
                        needed = fill(b, g, 0) if h == 0 else fill(b, g, slot_fill(h - 1, 2)) + 1
                        attend((h + 2) % GH, h % 2, n * GH + h, needed)
                    if h == 3 and has_chunk(b, g):
                        chunk_transposes(n + AHEAD, fill(b, g, 13), 1)

            def tail():
                n = STEPS
                pe.wait_ge(norm_done, n * GH)
                for f in range(3):
                    number = fill(BATCH - 1, GROUPS, f)
                    bank_free(number, whole=(f == 0))
                    for col, (kt, qt) in enumerate(T_FILLS[f]):
                        at = P_OFF[qt] + kt * P
                        mm = pe.transpose(t_ps[f % 2][:, col * P:(col + 1) * P],
                                          probs[1][:, at:at + P], ident[:, :])
                    mm.then_inc(fill_done, 1)
                attend(2, 0, n * GH, fill(BATCH - 1, GROUPS, 0))
                attend(3, 1, n * GH + 1, fill(BATCH - 1, GROUPS, 2) + 1)

            emit(pe, prologue, step, tail)


TILES = TOKENS // P
HALVES = D // SEQ
OTILES = D // P
DQ_OPS = 22


def output_phase(nc, outer, x, bo, att, qweight, lut4, x1, wl_hi, wl_lo, shifts, stage, wo_raw, att_raw,
                 wo_loaded, att_loaded, att_stored, x1_stored, x1_loaded):
    with ExitStack() as buffers:
        ph = Phase(nc, buffers, outer)
        sb, pb, sem = ph.sb, ph.pb, ph.sem
        ident = sb("ident2", [P, P])
        wo_hi = sb("wo_hi", [P, KT, D], F32R)
        wo_lo = stage
        bo_all = sb("bo_all", [P, D])
        att_hi = [sb(f"att_hi{i}", [P, KT, P], F32R) for i in range(2)]
        att_lo = [sb(f"att_lo{i}", [P, KT, P], F32R) for i in range(2)]
        x_t = [sb(f"x_t{i}", [P, D]) for i in range(2)]
        y_t = [sb(f"y_t{i}", [P, D]) for i in range(2)]
        ones = sb("ones", [P, 32], I32)
        words = sb("words", [P, 4, 32], I32)
        lut_in = sb("lut_in", [P, 16])
        lut = sb("lut", [P, 16])
        lut_xor = sb("lut_xor", [P, 8], I32)
        bits = [sb(f"bits{i}", [P, D], I32) for i in range(4)]
        r = [sb(f"r{i}", [P, D], I32) for i in range(4)]
        out_ps = [pb(f"out_ps{i}", [P, SEQ]) for i in range(4)]
        wt_ps = [pb(f"wt_ps{i}", [P, SEQ]) for i in range(2)]

        ident_done = sem("ident2_done")
        bo_loaded = sem("bo_loaded")
        tables_done = sem("tables_done")
        wo_hi_done = sem("wo_hi_done")
        wo_lo_done = sem("wo_lo_done")
        att_hi_done = sem("att_hi_done")
        att_lo_done = sem("att_lo_done")
        xt_loaded = [sem(f"xt_loaded{i}") for i in range(2)]
        xb_done = sem("xb_done")
        mm_done = sem("mm_done")
        y_taken = sem("y_taken")
        x1_done = sem("x1_done")
        words_loaded = sem("words_loaded")
        dq_done = sem("dq_done")
        wt_done = sem("wt_done")
        wt_hi_done = sem("wt_hi_done")
        wt_lo_done = sem("wt_lo_done")
        waited = sem("waited2")

        block = buffers.enter_context(nc.Block())

        @block.sync
        def _(sp):
            def load_words(p):
                sp.dma_start(words[:, :, :], qweight[0:4, bass.ds(p * P, P), :].rearrange("b o w -> o b w"))\
                    .then_inc(words_loaded, 16)
                sp.dma_start(lut_in[:, :], lut4[bass.ds(p * P, P), :]).then_inc(words_loaded, 16)

            def load_att(p, par):
                sp.wait_ge(att_lo_done, p * 2 + (par - 1))
                sp.sem_inc(waited, 1)
                first_row = (p // 2) * GROUPS
                col = (p % 2) * (2 * P) + par * P
                sp.dma_start(att_raw[par][:, :, :],
                             att[bass.ds(first_row, GROUPS), :, bass.ds(col, P)].rearrange("g p t -> p g t"))\
                    .then_inc(att_loaded[par], 16)

            def store_x1(p, par):
                sp.wait_ge(x1_done, p * 2 + (par + 3))
                sp.sem_inc(waited, 1)
                sp.dma_start(x1[bass.ds(p * (2 * P) + par * P, P), :], x_t[par][:, :]).then_inc(x1_stored[par], 16)

            def load_x(p, par):
                if not (isinstance(p, int) and p == 0):
                    sp.wait_ge(x1_stored[par], p * 16)
                    sp.sem_inc(waited, 1)
                sp.dma_start(x_t[par][:, :], x[bass.ds(p * (2 * P) + par * P, P), :]).then_inc(xt_loaded[par], 16)

            load_words(0)
            sp.dma_start(bo_all[:, :], bo.partition_broadcast(P)).then_inc(bo_loaded, 16)
            for par in range(2):
                load_x(0, par)
            for head in range(GH):
                sp.wait_ge(att_stored[head], STEPS * 16 + 16)
            with sp.Fori(0, OTILES - 1) as p:
                for par in range(2):
                    load_att(p + 1, par)
                sp.wait_ge(dq_done, p * DQ_OPS + 7)
                sp.sem_inc(waited, 1)
                load_words(p + 1)
                for par in range(2):
                    store_x1(p, par)
                    load_x(p + 1, par)
            for par in range(2):
                sp.wait_ge(att_lo_done, TILES - 1 + par)
                sp.wait_ge(x1_stored[par], 16)
                sp.dma_start(att_raw[par][:, :, :].rearrange("p k t -> p (k t)"), x1[par * P:(par + 1) * P, :])\
                    .then_inc(x1_loaded[par], 16)
            for par in range(2):
                store_x1(OTILES - 1, par)

        @block.gpsimd
        def _(pool):
            def x_plus_bias(p, par):
                pool.wait_ge(xt_loaded[par], p * 16 + 16)
                pool.tensor_tensor(x_t[par][:, :], x_t[par][:, :], bo_all[:, :], ALU.add).then_inc(xb_done, 1)

            def finish_x1(p, par):
                pool.wait_ge(xb_done, p * 2 + (par + 1))
                pool.wait_ge(y_taken, p * 4 + (2 * par + 2))
                pool.tensor_tensor(x_t[par][:, :], y_t[par][:, :], x_t[par][:, :], ALU.add).then_inc(x1_done, 1)

            def split_lo(p, par):
                pool.wait_ge(att_hi_done, p * 2 + (par + 1))
                pool.tensor_tensor(att_lo[par][:, :, :], att_raw[par][:, :, :],
                                   att_hi[par][:, :, :].bitcast(F32), ALU.subtract).then_inc(att_lo_done, 1)

            pool.iota(shifts[:, 0, :], pattern=[[-1, 32]], base=31, channel_multiplier=0).then_inc(tables_done, 1)
            pool.iota(shifts[:, 2, :], pattern=[[1, 32]], base=0, channel_multiplier=0).then_inc(tables_done, 1)
            pool.iota(ones[:, :], pattern=[[0, 32]], base=1, channel_multiplier=0).then_inc(tables_done, 1)
            pool.memset(ident[:, :], 0.0).then_inc(ident_done, 1)
            pool.wait_ge(ident_done, 1)
            pool.affine_select(out=ident[:, :], in_=ident[:, :], compare_op=ALU.not_equal, fill=1.0,
                               base=0, pattern=[[-1, P]], channel_multiplier=1).then_inc(ident_done, 1)
            pool.wait_ge(att_lo_done, 1)
            split_lo(0, 1)
            pool.wait_ge(bo_loaded, 16)
            with pool.Fori(0, OTILES - 1) as p:
                for par in range(2):
                    x_plus_bias(p, par)
                    finish_x1(p, par)
                    split_lo(p + 1, par)
            for par in range(2):
                x_plus_bias(OTILES - 1, par)
                finish_x1(OTILES - 1, par)

        @block.scalar
        def _(act):
            def split_hi(p, par):
                act.wait_ge(att_loaded[par], p * 16 + 16)
                if not (isinstance(p, int) and p == 0):
                    act.wait_ge(mm_done, p * 4 + (2 * par - 2))
                act.activation(att_hi[par][:, :, :], att_raw[par][:, :, :], ACT.Copy).then_inc(att_hi_done, 1)

            def take_out(p, par):
                act.wait_ge(x1_done, p * 2 + (par + 1))
                for half in range(HALVES):
                    cols = slice(half * SEQ, (half + 1) * SEQ)
                    act.wait_ge(mm_done, p * 4 + (2 * par + half + 1))
                    act.activation(y_t[par][:, cols], out_ps[2 * par + half][:, :], ACT.Copy).then_inc(y_taken, 1)

            def weights_hi(p):
                for half in range(2):
                    act.wait_ge(wt_done, p * 2 + half + 1)
                    act.activation(wl_hi[:, 4 * half:4 * half + 4, bass.ds(p * P, P)],
                                   wt_ps[half][:, :].rearrange("p (k o) -> p k o", k=4), ACT.Copy)\
                        .then_inc(wt_hi_done, 1)

            act.sem_inc(x1_done, 2)
            split_hi(0, 0)
            act.wait_ge(wo_loaded, KT * 16)
            for kt in range(KT):
                act.activation(wo_hi[:, kt, :], wo_raw[:, kt, :], ACT.Copy).then_inc(wo_hi_done, 1)
                if kt == 1:
                    split_hi(0, 1)
            with act.Fori(0, OTILES - 1) as p:
                for par in range(2):
                    take_out(p, par)
                    split_hi(p + 1, par)
                weights_hi(p)
            for par in range(2):
                take_out(OTILES - 1, par)
            weights_hi(OTILES - 1)

        @block.vector
        def _(dve):
            def dequantize(p):
                count = [0]

                def counted(instruction):
                    count[0] += 1
                    instruction.then_inc(dq_done, 1)

                def after(k):
                    dve.wait_ge(dq_done, p * DQ_OPS + k)

                def leaf(n, j):
                    counted(dve.tensor_scalar(r[n][:, :], bits[0][:, :], lut_xor[:, j:j + 1],
                                              lut[:, 2 * j:2 * j + 1].bitcast(I32),
                                              ALU.bitwise_and, ALU.bitwise_xor))

                def select(n, plane, m):
                    dve.sem_inc(waited, 1)
                    counted(dve.copy_predicated(r[n][:, :], bits[plane][:, :], r[m][:, :]))

                def word(plane):
                    return words[:, plane, :].unsqueeze(2).to_broadcast([P, 32, 32])

                def pattern(row):
                    return shifts[:, row, :].unsqueeze(1).to_broadcast([P, 32, 32])

                def spread(plane):
                    return bits[plane][:, :].rearrange("p (w s) -> p w s", s=32)

                dve.wait_ge(words_loaded, p * 32 + 32)
                counted(dve.tensor_copy(lut[:, :], lut_in[:, :]))
                yield
                counted(dve.tensor_tensor(spread(0), word(0), pattern(0), ALU.logical_shift_left))
                yield
                after(1)
                pairs = lut[:, :].bitcast(I32).rearrange("p (j b) -> p j b", b=2)
                counted(dve.tensor_tensor(lut_xor[:, :], pairs[:, :, 0], pairs[:, :, 1], ALU.bitwise_xor))
                yield
                for plane in (1, 2, 3):
                    counted(dve.tensor_tensor(spread(plane), word(plane), pattern(1), ALU.bitwise_and))
                    yield
                after(3)
                counted(dve.tensor_scalar(bits[0][:, :], bits[0][:, :], 31, None, ALU.arith_shift_right))
                yield
                if not (isinstance(p, int) and p == 0):
                    dve.wait_ge(wt_done, p * 2)
                after(7)
                leaf(0, 0)
                yield
                leaf(1, 1)
                yield
                leaf(2, 2)
                yield
                after(9)
                select(0, 1, 1)
                yield
                leaf(3, 3)
                yield
                after(11)
                leaf(1, 4)
                yield
                after(12)
                select(2, 1, 3)
                yield
                after(14)
                leaf(3, 5)
                yield
                select(0, 2, 2)
                yield
                after(15)
                select(1, 1, 3)
                yield
                after(16)
                leaf(2, 6)
                yield
                after(17)
                leaf(3, 7)
                yield
                after(19)
                select(2, 1, 3)
                yield
                after(20)
                select(1, 2, 2)
                yield
                after(21)
                select(0, 3, 1)
                assert count[0] == DQ_OPS
                yield

            def weights_lo(p):
                for half in range(2):
                    at = wl_hi[:, 4 * half:4 * half + 4, bass.ds(p * P, P)]
                    dve.wait_ge(wt_hi_done, p * 2 + half + 1)
                    dve.tensor_tensor(wl_lo[:, 4 * half:4 * half + 4, bass.ds(p * P, P)],
                                      wt_ps[half][:, :].rearrange("p (k o) -> p k o", k=4), at.bitcast(F32),
                                      ALU.subtract).then_inc(wt_lo_done, 1)

            dve.wait_ge(att_hi_done, 1)
            dve.tensor_tensor(att_lo[0][:, :, :], att_raw[0][:, :, :], att_hi[0][:, :, :].bitcast(F32),
                              ALU.subtract).then_inc(att_lo_done, 1)
            for kt in range(KT):
                dve.wait_ge(wo_hi_done, kt + 1)
                dve.tensor_tensor(wo_lo[:, kt, :], wo_raw[:, kt, :], wo_hi[:, kt, :].bitcast(F32),
                                  ALU.subtract).then_inc(wo_lo_done, 1)
            dve.wait_ge(tables_done, 3)
            dve.tensor_tensor(shifts[:, 1, :], ones[:, :], shifts[:, 2, :], ALU.logical_shift_left)\
                .then_inc(tables_done, 1)
            dve.wait_ge(tables_done, 4)

            def body(p):
                ops = dequantize(p)
                for _ in range(7):
                    next(ops)
                if not (isinstance(p, int) and p == 0):
                    weights_lo(p - 1)
                for _ in ops:
                    pass

            dve.sem_inc(wt_lo_done, 2)
            body(0)
            with dve.Fori(1, OTILES) as p:
                body(p)
            weights_lo(OTILES - 1)

        @block.tensor
        def _(pe):
            def multiply(p, par, halves):
                pe.wait_ge(att_lo_done, p * 2 + (par + 1))
                start = isinstance(p, int) and p == 0
                if not start:
                    pe.wait_ge(y_taken, p * 4 + (2 * par + halves[-1] - 3))
                for kt in range(KT):
                    if start and par == 0:
                        pe.wait_ge(wo_lo_done, kt + 1)
                    for half in halves:
                        for part in range(3):
                            a = (att_hi, att_lo, att_hi)[part][par]
                            w = (wo_hi, wo_hi, wo_lo)[part]
                            mm = pe.matmul(out_ps[2 * par + half][:, :], a[:, kt, :],
                                           w[:, kt, half * SEQ:(half + 1) * SEQ],
                                           start=(kt == 0 and part == 0), stop=(kt == KT - 1 and part == 2))
                            if kt == KT - 1 and part == 2:
                                mm.then_inc(mm_done, 1)

            def transpose_weights(p):
                pe.wait_ge(dq_done, (p + 1) * DQ_OPS)
                pe.wait_ge(wt_lo_done, p * 2 + 2)
                for half in range(2):
                    for i in range(4):
                        at = (4 * half + i) * P
                        mm = pe.transpose(wt_ps[half][:, i * P:(i + 1) * P], r[0][:, at:at + P].bitcast(F32),
                                          ident[:, :])
                    mm.then_inc(wt_done, 1)

            pe.wait_ge(ident_done, 2)

            multiply(0, 0, (0, 1))
            multiply(0, 1, (0,))
            multiply(0, 1, (1,))
            with pe.Fori(1, OTILES) as p:
                multiply(p, 0, (0,))
                transpose_weights(p - 1)
                multiply(p, 0, (1,))
                multiply(p, 1, (0,))
                multiply(p, 1, (1,))
            transpose_weights(OTILES - 1)


def feed_forward_phase(nc, outer, x1, fbias, out, wl_hi, wl_lo, flag, x_t, x_loaded, x1_stored, tag, high,
                       run_if=None):
    with ExitStack() as buffers:
        ph = Phase(nc, buffers, outer)

        def sb(name, shape, dt=F32):
            return ph.sb(name + tag, shape, dt)

        def pb(name, shape, dt=F32):
            return ph.pb(name + tag, shape, dt)

        def sem(name):
            return ph.sem(name + tag)

        ident = sb("f_ident", [P, P])
        neg_half = sb("f_neg_half", [P, 1])
        bias_all = sb("f_bias_all", [P, D])
        xb = [sb(f"f_xb{i}", [P, D]) for i in range(2)]
        xn = [sb(f"f_xn{i}", [P, D]) for i in range(2)]
        squares = sb("f_squares", [P, D])
        bn = sb("f_bn", [P, 2, 6])
        mv = sb("f_mv", [P, 2])
        rs = sb("f_rs", [P, 4])
        xT_hi = [sb(f"f_xT_hi{i}", [P, KT, P], F32R) for i in range(2)]
        xT_lo = [sb(f"f_xT_lo{i}", [P, KT, P], F32R) for i in range(2)]
        norm_sq = [sb(f"f_norm_sq{i}", [P, 1]) for i in range(2)]
        worst = sb("f_worst", [P, 1])
        worst_all = sb("f_worst_all", [P, 1])
        chosen = [sb(f"f_chosen{i}", [P, 1], I32) for i in range(2)]
        old = [sb(f"f_old{i}", [P, D]) for i in range(2)] if high else None
        t_ps = [pb(f"f_t{i}", [P, SEQ]) for i in range(2)]
        y_ps = [pb(f"f_y{i}", [P, SEQ]) for i in range(4)]

        consts = sem("f_consts")
        bias_loaded = sem("f_bias_loaded")
        old_loaded = [sem(f"f_old_loaded{i}") for i in range(2)]
        bn_done = sem("f_bn_done")
        stats_done = sem("f_stats_done")
        rstd_chain = sem("f_rstd_chain")
        rstd_done = sem("f_rstd_done")
        xn_done = sem("f_xn_done")
        norm_done = sem("f_norm_done")
        worst_done = sem("f_worst_done")
        xb_done = sem("f_xb_done")
        fill_done = sem("f_fill_done")
        hi_done = sem("f_hi_done")
        lo_done = sem("f_lo_done")
        mm_done = sem("f_mm_done")
        y_done = sem("f_y_done")
        out_done = sem("f_out_done")
        stored = [sem(f"f_stored{i}") for i in range(2)]
        worst_all_done = sem("f_worst_all_done")
        waited = sem("f_waited")

        block = buffers.enter_context(nc.Block())

        def guarded(eng, program):
            if run_if is None:
                program()
                return
            value = eng.value_load(run_if[0:1, 0:1], min_val=0, max_val=1)
            with eng.If(value > 0):
                program()
            with eng.Else():
                eng.nop()

        def tile(p, c):
            return p * 2 + c, c % 2, p + c // 2

        def early(t):
            return isinstance(t, int) and t < 2

        def hold(eng):
            eng.sem_inc(waited, 1)

        @block.sync
        def _(sp):
            def load(p, c):
                t, par, _ = tile(p, c)
                if not early(t):
                    sp.wait_ge(xn_done, t - 1)
                    hold(sp)
                    sp.wait_ge(xb_done, t - 1)
                    hold(sp)
                sp.dma_start(x_t[par][:, :], x1[bass.ds(t * P, P), :]).then_inc(x_loaded[par], 16)

            def load_old(p, c):
                if not high:
                    return
                t, par, uses = tile(p, c)
                if not early(t):
                    sp.wait_ge(stored[par], uses * 16)
                    hold(sp)
                sp.dma_start(old[par][:, :], out[bass.ds(t * P, P), :]).then_inc(old_loaded[par], 16)

            def store(p, c):
                t, par, _ = tile(p, c)
                sp.wait_ge(out_done, t + 1)
                hold(sp)
                src = old[par] if high else xb[par]
                sp.dma_start(out[bass.ds(t * P, P), :], src[:, :]).then_inc(stored[par], 16)

            def program():
                if high:
                    for c in range(2):
                        load(0, c)
                sp.dma_start(bias_all[:, :], fbias.partition_broadcast(P)).then_inc(bias_loaded, 16)
                for par in range(2):
                    sp.wait_ge(x1_stored[par], TILES // 2 * 16)
                for c in range(2):
                    load_old(0, c)
                load(1, 0)
                load(1, 1)
                store(0, 0)
                load_old(1, 0)
                with sp.Fori(2, TILES // 2) as p:
                    for c in range(2):
                        load(p, c)
                        store(p, c - 3)
                        load_old(p, c - 1)
                store(TILES // 2 - 1, -1)
                load_old(TILES // 2 - 1, 1)
                for c in range(2):
                    store(TILES // 2 - 1, c)
                for par in range(2):
                    sp.wait_ge(stored[par], TILES // 2 * 16)

            guarded(sp, program)

        @block.gpsimd
        def _(pool):
            def rstd(p, c):
                t, _, _ = tile(p, c)
                base = t * 5
                pool.wait_ge(stats_done, t + 1)
                hold(pool)
                pool.tensor_scalar(rs[:, 0:1], mv[:, 1:2], EPS, None, ALU.add).then_inc(rstd_chain, 1)
                pool.wait_ge(rstd_chain, base + 1)
                pool.tensor_tensor(rs[:, 1:2], rs[:, 0:1], neg_half[:, :], ALU.pow).then_inc(rstd_chain, 1)
                pool.wait_ge(rstd_chain, base + 2)
                pool.tensor_tensor(rs[:, 2:3], rs[:, 1:2], rs[:, 1:2], ALU.mult).then_inc(rstd_chain, 1)
                pool.wait_ge(rstd_chain, base + 3)
                pool.tensor_tensor(rs[:, 2:3], rs[:, 2:3], rs[:, 0:1], ALU.mult).then_inc(rstd_chain, 1)
                pool.wait_ge(rstd_chain, base + 4)
                hold(pool)
                pool.tensor_scalar(rs[:, 2:3], rs[:, 2:3], -0.5, 1.5, ALU.mult, ALU.add).then_inc(rstd_chain, 1)
                pool.wait_ge(rstd_chain, base + 5)
                pool.tensor_tensor(rs[:, 3:4], rs[:, 1:2], rs[:, 2:3], ALU.mult).then_inc(rstd_done, 1)

            def add_bias(p, c):
                t, par, uses = tile(p, c)
                if not early(t):
                    if high:
                        pool.wait_ge(out_done, t - 1)
                    else:
                        pool.wait_ge(stored[par], uses * 16)
                pool.wait_ge(x_loaded[par], uses * 16 + 16)
                pool.tensor_tensor(xb[par][:, :], x_t[par][:, :], bias_all[:, :], ALU.add).then_inc(xb_done, 1)

            def program():
                pool.memset(neg_half[:, :], -0.5)
                pool.memset(ident[:, :], 0.0).then_inc(consts, 1)
                pool.wait_ge(consts, 1)
                pool.affine_select(out=ident[:, :], in_=ident[:, :], compare_op=ALU.not_equal, fill=1.0,
                                   base=0, pattern=[[-1, P]], channel_multiplier=1).then_inc(consts, 1)
                rstd(0, 0)
                pool.wait_ge(bias_loaded, 16)
                for t in range(3):
                    rstd(0, t + 1)
                    add_bias(0, t)
                with pool.Fori(2, TILES // 2) as p:
                    rstd(p, 0)
                    add_bias(p, -1)
                    rstd(p, 1)
                    add_bias(p, 0)
                add_bias(TILES // 2 - 1, 1)
                if not high:
                    pool.wait_ge(worst_done, TILES + 1)
                    pool.partition_all_reduce(worst_all[:, :], worst[:, :], P, bass.bass_isa.ReduceOp.max)\
                        .then_inc(worst_all_done, 1)

            guarded(pool, program)

        @block.scalar
        def _(act):
            def norms(p, c):
                t, par, _ = tile(p, c)
                act.wait_ge(xn_done, t + 1)
                if not early(t):
                    act.wait_ge(worst_done, t)
                if not (isinstance(t, int) and t == 0):
                    act.wait_ge(norm_done, t)
                act.activation(squares[:, :], xn[par][:, :], ACT.Square, accum_out=norm_sq[par][:, :])\
                    .then_inc(norm_done, 1)

            def split_hi(p, c):
                t, par, _ = tile(p, c)
                for half in range(2):
                    act.wait_ge(fill_done, t * 2 + (half + 1))
                    act.activation(xT_hi[par][:, 4 * half:4 * half + 4, :],
                                   t_ps[half][:, :].rearrange("p (k t) -> p k t", k=4), ACT.Copy)\
                        .then_inc(hi_done, 1)

            def program():
                def pair(p):
                    for c in range(2):
                        split_hi(p, c)
                        norms(p, c)

                pair(0)
                with act.Fori(1, TILES // 2) as p:
                    pair(p)

            guarded(act, program)

        @block.vector
        def _(dve):
            def statistics(p, c):
                t, par, uses = tile(p, c)
                dve.wait_ge(x_loaded[par], uses * 16 + 16)
                for half in range(2):
                    last = dve.bn_stats(bn[:, half, :], x_t[par][:, half * SEQ:(half + 1) * SEQ])
                last.then_inc(bn_done, 1)
                dve.wait_ge(bn_done, t + 1)
                hold(dve)
                dve.bn_aggr(mv[:, :], bn[:, :, :].rearrange("p a b -> p (a b)")).then_inc(stats_done, 1)

            def normalize(p, c):
                t, par, _ = tile(p, c)
                dve.wait_ge(rstd_done, t + 1)
                if not early(t):
                    dve.wait_ge(fill_done, t * 2 - 2)
                    dve.wait_ge(norm_done, t - 1)
                dve.tensor_scalar(xn[par][:, :], x_t[par][:, :], mv[:, 0:1], rs[:, 3:4],
                                  ALU.subtract, ALU.mult).then_inc(xn_done, 1)

            def split_lo(p, c):
                t, par, _ = tile(p, c)
                for half in range(2):
                    dve.wait_ge(hi_done, t * 2 + (half + 1))
                    dve.tensor_tensor(xT_lo[par][:, 4 * half:4 * half + 4, :],
                                      t_ps[half][:, :].rearrange("p (k t) -> p k t", k=4),
                                      xT_hi[par][:, 4 * half:4 * half + 4, :].bitcast(F32),
                                      ALU.subtract).then_inc(lo_done, 1)

            def judge(p, c):
                t, par, _ = tile(p, c)
                dve.wait_ge(norm_done, t + 1)
                dve.wait_ge(worst_done, t + 1)
                if high:
                    if not early(t):
                        dve.wait_ge(out_done, t - 1)
                    hold(dve)
                    dve.tensor_scalar(chosen[par][:, :], norm_sq[par][:, :], THRESHOLD_SQ, None, ALU.is_gt)\
                        .then_inc(worst_done, 1)
                else:
                    dve.tensor_tensor(worst[:, :], worst[:, :], norm_sq[par][:, :], ALU.max)\
                        .then_inc(worst_done, 1)

            def finish(p, c, half):
                t, par, uses = tile(p, c)
                if half == 0:
                    dve.wait_ge(xb_done, t + 1)
                cols = slice(half * SEQ, (half + 1) * SEQ)
                dve.wait_ge(mm_done, t * 2 + (half + 1))
                add = dve.tensor_tensor(xb[par][:, cols], y_ps[2 * par + half][:, :], xb[par][:, cols], ALU.add)
                if half == 1:
                    add.then_inc(y_done if high else out_done, 1)
                if half == 1 and high:
                    dve.wait_ge(y_done, t + 1)
                    dve.wait_ge(old_loaded[par], uses * 16 + 16)
                    hold(dve)
                    dve.copy_predicated(old[par][:, :], chosen[par][:, 0:1].to_broadcast([P, D]), xb[par][:, :])\
                        .then_inc(out_done, 1)

            def slot(p, c, before=True, ahead=True, next_tile=True):
                if before:
                    finish(p, c - 1, 1)
                if ahead:
                    statistics(p, c + 2)
                    normalize(p, c + 2)
                if next_tile:
                    split_lo(p, c + 1)
                    judge(p, c + 1)
                finish(p, c, 0)

            def program():
                dve.memset(worst[:, :], 0.0).then_inc(worst_done, 1)
                statistics(0, 0)
                normalize(0, 0)
                statistics(0, 1)
                split_lo(0, 0)
                normalize(0, 1)
                judge(0, 0)
                for t in range(3):
                    slot(0, t, before=t > 0)
                with dve.Fori(1, TILES // 2 - 2) as p:
                    slot(p, 1)
                    slot(p, 2)
                for t in range(TILES - 3, TILES):
                    slot(0, t, ahead=t < TILES - 2, next_tile=t < TILES - 1)
                finish(0, TILES - 1, 1)
                if not high:
                    dve.wait_ge(worst_all_done, 1)
                    dve.tensor_scalar(flag[:, :], worst_all[0:1, :], THRESHOLD_SQ, None, ALU.is_gt)\
                        .then_inc(y_done, 1)
                    dve.wait_ge(y_done, 1)

            guarded(dve, program)

        @block.tensor
        def _(pe):
            def transposes(p, c):
                t, par, _ = tile(p, c)
                pe.wait_ge(xn_done, t + 1)
                for half in range(2):
                    if not (isinstance(t, int) and t == 0):
                        pe.wait_ge(lo_done, t * 2 + (half - 1))
                    for i in range(4):
                        at = (4 * half + i) * P
                        mm = pe.transpose(t_ps[half][:, i * P:(i + 1) * P], xn[par][:, at:at + P], ident[:, :])
                    mm.then_inc(fill_done, 1)

            def multiply(p, c, half):
                t, par, _ = tile(p, c)
                if half == 0:
                    pe.wait_ge(lo_done, t * 2 + 2)
                    if not early(t):
                        pe.wait_ge(y_done if high else out_done, t - 1)
                for kt in range(KT):
                    for part in range(3):
                        a = (xT_hi, xT_lo, xT_hi)[part][par]
                        w = (wl_hi, wl_hi, wl_lo)[part]
                        mm = pe.matmul(y_ps[2 * par + half][:, :], a[:, kt, :],
                                       w[:, kt, half * SEQ:(half + 1) * SEQ],
                                       start=(kt == 0 and part == 0), stop=(kt == KT - 1 and part == 2))
                mm.then_inc(mm_done, 1)

            def slot(p, c):
                multiply(p, c, 0)
                transposes(p, c + 1)
                multiply(p, c, 1)

            def program():
                pe.wait_ge(consts, 2)
                transposes(0, 0)
                for t in range(3):
                    slot(0, t)
                with pe.Fori(1, TILES // 2 - 1) as p:
                    for c in (1, 2):
                        slot(p, c)
                for half in range(HALVES):
                    multiply(0, TILES - 1, half)

            guarded(pe, program)


def wide_weights_phase(nc, outer, qweight, lut8, wl_hi, wl_lo, shifts, flag):
    with ExitStack() as buffers:
        ph = Phase(nc, buffers, outer)
        sb, pb, sem = ph.sb, ph.pb, ph.sem
        ident = sb("w_ident", [P, P])
        words = sb("w_words", [P, 8, 32], I32)
        table = sb("w_table", [P, 256])
        code = sb("w_code", [P, D], I32)
        bit = sb("w_bit", [P, D], I32)
        codef = sb("w_codef", [P, D])
        entry = sb("w_entry", [P, D])
        weights = sb("w_weights", [P, D])
        index = sb("w_index", [P, 1])
        wt_ps = [pb(f"w_t{i}", [P, SEQ]) for i in range(2)]
        ident_done = sem("w_ident_done")
        loaded = sem("w_loaded")
        chain = sem("w_chain")
        entries = sem("w_entries")
        built = sem("w_built")
        fill_done = sem("w_fill_done")
        hi_done = sem("w_hi8_done")
        lo_done = sem("w_lo8_done")
        waited = sem("w_waited")
        CODES = 256
        BITS = 8
        CHAIN = 3 * BITS + 2

        block = buffers.enter_context(nc.Block())

        def guarded(eng, program):
            value = eng.value_load(flag[0:1, 0:1], min_val=0, max_val=1)
            with eng.If(value > 0):
                program()
            with eng.Else():
                eng.nop()

        @block.sync
        def _(sp):
            def program():
                with sp.Fori(0, OTILES) as o:
                    sp.wait_ge(built, o + 1)
                    sp.sem_inc(waited, 1)
                    sp.dma_start(words[:, :, :], qweight[:, bass.ds(o * P, P), :].rearrange("b o w -> o b w"))\
                        .then_inc(loaded, 16)
                    sp.dma_start(table[:, :], lut8[bass.ds(o * P, P), :]).then_inc(loaded, 16)

            guarded(sp, program)

        @block.gpsimd
        def _(pool):
            def program():
                pool.memset(ident[:, :], 0.0).then_inc(ident_done, 1)
                pool.wait_ge(ident_done, 1)
                pool.affine_select(out=ident[:, :], in_=ident[:, :], compare_op=ALU.not_equal, fill=1.0,
                                   base=0, pattern=[[-1, P]], channel_multiplier=1).then_inc(ident_done, 1)

            guarded(pool, program)

        @block.vector
        def _(dve):
            def program():
                dve.sem_inc(built, 1)
                dve.sem_inc(lo_done, 2)
                with dve.Fori(0, OTILES) as o:
                    count = [0]

                    def chained(instruction):
                        count[0] += 1
                        instruction.then_inc(chain, 1)
                        dve.wait_ge(chain, o * CHAIN + count[0])

                    dve.wait_ge(loaded, o * 32 + 32)
                    for b in range(BITS):
                        target = code if b == 0 else bit
                        spread = target[:, :].rearrange("p (w s) -> p w s", s=32)
                        chained(dve.tensor_tensor(spread, words[:, b, :].unsqueeze(2).to_broadcast([P, 32, 32]),
                                                  shifts[:, 2, :].unsqueeze(1).to_broadcast([P, 32, 32]),
                                                  ALU.logical_shift_right))
                        dve.sem_inc(waited, 1)
                        chained(dve.tensor_scalar(target[:, :], target[:, :], 1, b,
                                                  ALU.bitwise_and, ALU.logical_shift_left))
                        if b:
                            chained(dve.tensor_tensor(code[:, :], code[:, :], bit[:, :], ALU.bitwise_or))
                    chained(dve.tensor_copy(codef[:, :], code[:, :]))
                    dve.wait_ge(fill_done, o * 2 + 2)
                    dve.sem_inc(waited, 1)
                    chained(dve.memset(weights[:, :], 0.0))
                    chained(dve.memset(index[:, :], 0.0))
                    dve.sem_inc(waited, 1)
                    assert count[0] == CHAIN
                    with dve.Fori(0, CODES) as j:
                        at = o * (3 * CODES) + j * 3
                        dve.tensor_scalar(entry[:, :], codef[:, :], index[:, 0:1], table[:, bass.ds(j, 1)],
                                          ALU.is_equal, ALU.mult).then_inc(entries, 1)
                        dve.wait_ge(entries, at + 1)
                        dve.tensor_tensor(weights[:, :], weights[:, :], entry[:, :], ALU.add).then_inc(entries, 1)
                        dve.wait_ge(entries, at + 2)
                        dve.sem_inc(waited, 1)
                        dve.tensor_scalar(index[:, :], index[:, :], 1.0, None, ALU.add).then_inc(entries, 1)
                        dve.wait_ge(entries, at + 3)
                        dve.sem_inc(waited, 1)
                    dve.sem_inc(built, 1)
                    for half in range(2):
                        at = wl_hi[:, 4 * half:4 * half + 4, bass.ds(o * P, P)]
                        dve.wait_ge(hi_done, o * 2 + half + 1)
                        dve.tensor_tensor(wl_lo[:, 4 * half:4 * half + 4, bass.ds(o * P, P)],
                                          wt_ps[half][:, :].rearrange("p (k o) -> p k o", k=4),
                                          at.bitcast(F32), ALU.subtract).then_inc(lo_done, 1)

            guarded(dve, program)

        @block.tensor
        def _(pe):
            def program():
                pe.wait_ge(ident_done, 2)
                pe.sem_inc(fill_done, 2)
                with pe.Fori(0, OTILES) as o:
                    pe.wait_ge(built, o + 2)
                    pe.wait_ge(lo_done, o * 2 + 2)
                    for half in range(2):
                        for i in range(4):
                            at = (4 * half + i) * P
                            mm = pe.transpose(wt_ps[half][:, i * P:(i + 1) * P], weights[:, at:at + P],
                                              ident[:, :])
                        mm.then_inc(fill_done, 1)

            guarded(pe, program)

        @block.scalar
        def _(act):
            def program():
                with act.Fori(0, OTILES) as o:
                    for half in range(2):
                        act.wait_ge(fill_done, o * 2 + half + 3)
                        act.activation(wl_hi[:, 4 * half:4 * half + 4, bass.ds(o * P, P)],
                                       wt_ps[half][:, :].rearrange("p (k o) -> p k o", k=4), ACT.Copy)\
                            .then_inc(hi_done, 1)

            guarded(act, program)


def build(nc, x, w_qkv, b_qkv, wo, bo, qweight, lut4, lut8, fbias, out):
    att = nc.dram_tensor("att_scratch", (STEPS, P, SEQ), F32, kind="Internal").ap()
    x1 = nc.dram_tensor("x1_scratch", (TOKENS, D), F32, kind="Internal").ap()
    with ExitStack() as outer:
        keep = Phase(nc, outer, outer)
        base = (nc.sbuf_base + 31) // 32 * 32
        stage = keep.sb("stage", [P, KT, D], F32R)
        wo_raw = nc.alloc_sbuf_tensor_at("wo_raw", [P, KT, D], F32, offset=base)
        att_raw = [keep.sb(f"att_raw{i}", [P, KT, P]) for i in range(2)]
        wo_loaded = keep.sem("wo_loaded")
        x1_stored = [keep.sem(f"x1_stored{i}") for i in range(2)]
        x1_loaded = [[keep.sem(f"x1_loaded{i}_{bits}") for i in range(2)] for bits in (4, 8)]
        att_loaded = [keep.sem(f"att_loaded{i}") for i in range(2)]
        o_out = keep.sb("o_out", [P, SEQ])
        att_stored = [keep.sem(f"att_stored{i}") for i in range(GH)]
        attention_phase(nc, outer, x, w_qkv, b_qkv, att, wo, stage, wo_raw, att_raw, wo_loaded, att_loaded,
                    att_stored, o_out)
        wl_hi = keep.sb("wl_hi", [P, KT, D], F32R)
        wl_lo = keep.sb("wl_lo", [P, KT, D], F32R)
        flag = keep.sb("flag", [1, 1], I32)
        shifts = keep.sb("shifts", [P, 3, 32], I32)
        output_phase(nc, outer, x, bo, att, qweight, lut4, x1, wl_hi, wl_lo, shifts, stage, wo_raw, att_raw,
                     wo_loaded, att_loaded, att_stored, x1_stored, x1_loaded[0])
        x_t = [tile[:, :, :].rearrange("p k t -> p (k t)") for tile in att_raw]
        feed_forward_phase(nc, outer, x1, fbias, out, wl_hi, wl_lo, flag, x_t, x1_loaded[0], x1_stored, "",
                           high=False)
        wide_weights_phase(nc, outer, qweight, lut8, wl_hi, wl_lo, shifts, flag)
        feed_forward_phase(nc, outer, x1, fbias, out, wl_hi, wl_lo, flag, x_t, x1_loaded[1], x1_stored, "_8",
                           high=True, run_if=flag)


def kernel(**inputs):
    import numpy as np
    import concourse.bacc as bacc
    from concourse.bass_utils import run_bass_kernel_spmd

    a = {name.split("_", 1)[1]: np.asarray(value) for name, value in inputs.items()}
    w = np.stack([a["attn_Wq"], a["attn_Wk"], a["attn_Wv"]]).reshape(3, GROUPS, P, KT, P)
    b = np.stack([a["attn_bq"], a["attn_bk"], a["attn_bv"]]).reshape(3, GROUPS, P)
    arrays = {
        "x": a["attn_x"].reshape(TOKENS, D),
        "w_qkv": np.ascontiguousarray(w.transpose(1, 4, 0, 3, 2)).reshape(GROUPS, P, 3, KT * P),
        "b_qkv": np.ascontiguousarray(b.transpose(2, 0, 1)),
        "wo": np.ascontiguousarray(a["attn_Wo"].reshape(D, KT, P).transpose(2, 1, 0)),
        "bo": a["attn_bo"],
        "qweight": a["ffn_qweight"],
        "lut4": a["ffn_lut4"],
        "lut8": a["ffn_lut8"],
        "fbias": a["ffn_bias"],
    }
    nc = bacc.Bacc("TRN2", target_bir_lowering=False, num_devices=1)
    args = {}
    for name, value in arrays.items():
        args[name] = nc.dram_tensor(name, value.shape, mybir.dt.from_np(value.dtype), kind="ExternalInput").ap()
    args["out"] = nc.dram_tensor("out", (TOKENS, D), F32, kind="ExternalOutput").ap()
    build(nc, **args)
    result = run_bass_kernel_spmd(nc, [arrays], core_ids=[0])
    return result.results[0]["out"].reshape(BATCH, SEQ, D)
```
